# Optimizing a Trainium2 kernel written in Bass

```python
import numpy as np
import jax
import jax.numpy as jnp

def _softmax(x, axis=-1):
    return jax.nn.softmax(x, axis=axis)

def _gelu(x):
    return jax.nn.gelu(x, approximate=True)

def _silu(x):
    return jax.nn.silu(x)

def _sigmoid(x):
    return jax.nn.sigmoid(x)

def _layernorm(x, axis=-1, eps=1e-05):
    m = jnp.mean(x, axis=axis, keepdims=True)
    v = jnp.var(x, axis=axis, keepdims=True)
    return (x - m) / jnp.sqrt(v + eps)

def _scatter_add(tgt, idx, src, axis=0):
    return tgt.at[idx].add(src)

def _segment_sum(src, seg, n):
    return jax.ops.segment_sum(src, seg, n)
kernel_name = 'mk_sandwich_d1_jaxref_r4_190b6e'

def setup_inputs(seed: int=0):
    np.random.seed(seed)
    _w = jnp.asarray

    def _L0_attn_setup():
        import jax, jax.numpy as jnp
        import numpy as np
        H = 16

        def rotate_half(x):
            x1 = x[..., ::2]
            x2 = x[..., 1::2]
            return jnp.concatenate((-x2, x1), axis=-1)

        def rope_cache(n, hd):
            freqs = 10000.0 ** (-jnp.arange(0, hd, 2, dtype=jnp.float32) / hd)
            angles = jnp.arange(n, dtype=jnp.float32)[:, None] * freqs
            sin = jnp.sin(angles)
            cos = jnp.cos(angles)
            sin = jnp.stack([sin, sin], axis=-1).reshape(n, hd)
            cos = jnp.stack([cos, cos], axis=-1).reshape(n, hd)
            return (sin, cos)
        key = jax.random.key(seed)
        k1, k2, k3 = jax.random.split(key, 3)
        dim, inner = (256, 256)
        x = jax.random.normal(k1, (2, 512, dim), dtype=jnp.float32)
        w_qkv = jax.random.normal(k2, (dim, 3 * inner), dtype=jnp.float32) * dim ** (-0.5)
        w_out = jax.random.normal(k3, (inner, dim), dtype=jnp.float32) * inner ** (-0.5)
        b_out = jnp.zeros((dim,), dtype=jnp.float32)
        return {'x': x, 'w_qkv': w_qkv, 'w_out': w_out, 'b_out': b_out}
    _L0_attn_in = _L0_attn_setup()

    def _L0_ffn_setup():
        import jax, jax.numpy as jnp
        import numpy as np
        TOP_K = 2
        key = jax.random.key(seed)
        ks = jax.random.split(key, 7)
        B, L, D, H, E, S = (2, 512, 256, 128, 16, 512)
        s = lambda fan_in: (1.0 / np.sqrt(fan_in)).astype(np.float32)
        return {'x': jax.random.normal(ks[0], (B, L, D), jnp.float32), 'gate_w': jax.random.normal(ks[1], (E, D), jnp.float32) * s(D), 'w1': jax.random.normal(ks[2], (E, H, D), jnp.float32) * s(D), 'w2': jax.random.normal(ks[3], (E, D, H), jnp.float32) * s(H), 'sfc1': jax.random.normal(ks[4], (S, D), jnp.float32) * s(D), 'sfc2': jax.random.normal(ks[5], (S, D), jnp.float32) * s(D), 'sfc3': jax.random.normal(ks[6], (D, S), jnp.float32) * s(S)}
    _L0_ffn_in = _L0_ffn_setup()
    _d = {'L0_attn_x': _L0_attn_in['x'], 'L0_attn_w_qkv': _L0_attn_in['w_qkv'], 'L0_attn_w_out': _L0_attn_in['w_out'], 'L0_attn_b_out': _L0_attn_in['b_out'], 'L0_ffn_gate_w': _L0_ffn_in['gate_w'], 'L0_ffn_w1': _L0_ffn_in['w1'], 'L0_ffn_w2': _L0_ffn_in['w2'], 'L0_ffn_sfc1': _L0_ffn_in['sfc1'], 'L0_ffn_sfc2': _L0_ffn_in['sfc2'], 'L0_ffn_sfc3': _L0_ffn_in['sfc3']}
    _x0 = _d['L0_attn_x']
    _d['L0_attn_x'] = jax.random.normal(jax.random.fold_in(jax.random.key(seed), 1), (8, 512, 256), dtype=_x0.dtype)
    del _x0
    return _d

def reference(L0_attn_x, L0_attn_w_qkv, L0_attn_w_out, L0_attn_b_out, L0_ffn_gate_w, L0_ffn_w1, L0_ffn_w2, L0_ffn_sfc1, L0_ffn_sfc2, L0_ffn_sfc3):

    def _L0_attn_ref(x, w_qkv, w_out, b_out):
        import jax, jax.numpy as jnp
        import numpy as np
        H = 16

        def rotate_half(x):
            x1 = x[..., ::2]
            x2 = x[..., 1::2]
            return jnp.concatenate((-x2, x1), axis=-1)

        def rope_cache(n, hd):
            freqs = 10000.0 ** (-jnp.arange(0, hd, 2, dtype=jnp.float32) / hd)
            angles = jnp.arange(n, dtype=jnp.float32)[:, None] * freqs
            sin = jnp.sin(angles)
            cos = jnp.cos(angles)
            sin = jnp.stack([sin, sin], axis=-1).reshape(n, hd)
            cos = jnp.stack([cos, cos], axis=-1).reshape(n, hd)
            return (sin, cos)
        b, n, dim = x.shape
        qkv = x @ w_qkv
        q, k, v = jnp.split(qkv, 3, axis=-1)
        heads = lambda t: t.reshape(b, n, H, -1).transpose(0, 2, 1, 3)
        q, k, v = (heads(q), heads(k), heads(v))
        hd = q.shape[-1]
        sin, cos = rope_cache(n, hd)
        q = q * cos + rotate_half(q) * sin
        k = k * cos + rotate_half(k) * sin
        scale = hd ** (-0.5)
        dots = jnp.einsum('bhid,bhjd->bhij', q, k) * scale
        attn = jax.nn.softmax(dots, axis=-1)
        out = jnp.einsum('bhij,bhjd->bhid', attn, v)
        out = out.transpose(0, 2, 1, 3).reshape(b, n, H * hd)
        return out @ w_out + b_out

    def _L0_ffn_ref(x, gate_w, w1, w2, sfc1, sfc2, sfc3):
        import jax, jax.numpy as jnp
        import numpy as np
        TOP_K = 2
        B, L, D = x.shape
        E = gate_w.shape[0]
        shared = jnp.einsum('bls,ds->bld', jax.nn.silu(jnp.einsum('bld,sd->bls', x, sfc1)) * jnp.einsum('bld,sd->bls', x, sfc2), sfc3)
        logits = jnp.einsum('bld,ed->ble', x, gate_w)
        top_w, top_idx = jax.lax.top_k(logits, TOP_K)
        top_w = jax.nn.softmax(top_w, axis=-1)
        xf = x.reshape(-1, D)
        T = xf.shape[0]
        idx = top_idx.reshape(T, TOP_K)
        wk = top_w.reshape(T, TOP_K)
        dispatch = jnp.zeros((T, E), xf.dtype).at[jnp.arange(T)[:, None], idx].add(wk)
        h = jax.nn.silu(jnp.einsum('td,ehd->teh', xf, w1))
        moe = jnp.einsum('teh,te,edh->td', h, dispatch, w2)
        return moe.reshape(B, L, D) + shared
    x = L0_attn_x
    x = x + _layernorm(_L0_attn_ref(_layernorm(x, axis=-1), L0_attn_w_qkv, L0_attn_w_out, L0_attn_b_out), axis=-1)
    x = x + _layernorm(_L0_ffn_ref(_layernorm(x, axis=-1), L0_ffn_gate_w, L0_ffn_w1, L0_ffn_w2, L0_ffn_sfc1, L0_ffn_sfc2, L0_ffn_sfc3), axis=-1)
    return x

_drawn_inputs = setup_inputs


def setup_inputs(seed=0):
    import zlib

    import numpy as np

    out = dict(_drawn_inputs(seed))
    spreads = {'L0_attn_b_out': (0.0, 0.1)}
    factors = {}
    for name, (base, spread) in spreads.items():
        noise = np.random.default_rng([zlib.crc32(name.encode()), seed]).standard_normal(out[name].shape)
        drawn = base * np.exp(spread * noise) if base else spread * noise
        out[name] = jnp.asarray(drawn.astype(out[name].dtype))
    for name, factor in factors.items():
        out[name] = (out[name] * factor).astype(out[name].dtype)
    return out
```

```python
import concourse.bass as bass
from concourse import mybir
from contextlib import ExitStack

B, N, D, H, HD = 8, 512, 256, 16, 16
P = 128
QT = N // P
DC = D // P
GH = 4
NG = H // GH
EPS = 1e-5

F32 = mybir.dt.float32
F32R = mybir.dt.float32r
ALU = mybir.AluOpType
ACT = mybir.ActivationFunctionType
AX = mybir.AxisListType


def later(count):
    return not isinstance(count, int) or count > 0


def attention(nc, ctx, x_in, w_qkv, cos_in, sin_in, ident_in, X, O, ident, ident_r):
    def sb(name, shape, dt=F32):
        return ctx.enter_context(nc.sbuf_tensor(name, shape, dt))

    def ps(name):
        return ctx.enter_context(nc.psum_tensor(name, [P, 512], F32))

    def sem(name):
        return ctx.enter_context(nc.semaphore(name))

    w_raw = sb("w_raw", [P, DC, 3 * D])
    w_hi = sb("w_hi", [P, DC, 3 * D], F32R)
    w_lo = sb("w_lo", [P, DC, 3 * D], F32R)
    cos = sb("cos", [P, QT, HD])
    sin = sb("sin", [P, QT, HD])
    halves = sb("halves", [P, QT])
    stats = sb("stats", [P, QT, 6])
    meanvar = sb("meanvar", [P, QT, 2])
    vareps = sb("vareps", [P, QT])
    rstd = sb("rstd", [P, QT])
    xn = sb("xn", [P, QT, D])
    xt_hi = sb("xt_hi", [P, DC, N], F32R)
    xt_lo = sb("xt_lo", [P, DC, N], F32R)
    qk_raw = [sb(f"qk_raw{i}", [P, 2 * D]) for i in range(2)]
    rope_a = sb("rope_a", [P, 2 * D])
    rope_b = sb("rope_b", [P, 2 * D])
    qk = [sb(f"qk{i}", [P, QT, 2 * D]) for i in range(2)]
    v_aug = [sb(f"v_aug{i}", [P, QT, H, 2 * HD]) for i in range(2)]
    stage_q = [sb(f"stage_q{i}", [P, QT, P], F32R) for i in range(2)]
    stage_k = [sb(f"stage_k{i}", [P, QT, P], F32R) for i in range(2)]
    q_st = [[sb(f"q_st{g}{p}", [P, N], F32R) for p in range(2)] for g in range(2)]
    k_st = [[[sb(f"k_st{g}{p}{a}", [P, N], F32R) for a in range(2)] for p in range(2)] for g in range(2)]
    probs = [[sb(f"probs{h}{k}", [P, N]) for k in range(QT)] for h in range(2)]
    negmax = [sb(f"negmax{p}", [P, QT, 2]) for p in range(2)]
    nm = [sb(f"nm{p}", [P, QT, 2, 2]) for p in range(2)]
    mt = [sb(f"mt{p}", [4, N], F32R) for p in range(2)]
    o_t = sb("o_t", [P, N])
    rden = sb("rden", [P, QT * GH])

    score = [ps(f"score{i}") for i in range(2)]
    natural = [ps(f"natural{i}") for i in range(2)]
    av = ps("av")
    bank_t = ps("bank_t")
    bank_a = ps("bank_a")
    bank_o = ps("bank_o")

    held = [sem(f"held{i}") for i in range(2)]
    x_first = sem("x_first")
    x_rest = sem("x_rest")
    w_loaded = sem("w_loaded")
    tables = sem("tables")
    w_hi_done = sem("w_hi_done")
    w_split = sem("w_split")
    consts = sem("consts")
    ones_v = sem("ones_v")
    stats_done = sem("stats_done")
    aggr_done = sem("aggr_done")
    var_done = sem("var_done")
    rstd_done = sem("rstd_done")
    xn_done = sem("xn_done")
    xt_ps = sem("xt_ps")
    xth_done = sem("xth_done")
    xtl_done = sem("xtl_done")
    qk_ps = sem("qk_ps")
    qk_out = sem("qk_out")
    v_ps = sem("v_ps")
    v_done = sem("v_done")
    rope_part = sem("rope_part")
    qk_done = sem("qk_done")
    stage_hi = sem("stage_hi")
    staged = sem("staged")
    tr_ps = sem("tr_ps")
    q_done = sem("q_done")
    k_done = sem("k_done")
    nat_ps = sem("nat_ps")
    max_done = sem("max_done")
    nm_hi = sem("nm_hi")
    nm_done = sem("nm_done")
    mt_ps = sem("mt_ps")
    mt_done = sem("mt_done")
    m_in = [sem(f"m_in{p}") for p in range(2)]
    sc_ps = sem("sc_ps")
    exp_done = sem("exp_done")
    av_ps = sem("av_ps")
    ot_done = sem("ot_done")
    nt_ps = sem("nt_ps")
    rden_done = sem("rden_done")
    on_done = sem("on_done")

    x_v = x_in.rearrange("b (t p) d -> p (b t) d", p=P)
    w_v = w_qkv.rearrange("(c p) n -> p c n", p=P)

    A_SLOT = {(0, 1, 1): ("xt", 0), (0, 2, 0): ("xt", 1), (0, 2, 3): ("qk", 0), (0, 3, 1): ("v", 0),
              (0, 3, 3): ("qk", 1), (1, 0, 0): ("v", 1), (1, 0, 3): ("qk", 2), (1, 1, 1): ("v", 2),
              (1, 1, 3): ("qk", 3), (1, 2, 1): ("v", 3)}
    T_SLOT = {(0, 1): (1, 1, "q"), (0, 3): (1, 1, "k"), (2, 1): (2, 0, "q"), (2, 3): (2, 0, "k")}

    def pairs(engine, batch):
        for b in range(2):
            batch(b, b % 2, b > 0, True)
        with engine.Fori(1, B // 2 - 1) as two:
            for odd in range(2):
                batch(two * 2 + odd, odd, True, True)
        for b in range(B - 2, B):
            batch(b, b % 2, True, b < B - 1)

    def sync_engine(sp):
        sp.dma_start(X[:, 0:QT, :], x_v[:, 0:QT, :]).then_inc(x_first, 16)
        sp.dma_start(w_raw[:, :, :], w_v).then_inc(w_loaded, 16)
        sp.dma_start(ident[:, :], ident_in).then_inc(tables, 16)
        sp.dma_start(cos[:, :, :], cos_in.rearrange("(t p) d -> p t d", p=P)).then_inc(tables, 16)
        sp.dma_start(sin[:, :, :], sin_in.rearrange("(t p) d -> p t d", p=P)).then_inc(tables, 16)
        for b in range(1, B):
            sp.dma_start(X[:, b * QT:(b + 1) * QT, :], x_v[:, b * QT:(b + 1) * QT, :]).then_inc(x_rest, 16)

        def max_rows(G, gp, p):
            sp.wait_ge(mt_done, G * 2 + p + 1)
            for a in range(2):
                sp.dma_start(q_st[gp][p][64 * a + 48:64 * a + 50, :].bitcast(F32),
                             mt[p][2 * a:2 * a + 2, :].bitcast(F32)).then_inc(m_in[p], 16)

        max_rows(0, 0, 0)

        def batch(b, odd, has_prev, has_next):
            for g in range(NG):
                max_rows(b * NG + g, g % 2, 1)
                if has_next or g < NG - 1:
                    max_rows(b * NG + g + 1, (g + 1) % 2, 0)
        pairs(sp, batch)

    def gpsimd_engine(pool):
        nc.gpsimd.memset(halves[:, :], -0.5)
        for p in range(2):
            nc.gpsimd.memset(stage_q[p][:, :, :].bitcast(F32), 0.0)
            nc.gpsimd.memset(stage_k[p][:, :, :].bitcast(F32), 0.0)
        for i in range(2):
            last = nc.gpsimd.memset(v_aug[i][:, :, :, :], 1.0)
        last.then_inc(ones_v, 1)
        pool.wait_ge(ones_v, 1)
        for p in range(2):
            ones = stage_k[p][:, :, :].bitcast(F32).rearrange("p t (a r) -> p (t a) r", a=2)
            last = nc.gpsimd.memset(ones[:, :, 48:50], 1.0)
        last.then_inc(consts, 1)
        pool.wait_ge(consts, 2)

        def row_scale(b):
            pool.wait_ge(var_done, b + 1)
            if later(b):
                pool.wait_ge(xn_done, b * QT)
            nc.gpsimd.tensor_tensor(rstd[:, :], vareps[:, :], halves[:, :], ALU.pow).then_inc(rstd_done, 1)

        def rope(b, odd, t):
            n = b * QT + t
            heads = lambda a: a.rearrange("p (h d) -> p h d", d=HD)
            src = heads(qk_raw[t % 2][:, :])
            c = cos[:, t, :].unsqueeze(1).broadcast_to([P, 2 * H, HD])
            s_ = sin[:, t, :]
            pool.wait_ge(qk_out, n + 1)
            if later(n):
                pool.wait_ge(qk_done, n)
            nc.gpsimd.tensor_tensor(heads(rope_a[:, :]), src, c, ALU.mult).then_inc(rope_part, 1)
            nc.gpsimd.tensor_tensor(heads(rope_b[:, :])[:, :, 0:8], src[:, :, 1::2],
                                    s_[:, 0:8].unsqueeze(1).broadcast_to([P, 2 * H, 8]), ALU.mult).then_inc(rope_part, 1)
            nc.gpsimd.tensor_tensor(heads(rope_b[:, :])[:, :, 8:16], src[:, :, 0::2],
                                    s_[:, 8:16].unsqueeze(1).broadcast_to([P, 2 * H, 8]), ALU.mult).then_inc(rope_part, 1)
            pool.wait_ge(rope_part, n * 3 + 3)
            nc.gpsimd.tensor_tensor(qk[odd][:, t, :], rope_a[:, :], rope_b[:, :], ALU.add).then_inc(qk_done, 1)

        def stage(b, odd, g, p):
            G = b * NG + g
            if g == 0 and p == 0:
                pool.wait_ge(qk_done, b * QT + QT)
            for kind, buf, his, lo in (("q", stage_q[p], (0, 32), 16), ("k", stage_k[p], (0, 16), 32)):
                job = G * 4 + 2 * p + (kind == "k")
                c0 = (kind == "k") * D + (g * GH + 2 * p) * HD
                src = qk[odd][:, :, c0:c0 + 2 * HD].rearrange("p t (a j) -> p t a j", a=2)
                part = lambda off, dt: (buf[:, :, :] if dt == F32R else buf[:, :, :].bitcast(F32)).rearrange(
                    "p t (a r) -> p t a r", a=2)[:, :, :, off:off + HD]
                if later(job - 3):
                    pool.wait_ge(tr_ps, job - 3)
                pool.sem_inc(held[1], 1)
                nc.gpsimd.tensor_copy(part(his[0], F32R), src).then_inc(stage_hi, 1)
                nc.gpsimd.tensor_copy(part(his[1], F32R), src)
                pool.wait_ge(stage_hi, job + 1)
                nc.gpsimd.tensor_tensor(part(lo, F32R), src, part(his[0], F32), ALU.subtract).then_inc(staged, 1)

        pool.wait_ge(tables, 48)
        row_scale(0)
        for t in range(QT):
            rope(0, 0, t)
        for g in range(2):
            for p in range(2):
                stage(0, 0, g, p)

        def batch(b, odd, has_prev, has_next):
            if has_next:
                row_scale(b + 1)
            stage(b, odd, 2, 0)
            stage(b, odd, 2, 1)
            if has_next:
                rope(b + 1, 1 - odd, 0)
            stage(b, odd, 3, 0)
            if has_next:
                rope(b + 1, 1 - odd, 1)
            stage(b, odd, 3, 1)
            if has_next:
                rope(b + 1, 1 - odd, 2)
                rope(b + 1, 1 - odd, 3)
                for g in range(2):
                    for p in range(2):
                        stage(b + 1, 1 - odd, g, p)
        pairs(pool, batch)

    def scalar_engine(act):
        def evacuate_t(G, gp, p, kind):
            if kind == "q":
                act.wait_ge(tr_ps, G * 4 + 2 * p + 1)
                if later(G * 16 + 8 * p - 24):
                    act.wait_ge(sc_ps, G * 16 + 8 * p - 24)
                nc.scalar.copy(q_st[gp][p][:, :], bank_t[:, :]).then_inc(q_done, 1)
            else:
                act.wait_ge(tr_ps, G * 4 + 2 * p + 2)
                nc.scalar.copy(k_st[gp][p][0][0:64, :], bank_t[0:64, :])
                nc.scalar.copy(k_st[gp][p][1][64:128, :], bank_t[64:128, :]).then_inc(k_done, 1)

        def a_job(b, odd, what, n):
            if what == "xt":
                act.wait_ge(xt_ps, b * DC + n + 1)
                if later(b) and n == 0:
                    act.wait_ge(v_ps, b * QT)
                nc.scalar.copy(xt_hi[:, n, :], bank_a[:, :]).then_inc(xth_done, 1)
            if what == "qk":
                act.wait_ge(qk_ps, b * QT + n + 1)
                if later(b * QT + n - 1):
                    act.wait_ge(qk_done, b * QT + n - 1)
                nc.scalar.copy(qk_raw[n % 2][:, :], bank_a[:, :]).then_inc(qk_out, 1)
            if what == "v":
                act.wait_ge(v_ps, b * QT + n + 1)
                if later(b * H - H) and n == 0:
                    act.wait_ge(av_ps, b * H - H)
                nc.scalar.copy(v_aug[odd][:, n, :, 0:HD],
                               bank_a[:, 0:D].rearrange("p (h d) -> p h d", d=HD)).then_inc(v_done, 1)

        def max_job(G, p):
            act.wait_ge(mt_ps, G * 2 + p + 1)
            if later(G * 32):
                act.wait_ge(m_in[p], G * 32)
            nc.scalar.copy(mt[p][:, :], bank_o[0:4, :]).then_inc(mt_done, 1)

        def out_job(G):
            act.wait_ge(av_ps, G * GH + GH)
            if later(G):
                act.wait_ge(nt_ps, G)
            nc.scalar.copy(o_t[:, :], av[:, :]).then_inc(ot_done, 1)

        act.wait_ge(tables, 48)
        nc.scalar.copy(ident_r[:, :], ident[:, :]).then_inc(w_hi_done, 1)
        act.wait_ge(w_loaded, 16)
        nc.scalar.copy(w_hi[:, :, :], w_raw[:, :, :]).then_inc(w_hi_done, 1)
        act.wait_ge(consts, 2)
        for n in range(DC):
            a_job(0, 0, "xt", n)
        for t in range(QT):
            a_job(0, 0, "qk", t)
            a_job(0, 0, "v", t)
        for p in range(2):
            for kind in "qk":
                evacuate_t(0, 0, p, kind)
        max_job(0, 0)
        for kind in "qk":
            evacuate_t(1, 1, 0, kind)

        def batch(b, odd, has_prev, has_next):
            for g in range(NG):
                G = b * NG + g
                for i in range(GH):
                    head = b * H + g * GH + i
                    for kt in range(QT):
                        act.wait_ge(sc_ps, head * QT + kt + 1)
                        if kt == 0 and later(head - 1):
                            act.wait_ge(av_ps, head - 1)
                        nc.scalar.activation(probs[i % 2][kt][:, :], score[kt % 2][:, :], ACT.Exp,
                                             scale=HD ** -0.5).then_inc(exp_done, 1)
                        if (i, kt) in T_SLOT:
                            ahead, p, kind = T_SLOT[i, kt]
                            if has_next or g + ahead < NG:
                                evacuate_t(G + ahead, (g + ahead) % 2, p, kind)
                        if (g, i, kt) in A_SLOT and has_next:
                            a_job(b + 1, 1 - odd, *A_SLOT[g, i, kt])
                        if (i, kt) == (0, 2):
                            max_job(G, 1)
                        if (i, kt) == (1, 0) and (has_prev or g > 0):
                            out_job(G - 1)
                        if (i, kt) == (2, 2) and (has_next or g < NG - 1):
                            max_job(G + 1, 0)
        pairs(act, batch)
        out_job(B * NG - 1)

    def vector_engine(dve):
        def norm_stats(b):
            for t in range(QT):
                nc.vector.bn_stats(stats[:, t, :], X[:, bass.ds(b * QT + t, 1), :].rearrange("p a d -> p (a d)")).then_inc(stats_done, 1)
            dve.wait_ge(stats_done, b * QT + QT)
            dve.sem_inc(held[0], 1)
            for t in range(QT):
                nc.vector.bn_aggr(meanvar[:, t, :], stats[:, t, :]).then_inc(aggr_done, 1)
            dve.wait_ge(aggr_done, b * QT + QT)
            nc.vector.tensor_scalar_add(vareps[:, :], meanvar[:, :, 1], EPS).then_inc(var_done, 1)

        def norm_apply(b):
            dve.wait_ge(rstd_done, b + 1)
            if later(b):
                dve.wait_ge(xt_ps, b * DC)
            for t in range(QT):
                nc.vector.tensor_scalar(xn[:, t, :], X[:, bass.ds(b * QT + t, 1), :].rearrange("p a d -> p (a d)"),
                                        meanvar[:, t, 0:1], rstd[:, t:t + 1],
                                        ALU.subtract, ALU.mult).then_inc(xn_done, 1)

        def xt_low(b, c):
            dve.wait_ge(xth_done, b * DC + c + 1)
            nc.vector.tensor_tensor(xt_lo[:, c, :], bank_a[:, :], xt_hi[:, c, :].bitcast(F32),
                                    ALU.subtract).then_inc(xtl_done, 1)

        def row_max(G, i, t):
            n = G * 16 + i * QT + t
            dve.wait_ge(nat_ps, n + 1)
            if i % 2 == 0 and t == 0 and later(G):
                dve.wait_ge(nm_done, G * 2 + i // 2 - 1)
            nc.vector.tensor_reduce(negmax[i // 2][:, t, i % 2:i % 2 + 1], natural[t % 2][:, :], AX.X, ALU.max,
                                    negate=True).then_inc(max_done, 1)

        def max_split(G, p):
            dve.wait_ge(max_done, G * 16 + 8 * p + 8)
            if later(G):
                dve.wait_ge(mt_ps, G * 2 + p - 1)
            nc.vector.tensor_copy(nm[p][:, :, :, 0].bitcast(F32R), negmax[p][:, :, :]).then_inc(nm_hi, 1)
            dve.wait_ge(nm_hi, G * 2 + p + 1)
            nc.vector.tensor_tensor(nm[p][:, :, :, 1], negmax[p][:, :, :], nm[p][:, :, :, 0],
                                    ALU.subtract).then_inc(nm_done, 1)

        def normalise(b, g):
            G = b * NG + g
            dve.wait_ge(nt_ps, G + 1)
            view = bank_o[:, :].rearrange("p (t i) -> p t i", i=2 * HD)
            nc.vector.reciprocal(rden[:, :], view[:, :, HD]).then_inc(rden_done, 1)
            dve.wait_ge(rden_done, G + 1)
            nc.vector.tensor_tensor(
                O[:, bass.ds(b * QT, QT), g * GH * HD:(g + 1) * GH * HD].rearrange("p t (i j) -> p t i j", i=GH),
                view[:, :, 0:HD].rearrange("p (t i) j -> p t i j", t=QT),
                rden[:, :].rearrange("p (t i) -> p t i", t=QT).unsqueeze(3).broadcast_to([P, QT, GH, HD]),
                ALU.mult).then_inc(on_done, 1)

        for g in range(2):
            for p in range(2):
                nc.vector.memset(k_st[g][p][0][64:128, :].bitcast(F32), 0.0)
                last = nc.vector.memset(k_st[g][p][1][0:64, :].bitcast(F32), 0.0)
        last.then_inc(consts, 1)
        dve.wait_ge(x_first, 16)
        norm_stats(0)
        dve.wait_ge(w_hi_done, 2)
        nc.vector.tensor_tensor(w_lo[:, :, :], w_raw[:, :, :], w_hi[:, :, :].bitcast(F32),
                                ALU.subtract).then_inc(w_split, 1)
        norm_apply(0)
        for c in range(DC):
            xt_low(0, c)
        for i in range(GH):
            if i == 2:
                max_split(0, 0)
            for t in range(QT):
                row_max(0, i, t)
        dve.wait_ge(x_rest, 16 * (B - 1))

        def batch(b, odd, has_prev, has_next):
            for g in range(NG):
                G = b * NG + g
                ahead = has_next or g < NG - 1
                for i in range(GH):
                    for kt in range(QT):
                        if (i, kt) == (0, 0):
                            max_split(G, 1)
                        if (i, kt) == (2, 0) and ahead:
                            max_split(G + 1, 0)
                        if ahead:
                            row_max(G + 1, i, kt)
                        if g == 0 and has_next:
                            if (i, kt) == (0, 1):
                                norm_stats(b + 1)
                            if (i, kt) == (1, 0):
                                norm_apply(b + 1)
                        if A_SLOT.get((g, i, kt), ("", 0))[0] == "xt" and has_next:
                            xt_low(b + 1, A_SLOT[g, i, kt][1])
                        if (i, kt) == (1, 2) and g > 0:
                            normalise(b, g - 1)
                        if (i, kt) == (1, 2) and g == 0 and has_prev:
                            normalise(b - 1, NG - 1)
        pairs(dve, batch)
        normalise(B - 1, NG - 1)

    def tensor_engine(pe):
        def a_job(b, what, n):
            if what == "xt":
                pe.wait_ge(xn_done, b * QT + QT)
                if n == 0:
                    if later(b):
                        pe.wait_ge(v_done, b * QT)
                else:
                    pe.wait_ge(xtl_done, b * DC + n)
                for t in range(QT):
                    last = nc.tensor.transpose(bank_a[:, t * P:(t + 1) * P], xn[:, t, n * P:(n + 1) * P], ident[:, :])
                last.then_inc(xt_ps, 1)
                return
            if what == "qk":
                cols, out = slice(0, 2 * D), bank_a[:, :]
                if n == 0:
                    pe.wait_ge(xtl_done, b * DC + DC)
                else:
                    pe.wait_ge(v_done, b * QT + n)
            else:
                cols, out = slice(2 * D, 3 * D), bank_a[:, 0:D]
                pe.wait_ge(qk_out, b * QT + n + 1)
            terms = [(c, x, w) for c in range(DC) for x, w in ((xt_lo, w_hi), (xt_hi, w_lo), (xt_hi, w_hi))]
            for k, (c, x, w) in enumerate(terms):
                last = nc.tensor.matmul(out, x[:, c, n * P:(n + 1) * P], w[:, c, cols],
                                        start=k == 0, stop=k == len(terms) - 1)
            last.then_inc(qk_ps if what == "qk" else v_ps, 1)

        def t_job(G, p, kind):
            if kind == "q":
                pe.wait_ge(staged, G * 4 + 2 * p + 1)
                if later(G * 2 + p):
                    pe.wait_ge(k_done, G * 2 + p)
                src = stage_q[p]
            else:
                pe.wait_ge(staged, G * 4 + 2 * p + 2)
                pe.wait_ge(q_done, G * 2 + p + 1)
                src = stage_k[p]
            for t in range(QT):
                last = nc.tensor.matmul(bank_t[:, t * P:(t + 1) * P], src[:, t, :], ident_r[:, :], start=True, stop=True)
            last.then_inc(tr_ps, 1)

        def natural_scores(G, gp, i, t):
            p, a = i // 2, i % 2
            n = G * 16 + i * QT + t
            if a == 0 and t == 0:
                pe.wait_ge(k_done, G * 2 + p + 1)
            if later(n - 1):
                pe.wait_ge(max_done, n - 1)
            nc.tensor.matmul(natural[t % 2][:, :], q_st[gp][p][:, t * P:(t + 1) * P], k_st[gp][p][a][:, :],
                             start=True, stop=True).then_inc(nat_ps, 1)

        def m_job(G, p):
            pe.wait_ge(nm_done, G * 2 + p + 1)
            if later(G * 2 + p):
                pe.wait_ge(mt_done, G * 2 + p)
            if p == 0 and later(G - 1):
                pe.wait_ge(on_done, G - 1)
            for t in range(QT):
                last = nc.tensor.transpose(bank_o[0:4, t * P:(t + 1) * P],
                                           nm[p][:, t, :, :].rearrange("p i s -> p (i s)"), ident[:, :])
            last.then_inc(mt_ps, 1)

        def n_job(G, before_mt):
            pe.wait_ge(ot_done, G + 1)
            pe.wait_ge(mt_done, before_mt)
            for t in range(QT):
                last = nc.tensor.transpose(bank_o[:, t * P:(t + 1) * P], o_t[:, t * P:(t + 1) * P], ident[:, :])
            last.then_inc(nt_ps, 1)

        def attend(b, odd, hl, kt):
            head = b * H + hl
            i = hl % GH
            pe.wait_ge(exp_done, head * QT + kt + 1)
            if i == 0 and kt == 0 and later(b * NG + hl // GH):
                pe.wait_ge(ot_done, b * NG + hl // GH)
            if hl == 0 and kt == 0:
                pe.wait_ge(v_done, b * QT + QT)
            last = nc.tensor.matmul(av[32 * i:32 * i + 32, :], v_aug[odd][:, kt, hl, :], probs[hl % 2][kt][:, :],
                                    start=kt == 0, stop=kt == QT - 1)
            if kt == QT - 1:
                last.then_inc(av_ps, 1)

        pe.wait_ge(w_hi_done, 2)
        pe.wait_ge(consts, 2)
        for n in range(DC):
            a_job(0, "xt", n)
        pe.wait_ge(w_split, 1)
        for t in range(QT):
            a_job(0, "qk", t)
            a_job(0, "v", t)
        for p in range(2):
            for kind in "qk":
                t_job(0, p, kind)
        for i in range(GH):
            for t in range(QT):
                natural_scores(0, 0, i, t)
            if i == 2:
                m_job(0, 0)
        for kind in "qk":
            t_job(1, 0, kind)

        def batch(b, odd, has_prev, has_next):
            for g in range(NG):
                G = b * NG + g
                gp = g % 2
                for i in range(GH):
                    p, a = i // 2, i % 2
                    hl = g * GH + i
                    for kt in range(QT):
                        n = (b * H + hl) * QT + kt
                        if kt == 0 and a == 0:
                            pe.wait_ge(m_in[p], (G + 1) * 32)
                        if later(n - 1):
                            pe.wait_ge(exp_done, n - 1)
                        nc.tensor.matmul(score[kt % 2][:, :], k_st[gp][p][a][:, kt * P:(kt + 1) * P],
                                         q_st[gp][p][:, :], start=True, stop=True).then_inc(sc_ps, 1)
                        if has_next or g < NG - 1:
                            natural_scores(G + 1, 1 - gp, i, kt)
                        if hl > 0:
                            attend(b, odd, hl - 1, kt)
                        elif has_prev:
                            attend(b - 1, 1 - odd, H - 1, kt)
                        if (i, kt) in T_SLOT:
                            ahead, tp, kind = T_SLOT[i, kt]
                            if has_next or g + ahead < NG:
                                t_job(G + ahead, tp, kind)
                        if (g, i, kt) in A_SLOT and has_next:
                            a_job(b + 1, *A_SLOT[g, i, kt])
                        if (i, kt) == (0, 2):
                            m_job(G, 1)
                        if (i, kt) == (1, 1) and (has_prev or g > 0):
                            n_job(G - 1, G * 2 + 2)
                        if (i, kt) == (2, 2) and (has_next or g < NG - 1):
                            m_job(G + 1, 0)
        pairs(pe, batch)
        for kt in range(QT):
            attend(B - 1, (B - 1) % 2, H - 1, kt)
        pe.wait_ge(on_done, B * NG - 1)
        n_job(B * NG - 1, B * NG * 2)

    return sync_engine, gpsimd_engine, scalar_engine, vector_engine, tensor_engine


NT = B * QT
E, HID = 16, 128
S = 512
SC = S // P
U32 = mybir.dt.uint32


class Chain:

    def __init__(self, engine, semaphore, per):
        self.engine, self.semaphore, self.per, self.round, self.n = engine, semaphore, per, 0, 0

    def start(self, round_):
        assert self.n in (0, self.per), self.n
        self.round, self.n = round_, 0

    def step(self, instruction):
        self.n += 1
        instruction.then_inc(self.semaphore, 1)
        self.engine.wait_ge(self.semaphore, self.round * self.per + self.n)


def for_rows(engine, row):
    row(0)
    with engine.Fori(1, B) as b:
        row(b)


def run_block(nc, sync=None, gpsimd=None, scalar=None, vector=None, tensor=None):
    with nc.Block() as block:
        if sync:
            block.sync(sync)
        if gpsimd:
            block.gpsimd(gpsimd)
        if scalar:
            block.scalar(scalar)
        if vector:
            block.vector(vector)
        if tensor:
            block.tensor(tensor)


def tiles_of(T, b, n=QT):
    return T[:, bass.ds(b * QT, n), :]


def feed_forward(nc, ctx, w_out, b_out, gate_t, w1_t, w2_t, s1_t, s2_t, s3_t, iota_in, out, X, O, ident):
    def sb(name, shape, dt=F32):
        return ctx.enter_context(nc.sbuf_tensor(name, shape, dt))

    def sem(name):
        return ctx.enter_context(nc.semaphore(name))

    raw = [sb(f"raw{i}", [P, 2048]) for i in range(2)]
    weights = []
    def split_weight(name, dram, inner):
        hi, lo = sb(name + "_hi", [P, inner], F32R), sb(name + "_lo", [P, inner], F32R)
        for c in range(0, inner, 2048):
            weights.append((dram[:, c:min(c + 2048, inner)], hi[:, c:min(c + 2048, inner)], lo[:, c:min(c + 2048, inner)]))
        return hi, lo
    wo = split_weight("wo", w_out, DC * D)
    gw = split_weight("gw", gate_t, DC * P)
    s1 = split_weight("s1w", s1_t, DC * S)
    s2 = split_weight("s2w", s2_t, DC * S)
    s3 = split_weight("s3w", s3_t, SC * D)
    w1 = split_weight("w1w", w1_t, E * DC * HID)
    w2 = split_weight("w2w", w2_t, E * D)
    bias = sb("bias", [P, D])
    halves = sb("halves32", [P, NT])
    iota = sb("iota", [P, E])
    stats = sb("stats32", [P, NT, 6])
    meanvar = sb("meanvar32", [P, NT, 2])
    vareps = sb("vareps32", [P, NT])
    rstd = sb("rstd32", [P, NT])
    flat = sb("flat", [P, QT, D])
    t_hi = sb("t_hi", [P, DC, N], F32R)
    t_lo = sb("t_lo", [P, DC, N], F32R)
    lt = sb("lt", [E, N])
    logits = sb("logits", [P, QT, E])
    top = sb("top", [P, QT, 8])
    topi = sb("topi", [P, QT, 8], U32)
    ids = sb("ids", [P, NT, 2])
    ratio = sb("ratio", [P, QT])
    wts = sb("wts", [P, NT, 2])
    den = sb("den", [P, QT])
    disp = sb("disp", [P, NT, E])
    onehot = sb("onehot", [P, QT, E])
    silu = [sb(f"silu{i}", [P, N]) for i in range(2)]
    h_hi = [sb(f"h_hi{i}", [P, N], F32R) for i in range(2)]
    h_lo = [sb(f"h_lo{i}", [P, N], F32R) for i in range(2)]
    acc = raw[0][:, 0:QT * D].rearrange("p (t d) -> p t d", t=QT)

    def three(out_ap, pieces, first=True, last=True):
        k = 0
        for st, mv in pieces:
            for a, b in ((st[1], mv[0]), (st[0], mv[1]), (st[0], mv[0])):
                ins = nc.tensor.matmul(out_ap, a, b, start=first and k == 0, stop=last and k == 3 * len(pieces) - 1)
                k += 1
        return ins

    def three_acc(out_ap, st, mv, start, stop):
        for k, (a, b) in enumerate(((st[1], mv[0]), (st[0], mv[1]), (st[0], mv[0]))):
            ins = nc.tensor.matmul(out_ap, a, b, start=start and k == 0, stop=stop and k == 2, skip_group_check=True)
        return ins

    def t_parts(c, cols):
        return t_hi[:, c, cols], t_lo[:, c, cols]

    def part(w, c0, n):
        return w[0][:, c0:c0 + n], w[1][:, c0:c0 + n]

    with ExitStack() as sub:
        ws = [sub.enter_context(nc.semaphore(f"raw_in{i}")) for i in range(2)]
        small = sub.enter_context(nc.semaphore("small_in"))
        hi_s = sub.enter_context(nc.semaphore("w_hi_s"))
        lo_s = sub.enter_context(nc.semaphore("w_lo_s"))

        def sync(sp):
            sp.dma_start(bias[:, :], b_out[None, :].broadcast_to([P, D])).then_inc(small, 16)
            sp.dma_start(iota[:, :], iota_in).then_inc(small, 16)
            for n, (dram, hi, lo) in enumerate(weights):
                if n >= 2:
                    sp.wait_ge(lo_s, n - 1)
                sp.dma_start(raw[n % 2][:, 0:dram.shape[1]], dram).then_inc(ws[n % 2], 16)
            sp.wait_ge(small, 32)

        def gpsimd(pool):
            nc.gpsimd.memset(halves[:, :], -0.5)

        def scalar(act):
            for n, (dram, hi, lo) in enumerate(weights):
                act.wait_ge(ws[n % 2], 16 * (n // 2 + 1))
                nc.scalar.copy(hi, raw[n % 2][:, 0:dram.shape[1]]).then_inc(hi_s, 1)

        def vector(dve):
            for n, (dram, hi, lo) in enumerate(weights):
                dve.wait_ge(hi_s, n + 1)
                nc.vector.tensor_tensor(lo, raw[n % 2][:, 0:dram.shape[1]], hi.bitcast(F32), ALU.subtract).then_inc(lo_s, 1)
        run_block(nc, sync=sync, gpsimd=gpsimd, scalar=scalar, vector=vector)

    with ExitStack() as sub:
        psem = lambda name: sub.enter_context(nc.semaphore(name))
        flat_s, tr_s, hi_s, lo_s, y_s, yb_s, bn_s, var_s = (psem(x) for x in (
            "p_flat", "p_tr", "p_hi", "p_lo", "p_y", "p_yb", "p_bn", "p_var"))
        bank_t = [sub.enter_context(nc.psum_tensor(f"p_t{c}", [P, N], F32)) for c in range(DC)]
        bank_y = [sub.enter_context(nc.psum_tensor(f"p_y{c}", [P, 2, D], F32)) for c in range(2)]

        def scalar(act):
            def row(b):
                if later(b):
                    if later(b * DC):
                        act.wait_ge(tr_s, b * DC)
                nc.scalar.copy(flat[:, :, :], tiles_of(O, b)).then_inc(flat_s, 1)
                for c in range(DC):
                    act.wait_ge(tr_s, b * DC + c + 1)
                    if later(b):
                        if later(b * QT):
                            act.wait_ge(y_s, b * QT)
                    nc.scalar.copy(t_hi[:, c, :], bank_t[c][:, :]).then_inc(hi_s, 1)
            for_rows(act, row)

        def vector(dve):
            def row(b):
                for c in range(DC):
                    dve.wait_ge(hi_s, b * DC + c + 1)
                    nc.vector.tensor_tensor(t_lo[:, c, :], bank_t[c][:, :], t_hi[:, c, :].bitcast(F32), ALU.subtract).then_inc(lo_s, 1)
                for t in range(QT):
                    dve.wait_ge(y_s, b * QT + t // 2 * 2 + 2)
                    nc.vector.tensor_tensor(O[:, bass.ds(b * QT + t, 1), :], bank_y[t // 2][:, t % 2:t % 2 + 1, :], bias[:, :].unsqueeze(1), ALU.add).then_inc(yb_s, 1)
                for t in range(QT):
                    dve.wait_ge(yb_s, b * QT + t + 1)
                    nc.vector.bn_stats(stats[:, bass.ds(b * QT + t, 1), :].rearrange("p a d -> p (a d)"), O[:, bass.ds(b * QT + t, 1), :].rearrange("p a d -> p (a d)")).then_inc(bn_s, 1)
            for_rows(dve, row)
            for t in range(NT):
                dve.wait_ge(bn_s, t + 1)
                last = nc.vector.bn_aggr(meanvar[:, t, :], stats[:, t, :])
            last.then_inc(bn_s, 1)
            dve.wait_ge(bn_s, NT + 1)
            nc.vector.tensor_scalar_add(vareps[:, :], meanvar[:, :, 1], EPS).then_inc(var_s, 1)

        def gpsimd(pool):
            pool.wait_ge(var_s, 1)
            nc.gpsimd.tensor_tensor(rstd[:, :], vareps[:, :], halves[:, :], ALU.pow)

        def tensor(pe):
            def transposes(b):
                pe.wait_ge(flat_s, b + 1)
                for c in range(DC):
                    if later(b):
                        pe.wait_ge(lo_s, (b - 1) * DC + c + 1)
                    for t in range(QT):
                        last = nc.tensor.transpose(bank_t[c][:, t * P:(t + 1) * P], flat[:, t, c * P:(c + 1) * P], ident[:, :])
                    last.then_inc(tr_s, 1)

            def project(b):
                pe.wait_ge(lo_s, b * DC + DC)
                for t in range(QT):
                    if later(b):
                        if later((b - 1) * QT + t // 2 * 2 + 2):
                            pe.wait_ge(yb_s, (b - 1) * QT + t // 2 * 2 + 2)
                    three(bank_y[t // 2][:, t % 2, :], [(t_parts(c, slice(t * P, (t + 1) * P)), part(wo, c * D, D)) for c in range(DC)]).then_inc(y_s, 1)

            transposes(0)
            project(0)
            with pe.Fori(1, B) as b:
                transposes(b)
                project(b)
        run_block(nc, gpsimd=gpsimd, scalar=scalar, vector=vector, tensor=tensor)

    with ExitStack() as sub:
        psem = lambda name: sub.enter_context(nc.semaphore(name))
        z_s, x1_s, bn_s, var_s = (psem(x) for x in ("r_z", "r_x1", "r_bn", "r_var"))

        def vector(dve):
            one = lambda T, n: T[:, bass.ds(n, 1), :].rearrange("p a d -> p (a d)")
            def row(b):
                for t in range(QT):
                    n = b * QT + t
                    nc.vector.tensor_scalar(one(O, n), one(O, n), meanvar[:, bass.ds(n, 1), 0], rstd[:, bass.ds(n, 1)], ALU.subtract, ALU.mult).then_inc(z_s, 1)
                for t in range(QT):
                    dve.wait_ge(z_s, b * QT + t + 1)
                    nc.vector.tensor_tensor(one(X, b * QT + t), one(X, b * QT + t), one(O, b * QT + t), ALU.add).then_inc(x1_s, 1)
                for t in range(QT):
                    dve.wait_ge(x1_s, b * QT + t + 1)
                    nc.vector.bn_stats(one(stats, b * QT + t), one(X, b * QT + t)).then_inc(bn_s, 1)
            for_rows(dve, row)
            for t in range(NT):
                dve.wait_ge(bn_s, t + 1)
                last = nc.vector.bn_aggr(meanvar[:, t, :], stats[:, t, :])
            last.then_inc(bn_s, 1)
            dve.wait_ge(bn_s, NT + 1)
            nc.vector.tensor_scalar_add(vareps[:, :], meanvar[:, :, 1], EPS).then_inc(var_s, 1)

        def gpsimd(pool):
            pool.wait_ge(var_s, 1)
            nc.gpsimd.tensor_tensor(rstd[:, :], vareps[:, :], halves[:, :], ALU.pow)
        run_block(nc, gpsimd=gpsimd, vector=vector)

    with ExitStack() as sub:
        psem = lambda name: sub.enter_context(nc.semaphore(name))
        x2_s, keep_s, tr_s, hi_s, lo_s, g_s, lt_s, lg_s, chain_s, gap_s, ratio_s, route_s, held = (psem(x) for x in (
            "g_x2", "g_keep", "g_tr", "g_hi", "g_lo", "g_g", "g_lt", "g_lg", "g_chain", "g_gap", "g_ratio", "g_route", "g_held"))
        bank_t = [sub.enter_context(nc.psum_tensor(f"g_t{c}", [P, N], F32)) for c in range(DC)]
        bank_g = sub.enter_context(nc.psum_tensor("g_g_bank", [P, N], F32))
        bank_l = sub.enter_context(nc.psum_tensor("g_l_bank", [P, QT, E], F32))

        def scalar(act):
            def row(b):
                for t in range(QT):
                    act.wait_ge(x2_s, b * QT + t + 1)
                nc.scalar.copy(tiles_of(O, b), flat[:, :, :]).then_inc(keep_s, 1)
                for c in range(DC):
                    act.wait_ge(tr_s, b * DC + c + 1)
                    if later(b):
                        act.wait_ge(g_s, b)
                    nc.scalar.copy(t_hi[:, c, :], bank_t[c][:, :]).then_inc(hi_s, 1)
                act.wait_ge(g_s, b + 1)
                if later(b):
                    act.wait_ge(lg_s, b)
                nc.scalar.copy(lt[:, :], bank_g[0:E, :]).then_inc(lt_s, 1)
                act.wait_ge(gap_s, b + 1)
                nc.scalar.activation(ratio[:, :], den[:, :], ACT.Exp).then_inc(ratio_s, 1)
            for_rows(act, row)

        def vector(dve):
            chain = Chain(dve, chain_s, 1 + 1 + 1 + 1 + 1 + 1 + 1 + 2 * 4)
            def row(b):
                chain.start(b)
                if later(b):
                    dve.wait_ge(keep_s, b)
                if later(b * DC):
                    dve.wait_ge(tr_s, b * DC)
                for t in range(QT):
                    nc.vector.tensor_scalar(flat[:, t, :], X[:, bass.ds(b * QT + t, 1), :].rearrange("p a d -> p (a d)"), meanvar[:, bass.ds(b * QT + t, 1), 0], rstd[:, bass.ds(b * QT + t, 1)], ALU.subtract, ALU.mult).then_inc(x2_s, 1)
                for c in range(DC):
                    dve.wait_ge(hi_s, b * DC + c + 1)
                    nc.vector.tensor_tensor(t_lo[:, c, :], bank_t[c][:, :], t_hi[:, c, :].bitcast(F32), ALU.subtract).then_inc(lo_s, 1)
                dve.wait_ge(lg_s, b + 1)
                chain.step(nc.vector.tensor_copy(logits[:, :, :], bank_l[:, :, :]))
                dve.sem_inc(held, 1)
                for t in range(QT):
                    last = nc.vector.max(top[:, t, :], logits[:, t, :])
                chain.step(last)
                dve.sem_inc(held, 1)
                for t in range(QT):
                    last = nc.vector.max_index(topi[:, t, :], top[:, t, :], logits[:, t, :])
                chain.step(last)
                chain.step(nc.vector.tensor_copy(ids[:, bass.ds(b * QT, QT), :], topi[:, :, 0:2]))
                nc.vector.tensor_tensor(den[:, :], top[:, :, 1], top[:, :, 0], ALU.subtract).then_inc(gap_s, 1)
                dve.wait_ge(ratio_s, b + 1)
                chain.step(nc.vector.tensor_scalar_add(den[:, :], ratio[:, :], 1.0))
                chain.step(nc.vector.reciprocal(wts[:, bass.ds(b * QT, QT), 0], den[:, :]))
                chain.step(nc.vector.tensor_tensor(wts[:, bass.ds(b * QT, QT), 1], ratio[:, :], wts[:, bass.ds(b * QT, QT), 0], ALU.mult))
                for t in range(QT):
                    n = b * QT + t
                    row = disp[:, bass.ds(n, 1), :].rearrange("p a e -> p (a e)")
                    chain.step(nc.vector.tensor_scalar(onehot[:, t, :], iota[:, :], ids[:, bass.ds(n, 1), 0], wts[:, bass.ds(n, 1), 0], ALU.is_equal, ALU.mult))
                    chain.step(nc.vector.tensor_scalar(row, iota[:, :], ids[:, bass.ds(n, 1), 1], wts[:, bass.ds(n, 1), 1], ALU.is_equal, ALU.mult))
                    nc.vector.tensor_tensor(row, row, onehot[:, t, :], ALU.add).then_inc(route_s, 1)
            for_rows(dve, row)

        def tensor(pe):
            def row(b):
                pe.wait_ge(x2_s, b * QT + QT)
                for c in range(DC):
                    if later(b * DC):
                        pe.wait_ge(lo_s, b * DC)
                    for t in range(QT):
                        last = nc.tensor.transpose(bank_t[c][:, t * P:(t + 1) * P], flat[:, t, c * P:(c + 1) * P], ident[:, :])
                    last.then_inc(tr_s, 1)
                pe.wait_ge(lo_s, b * DC + DC)
                if later(b):
                    pe.wait_ge(lt_s, b)
                three(bank_g[:, :], [(part(gw, c * P, P), t_parts(c, slice(0, N))) for c in range(DC)]).then_inc(g_s, 1)
                pe.wait_ge(lt_s, b + 1)
                if later(b * QT):
                    pe.wait_ge(route_s, b * QT)
                pe.sem_inc(held, 1)
                for t in range(QT):
                    last = nc.tensor.transpose(bank_l[:, t, :], lt[:, t * P:(t + 1) * P], ident[0:E, 0:E])
                last.then_inc(lg_s, 1)
            for_rows(pe, row)

        run_block(nc, scalar=scalar, vector=vector, tensor=tensor)

    with ExitStack() as sub:
        psem = lambda name: sub.enter_context(nc.semaphore(name))
        (flat_s, tr_s, hi_s, lo_s, a_s, g_s, silu_s, h_s, hh_s, hl_s, sh_s, acc_s, eh_s, es_s, ehh_s, ehl_s, ey_s,
         ea_s, chain_s, var_s, rs_s, res_s, out_s, held) = (psem("e_" + x) for x in (
            "flat tr hi lo a g silu h hh hl sh acc eh es ehh ehl ey ea chain var rs res out held").split())
        bank = [sub.enter_context(nc.psum_tensor(f"e{i}", [P, N], F32)) for i in range(8)]
        out_v = out.rearrange("b (t p) d -> p (b t) d", p=P)

        CH = SC + E

        def sync(sp):
            def row(b):
                sp.wait_ge(res_s, b * QT + QT)
                sp.dma_start(out_v[:, bass.ds(b * QT, QT), :], tiles_of(X, b)).then_inc(out_s, 16)
            for_rows(sp, row)
            sp.wait_ge(out_s, 16 * B)

        def scalar(act):
            def row(b):
                if later(b * DC):
                    act.wait_ge(tr_s, b * DC)
                nc.scalar.copy(flat[:, :, :], tiles_of(O, b)).then_inc(flat_s, 1)
                for c in range(DC):
                    act.wait_ge(tr_s, b * DC + c + 1)
                    if later(b * CH):
                        act.wait_ge(a_s, b * CH)
                    nc.scalar.copy(t_hi[:, c, :], bank[c][:, :]).then_inc(hi_s, 1)
                for n in range(CH):
                    m = b * CH + n
                    act.wait_ge(a_s, m + 1)
                    if n == 0:
                        act.wait_ge(hl_s, m)
                    elif n > 1:
                        act.wait_ge(hl_s, m - 1)
                    nc.scalar.activation(silu[n % 2][:, :], bank[2 + n % 2][:, :], ACT.Silu).then_inc(silu_s, 1)
                    if n < SC:
                        act.wait_ge(h_s, b * SC + n + 1)
                    else:
                        act.wait_ge(silu_s, m + 1)
                    if n == 0:
                        act.wait_ge(ey_s, m)
                    elif n > 1:
                        act.wait_ge(ey_s, m - 1)
                    nc.scalar.copy(h_hi[n % 2][:, :], silu[n % 2][:, :]).then_inc(hh_s, 1)
            for_rows(act, row)

        def vector(dve):
            chain = Chain(dve, chain_s, QT + 1 + 1 + QT)
            def row(b):
                chain.start(b)
                for c in range(DC):
                    dve.wait_ge(hi_s, b * DC + c + 1)
                    nc.vector.tensor_tensor(t_lo[:, c, :], bank[c][:, :], t_hi[:, c, :].bitcast(F32), ALU.subtract).then_inc(lo_s, 1)
                for n in range(CH):
                    m = b * CH + n
                    if n < SC:
                        dve.wait_ge(silu_s, m + 1)
                        dve.wait_ge(g_s, b * SC + n + 1)
                        nc.vector.tensor_tensor(silu[n % 2][:, :], silu[n % 2][:, :], bank[4][:, :], ALU.mult).then_inc(h_s, 1)
                    dve.wait_ge(hh_s, m + 1)
                    nc.vector.tensor_tensor(h_lo[n % 2][:, :], silu[n % 2][:, :], h_hi[n % 2][:, :].bitcast(F32), ALU.subtract).then_inc(hl_s, 1)
                    if n == SC - 1:
                        dve.wait_ge(ey_s, b * CH + SC)
                        for half in range(2):
                            last = nc.vector.tensor_copy(acc[:, 2 * half:2 * half + 2, :].rearrange("p t d -> p (t d)"), bank[6 + half][:, :])
                        last.then_inc(acc_s, 1)
                        dve.wait_ge(acc_s, b * (E + 1) + 1)
                    if n >= SC:
                        e = n - SC
                        dve.wait_ge(ey_s, m + 1)
                        for t in range(QT):
                            last = nc.vector.scalar_tensor_tensor(acc[:, t, :], bank[6 + t // 2][:, (t % 2) * D:(t % 2 + 1) * D], disp[:, bass.ds(b * QT + t, 1), e], acc[:, t, :], ALU.mult, ALU.add)
                        last.then_inc(acc_s, 1)
                        dve.wait_ge(acc_s, b * (E + 1) + e + 2)
                for t in range(QT):
                    chain.step(nc.vector.bn_stats(stats[:, t, :], acc[:, t, :]))
                dve.sem_inc(held, 1)
                for t in range(QT):
                    last = nc.vector.bn_aggr(meanvar[:, t, :], stats[:, t, :])
                chain.step(last)
                nc.vector.tensor_scalar_add(vareps[:, 0:QT], meanvar[:, 0:QT, 1], EPS).then_inc(var_s, 1)
                dve.wait_ge(rs_s, b + 1)
                chain.step(nc.vector.tensor_copy(den[:, :], rstd[:, 0:QT]))
                for t in range(QT):
                    chain.step(nc.vector.tensor_scalar(acc[:, t, :], acc[:, t, :], meanvar[:, t, 0:1], rstd[:, t:t + 1], ALU.subtract, ALU.mult))
                    nc.vector.tensor_tensor(X[:, bass.ds(b * QT + t, 1), :], X[:, bass.ds(b * QT + t, 1), :], acc[:, t:t + 1, :], ALU.add).then_inc(res_s, 1)
            for_rows(dve, row)

        def gpsimd(pool):
            def row(b):
                pool.wait_ge(var_s, b + 1)
                nc.gpsimd.tensor_tensor(rstd[:, 0:QT], vareps[:, 0:QT], halves[:, 0:QT], ALU.pow).then_inc(rs_s, 1)
            for_rows(pool, row)

        def tensor(pe):
            def row(b):
                pe.wait_ge(flat_s, b + 1)
                for c in range(DC):
                    if later(b * DC):
                        pe.wait_ge(lo_s, b * DC)
                    for t in range(QT):
                        last = nc.tensor.transpose(bank[c][:, t * P:(t + 1) * P], flat[:, t, c * P:(c + 1) * P], ident[:, :])
                    last.then_inc(tr_s, 1)
                pe.wait_ge(lo_s, b * DC + DC)

                def first(n):
                    m = b * CH + n
                    if n == 0:
                        pe.wait_ge(silu_s, m)
                    elif n > 1:
                        pe.wait_ge(silu_s, m - 1)
                    if n < SC:
                        w = [part(s1, c * S + n * P, P) for c in range(DC)]
                        v = [part(s2, c * S + n * P, P) for c in range(DC)]
                        three(bank[2 + n % 2][:, :], [(w[c], t_parts(c, slice(0, N))) for c in range(DC)]).then_inc(a_s, 1)
                        pe.wait_ge(h_s, b * SC + n)
                        three(bank[4][:, :], [(v[c], t_parts(c, slice(0, N))) for c in range(DC)]).then_inc(g_s, 1)
                    else:
                        w = [part(w1, ((n - SC) * DC + c) * HID, HID) for c in range(DC)]
                        three(bank[2 + n % 2][:, :], [(w[c], t_parts(c, slice(0, N))) for c in range(DC)]).then_inc(a_s, 1)

                def second(n):
                    m = b * CH + n
                    pe.wait_ge(hl_s, m + 1)
                    if n == 0:
                        if later(b * (E + 1)):
                            pe.wait_ge(acc_s, b * (E + 1))
                    if n >= SC:
                        pe.wait_ge(acc_s, b * (E + 1) + n - SC + 1)
                    w = part(s3, n * D, D) if n < SC else part(w2, (n - SC) * D, D)
                    for t in range(QT):
                        lhs = (h_hi[n % 2][:, t * P:(t + 1) * P], h_lo[n % 2][:, t * P:(t + 1) * P])
                        last = three_acc(bank[6 + t // 2][:, (t % 2) * D:(t % 2 + 1) * D], lhs, w,
                                         (n == 0 or n >= SC) and t % 2 == 0, n >= SC - 1)
                    last.then_inc(ey_s, 1)

                for n in range(CH):
                    first(n)
                    if n:
                        second(n - 1)
                second(CH - 1)
            for_rows(pe, row)

        run_block(nc, sync=sync, gpsimd=gpsimd, scalar=scalar, vector=vector, tensor=tensor)


def transformer_layer(nc, x, w_qkv, w_out, b_out, gate_t, w1_t, w2_t, s1_t, s2_t, s3_t, cos, sin, ident_in, iota, out):
    with ExitStack() as ctx:
        X = ctx.enter_context(nc.sbuf_tensor("X", [P, NT, D], F32))
        O = ctx.enter_context(nc.sbuf_tensor("O", [P, NT, D], F32))
        ident = ctx.enter_context(nc.sbuf_tensor("identity", [P, P], F32))
        ident_r = ctx.enter_context(nc.sbuf_tensor("identity_r", [P, P], F32R))
        with ExitStack() as sub:
            sync, gpsimd, scalar, vector, tensor = attention(nc, sub, x, w_qkv, cos, sin, ident_in, X, O, ident, ident_r)
            run_block(nc, sync, gpsimd, scalar, vector, tensor)
        with ExitStack() as sub:
            feed_forward(nc, sub, w_out, b_out, gate_t, w1_t, w2_t, s1_t, s2_t, s3_t, iota, out, X, O, ident)


def kernel(L0_attn_x, L0_attn_w_qkv, L0_attn_w_out, L0_attn_b_out, L0_ffn_gate_w, L0_ffn_w1, L0_ffn_w2,
           L0_ffn_sfc1, L0_ffn_sfc2, L0_ffn_sfc3):
    import numpy as np
    import concourse.bacc as bacc
    from concourse.bass_utils import run_bass_kernel_spmd

    def rows(a):
        a = np.asarray(a)
        return np.ascontiguousarray(a.reshape(-1, P, a.shape[1]).transpose(1, 0, 2).reshape(P, -1))

    w1 = np.asarray(L0_ffn_w1)
    w2 = np.asarray(L0_ffn_w2)
    gate = np.zeros((D, P), w1.dtype)
    gate[:, 0:E] = np.asarray(L0_ffn_gate_w).T
    freqs = np.float32(10000.0) ** (-np.arange(0, HD, 2, dtype=np.float32) / np.float32(HD))
    angles = np.arange(N, dtype=np.float32)[:, None] * freqs
    sin = np.repeat(np.sin(angles), 2, axis=1).astype(np.float32)
    sin[:, 0:HD // 2] *= -1
    inputs = {
        "x": np.asarray(L0_attn_x),
        "w_qkv": np.asarray(L0_attn_w_qkv),
        "w_out": rows(L0_attn_w_out),
        "b_out": np.asarray(L0_attn_b_out),
        "gate_t": rows(gate),
        "w1_t": np.ascontiguousarray(w1.reshape(E, HID, DC, P).transpose(3, 0, 2, 1).reshape(P, -1)),
        "w2_t": np.ascontiguousarray(w2.transpose(2, 0, 1).reshape(P, -1)),
        "s1_t": rows(np.asarray(L0_ffn_sfc1).T),
        "s2_t": rows(np.asarray(L0_ffn_sfc2).T),
        "s3_t": rows(np.asarray(L0_ffn_sfc3).T),
        "cos": np.repeat(np.cos(angles), 2, axis=1).astype(np.float32),
        "sin": sin,
        "ident_in": np.eye(P, dtype=np.float32),
        "iota": np.tile(np.arange(E, dtype=np.float32), (P, 1)),
    }
    nc = bacc.Bacc("TRN2", target_bir_lowering=False, num_devices=1)
    aps = {k: nc.dram_tensor("in_" + k, a.shape, mybir.dt.from_np(a.dtype), kind="ExternalInput").ap()
           for k, a in inputs.items()}
    out = nc.dram_tensor("out", (B, N, D), F32, kind="ExternalOutput").ap()
    transformer_layer(nc, **aps, out=out)
    results = run_bass_kernel_spmd(nc, [{"in_" + k: a for k, a in inputs.items()}], core_ids=[0])
    return results.results[0]["out"]
```

```python
import concourse.bass as bass
from concourse import mybir
from contextlib import ExitStack

B, N, D, H, HD = 8, 512, 256, 16, 16
P = 128
QT = N // P
DC = D // P
GH = 4
NG = H // GH
EPS = 1e-5

F32 = mybir.dt.float32
F32R = mybir.dt.float32r
ALU = mybir.AluOpType
ACT = mybir.ActivationFunctionType
AX = mybir.AxisListType


def later(count):
    return not isinstance(count, int) or count > 0


def attention(nc, ctx, x_in, w_qkv, cos_in, sin_in, ident_in, rows_in, X, O, ident, ident_r):
    def sb(name, shape, dt=F32):
        return ctx.enter_context(nc.sbuf_tensor(name, shape, dt))

    def ps(name):
        return ctx.enter_context(nc.psum_tensor(name, [P, 512], F32))

    def sem(name):
        return ctx.enter_context(nc.semaphore(name))

    w_raw = sb("w_raw", [P, DC, 3 * D])
    w_hi = sb("w_hi", [P, DC, 3 * D], F32R)
    w_lo = sb("w_lo", [P, DC, 3 * D], F32R)
    cos = sb("cos", [P, QT, HD])
    sin = sb("sin", [P, QT, HD])
    halves = sb("halves", [P, QT])
    zero = sb("zero", [P, D])
    stats = sb("stats", [P, QT, 6])
    meanvar = sb("meanvar", [P, QT, 2])
    vareps = sb("vareps", [P, QT])
    rstd = sb("rstd", [P, QT])
    xn = sb("xn", [P, QT, D])
    xt_hi = sb("xt_hi", [P, DC, N], F32R)
    xt_lo = sb("xt_lo", [P, DC, N], F32R)
    qk_raw = [sb(f"qk_raw{i}", [P, 2 * D]) for i in range(2)]
    rope_a = sb("rope_a", [P, 2 * D])
    rope_b = sb("rope_b", [P, 2 * D])
    qk = [sb(f"qk{i}", [P, QT, 2 * D]) for i in range(2)]
    v_aug = [sb(f"v_aug{i}", [P, QT, H, 2 * HD]) for i in range(2)]
    stage_q = [sb(f"stage_q{i}", [P, QT, P], F32R) for i in range(2)]
    stage_k = [sb(f"stage_k{i}", [P, QT, P], F32R) for i in range(2)]
    q_st = [[sb(f"q_st{g}{p}", [P, N], F32R) for p in range(2)] for g in range(2)]
    k_st = [[[sb(f"k_st{g}{p}{a}", [P, N], F32R) for a in range(2)] for p in range(2)] for g in range(2)]
    probs = [[sb(f"probs{h}{k}", [P, N]) for k in range(QT)] for h in range(2)]
    negmax = [sb(f"negmax{p}", [P, QT, 2]) for p in range(2)]
    nm = [sb(f"nm{p}", [P, QT, 2, 2]) for p in range(2)]
    mt = [sb(f"mt{p}", [4, N], F32R) for p in range(2)]
    o_t = sb("o_t", [P, N])
    rden = sb("rden", [P, QT * GH])

    score = [ps(f"score{i}") for i in range(2)]
    natural = [ps(f"natural{i}") for i in range(2)]
    av = ps("av")
    bank_t = ps("bank_t")
    bank_a = ps("bank_a")
    bank_o = ps("bank_o")

    held = [sem(f"held{i}") for i in range(2)]
    zero_done = sem("zero_done")
    filled = sem("filled")
    x_first = sem("x_first")
    x_rest = sem("x_rest")
    w_loaded = sem("w_loaded")
    tables = sem("tables")
    w_hi_done = sem("w_hi_done")
    w_split = sem("w_split")
    consts = sem("consts")
    ones_v = sem("ones_v")
    stats_done = sem("stats_done")
    aggr_done = sem("aggr_done")
    var_done = sem("var_done")
    rstd_done = sem("rstd_done")
    xn_done = sem("xn_done")
    xt_ps = sem("xt_ps")
    xth_done = sem("xth_done")
    xtl_done = sem("xtl_done")
    qk_ps = sem("qk_ps")
    qk_out = sem("qk_out")
    v_ps = sem("v_ps")
    v_done = sem("v_done")
    rope_part = sem("rope_part")
    qk_done = sem("qk_done")
    stage_hi = sem("stage_hi")
    staged = sem("staged")
    tr_ps = sem("tr_ps")
    q_done = sem("q_done")
    k_done = sem("k_done")
    nat_ps = sem("nat_ps")
    max_done = sem("max_done")
    nm_hi = sem("nm_hi")
    nm_done = sem("nm_done")
    mt_ps = sem("mt_ps")
    mt_done = sem("mt_done")
    m_in = [sem(f"m_in{p}") for p in range(2)]
    sc_ps = sem("sc_ps")
    exp_done = sem("exp_done")
    av_ps = sem("av_ps")
    ot_done = sem("ot_done")
    nt_ps = sem("nt_ps")
    rden_done = sem("rden_done")
    on_done = sem("on_done")

    x_v = x_in.rearrange("b (t p) d -> p (b t) d", p=P)
    w_v = w_qkv.rearrange("(c p) n -> p c n", p=P)

    A_SLOT = {(0, 1, 1): ("xt", 0), (0, 2, 0): ("xt", 1), (0, 2, 3): ("qk", 0), (0, 3, 1): ("v", 0),
              (0, 3, 3): ("qk", 1), (1, 0, 0): ("v", 1), (1, 0, 3): ("qk", 2), (1, 1, 1): ("v", 2),
              (1, 1, 3): ("qk", 3), (1, 2, 1): ("v", 3)}
    T_SLOT = {(0, 1): (1, 1, "q"), (0, 3): (1, 1, "k"), (2, 1): (2, 0, "q"), (2, 3): (2, 0, "k")}

    def pairs(engine, batch):
        for b in range(2):
            batch(b, b % 2, b > 0, True)
        with engine.Fori(1, B // 2 - 1) as two:
            for odd in range(2):
                batch(two * 2 + odd, odd, True, True)
        for b in range(B - 2, B):
            batch(b, b % 2, True, b < B - 1)

    def sync_engine(sp):
        sp.dma_start(X[:, 0:QT, :], x_v[:, 0:QT, :]).then_inc(x_first, 16)
        sp.dma_start(w_raw[:, :, :], w_v).then_inc(w_loaded, 16)
        sp.dma_start(ident[:, :], ident_in).then_inc(tables, 16)
        sp.dma_start(cos[:, :, :], cos_in.rearrange("(t p) d -> p t d", p=P)).then_inc(tables, 16)
        sp.dma_start(sin[:, :, :], sin_in.rearrange("(t p) d -> p t d", p=P)).then_inc(tables, 16)
        for b in range(1, B):
            sp.dma_start(X[:, b * QT:(b + 1) * QT, :], x_v[:, b * QT:(b + 1) * QT, :]).then_inc(x_rest, 16)

        sp.wait_ge(zero_done, 1)
        fill = rows_in.rearrange("(n s p) d -> n p s d", n=4, p=P)
        for n in range(4):
            sp.dma_start(fill[n], zero[:, :].unsqueeze(1).broadcast_to([P, fill.shape[2], D])).then_inc(filled, 16)

        def max_rows(G, gp, p):
            sp.wait_ge(mt_done, G * 2 + p + 1)
            for a in range(2):
                sp.dma_start(q_st[gp][p][64 * a + 48:64 * a + 50, :].bitcast(F32),
                             mt[p][2 * a:2 * a + 2, :].bitcast(F32)).then_inc(m_in[p], 16)

        max_rows(0, 0, 0)

        def batch(b, odd, has_prev, has_next):
            for g in range(NG):
                max_rows(b * NG + g, g % 2, 1)
                if has_next or g < NG - 1:
                    max_rows(b * NG + g + 1, (g + 1) % 2, 0)
        pairs(sp, batch)
        sp.wait_ge(filled, 64)

    def gpsimd_engine(pool):
        nc.gpsimd.memset(halves[:, :], -0.5)
        nc.gpsimd.memset(zero[:, :], 0.0).then_inc(zero_done, 1)
        for p in range(2):
            nc.gpsimd.memset(stage_q[p][:, :, :].bitcast(F32), 0.0)
            nc.gpsimd.memset(stage_k[p][:, :, :].bitcast(F32), 0.0)
        for i in range(2):
            last = nc.gpsimd.memset(v_aug[i][:, :, :, :], 1.0)
        last.then_inc(ones_v, 1)
        pool.wait_ge(ones_v, 1)
        for p in range(2):
            ones = stage_k[p][:, :, :].bitcast(F32).rearrange("p t (a r) -> p (t a) r", a=2)
            last = nc.gpsimd.memset(ones[:, :, 48:50], 1.0)
        last.then_inc(consts, 1)
        pool.wait_ge(consts, 2)

        def row_scale(b):
            pool.wait_ge(var_done, b + 1)
            if later(b):
                pool.wait_ge(xn_done, b * QT)
            nc.gpsimd.tensor_tensor(rstd[:, :], vareps[:, :], halves[:, :], ALU.pow).then_inc(rstd_done, 1)

        def rope(b, odd, t):
            n = b * QT + t
            heads = lambda a: a.rearrange("p (h d) -> p h d", d=HD)
            src = heads(qk_raw[t % 2][:, :])
            c = cos[:, t, :].unsqueeze(1).broadcast_to([P, 2 * H, HD])
            s_ = sin[:, t, :]
            pool.wait_ge(qk_out, n + 1)
            if later(n):
                pool.wait_ge(qk_done, n)
            nc.gpsimd.tensor_tensor(heads(rope_a[:, :]), src, c, ALU.mult).then_inc(rope_part, 1)
            nc.gpsimd.tensor_tensor(heads(rope_b[:, :])[:, :, 0:8], src[:, :, 1::2],
                                    s_[:, 0:8].unsqueeze(1).broadcast_to([P, 2 * H, 8]), ALU.mult).then_inc(rope_part, 1)
            nc.gpsimd.tensor_tensor(heads(rope_b[:, :])[:, :, 8:16], src[:, :, 0::2],
                                    s_[:, 8:16].unsqueeze(1).broadcast_to([P, 2 * H, 8]), ALU.mult).then_inc(rope_part, 1)
            pool.wait_ge(rope_part, n * 3 + 3)
            nc.gpsimd.tensor_tensor(qk[odd][:, t, :], rope_a[:, :], rope_b[:, :], ALU.add).then_inc(qk_done, 1)

        def stage(b, odd, g, p):
            G = b * NG + g
            if g == 0 and p == 0:
                pool.wait_ge(qk_done, b * QT + QT)
            for kind, buf, his, lo in (("q", stage_q[p], (0, 32), 16), ("k", stage_k[p], (0, 16), 32)):
                job = G * 4 + 2 * p + (kind == "k")
                c0 = (kind == "k") * D + (g * GH + 2 * p) * HD
                src = qk[odd][:, :, c0:c0 + 2 * HD].rearrange("p t (a j) -> p t a j", a=2)
                part = lambda off, dt: (buf[:, :, :] if dt == F32R else buf[:, :, :].bitcast(F32)).rearrange(
                    "p t (a r) -> p t a r", a=2)[:, :, :, off:off + HD]
                if later(job - 3):
                    pool.wait_ge(tr_ps, job - 3)
                pool.sem_inc(held[1], 1)
                nc.gpsimd.tensor_copy(part(his[0], F32R), src).then_inc(stage_hi, 1)
                nc.gpsimd.tensor_copy(part(his[1], F32R), src)
                pool.wait_ge(stage_hi, job + 1)
                nc.gpsimd.tensor_tensor(part(lo, F32R), src, part(his[0], F32), ALU.subtract).then_inc(staged, 1)

        pool.wait_ge(tables, 48)
        row_scale(0)
        for t in range(QT):
            rope(0, 0, t)
        for g in range(2):
            for p in range(2):
                stage(0, 0, g, p)

        def batch(b, odd, has_prev, has_next):
            if has_next:
                row_scale(b + 1)
            stage(b, odd, 2, 0)
            stage(b, odd, 2, 1)
            if has_next:
                rope(b + 1, 1 - odd, 0)
            stage(b, odd, 3, 0)
            if has_next:
                rope(b + 1, 1 - odd, 1)
            stage(b, odd, 3, 1)
            if has_next:
                rope(b + 1, 1 - odd, 2)
                rope(b + 1, 1 - odd, 3)
                for g in range(2):
                    for p in range(2):
                        stage(b + 1, 1 - odd, g, p)
        pairs(pool, batch)

    def scalar_engine(act):
        def evacuate_t(G, gp, p, kind):
            if kind == "q":
                act.wait_ge(tr_ps, G * 4 + 2 * p + 1)
                if later(G * 16 + 8 * p - 24):
                    act.wait_ge(sc_ps, G * 16 + 8 * p - 24)
                nc.scalar.copy(q_st[gp][p][:, :], bank_t[:, :]).then_inc(q_done, 1)
            else:
                act.wait_ge(tr_ps, G * 4 + 2 * p + 2)
                nc.scalar.copy(k_st[gp][p][0][0:64, :], bank_t[0:64, :])
                nc.scalar.copy(k_st[gp][p][1][64:128, :], bank_t[64:128, :]).then_inc(k_done, 1)

        def a_job(b, odd, what, n):
            if what == "xt":
                act.wait_ge(xt_ps, b * DC + n + 1)
                if later(b) and n == 0:
                    act.wait_ge(v_ps, b * QT)
                nc.scalar.copy(xt_hi[:, n, :], bank_a[:, :]).then_inc(xth_done, 1)
            if what == "qk":
                act.wait_ge(qk_ps, b * QT + n + 1)
                if later(b * QT + n - 1):
                    act.wait_ge(qk_done, b * QT + n - 1)
                nc.scalar.copy(qk_raw[n % 2][:, :], bank_a[:, :]).then_inc(qk_out, 1)
            if what == "v":
                act.wait_ge(v_ps, b * QT + n + 1)
                if later(b * H - H) and n == 0:
                    act.wait_ge(av_ps, b * H - H)
                nc.scalar.copy(v_aug[odd][:, n, :, 0:HD],
                               bank_a[:, 0:D].rearrange("p (h d) -> p h d", d=HD)).then_inc(v_done, 1)

        def max_job(G, p):
            act.wait_ge(mt_ps, G * 2 + p + 1)
            if later(G * 32):
                act.wait_ge(m_in[p], G * 32)
            nc.scalar.copy(mt[p][:, :], bank_o[0:4, :]).then_inc(mt_done, 1)

        def out_job(G):
            act.wait_ge(av_ps, G * GH + GH)
            if later(G):
                act.wait_ge(nt_ps, G)
            nc.scalar.copy(o_t[:, :], av[:, :]).then_inc(ot_done, 1)

        act.wait_ge(tables, 48)
        nc.scalar.copy(ident_r[:, :], ident[:, :]).then_inc(w_hi_done, 1)
        act.wait_ge(w_loaded, 16)
        nc.scalar.copy(w_hi[:, :, :], w_raw[:, :, :]).then_inc(w_hi_done, 1)
        act.wait_ge(consts, 2)
        for n in range(DC):
            a_job(0, 0, "xt", n)
        for t in range(QT):
            a_job(0, 0, "qk", t)
            a_job(0, 0, "v", t)
        for p in range(2):
            for kind in "qk":
                evacuate_t(0, 0, p, kind)
        max_job(0, 0)
        for kind in "qk":
            evacuate_t(1, 1, 0, kind)

        def batch(b, odd, has_prev, has_next):
            for g in range(NG):
                G = b * NG + g
                for i in range(GH):
                    head = b * H + g * GH + i
                    for kt in range(QT):
                        act.wait_ge(sc_ps, head * QT + kt + 1)
                        if kt == 0 and later(head - 1):
                            act.wait_ge(av_ps, head - 1)
                        nc.scalar.activation(probs[i % 2][kt][:, :], score[kt % 2][:, :], ACT.Exp,
                                             scale=HD ** -0.5).then_inc(exp_done, 1)
                        if (i, kt) in T_SLOT:
                            ahead, p, kind = T_SLOT[i, kt]
                            if has_next or g + ahead < NG:
                                evacuate_t(G + ahead, (g + ahead) % 2, p, kind)
                        if (g, i, kt) in A_SLOT and has_next:
                            a_job(b + 1, 1 - odd, *A_SLOT[g, i, kt])
                        if (i, kt) == (0, 2):
                            max_job(G, 1)
                        if (i, kt) == (1, 0) and (has_prev or g > 0):
                            out_job(G - 1)
                        if (i, kt) == (2, 2) and (has_next or g < NG - 1):
                            max_job(G + 1, 0)
        pairs(act, batch)
        out_job(B * NG - 1)

    def vector_engine(dve):
        def norm_stats(b):
            for t in range(QT):
                nc.vector.bn_stats(stats[:, t, :], X[:, bass.ds(b * QT + t, 1), :].rearrange("p a d -> p (a d)")).then_inc(stats_done, 1)
            dve.wait_ge(stats_done, b * QT + QT)
            dve.sem_inc(held[0], 1)
            for t in range(QT):
                nc.vector.bn_aggr(meanvar[:, t, :], stats[:, t, :]).then_inc(aggr_done, 1)
            dve.wait_ge(aggr_done, b * QT + QT)
            nc.vector.tensor_scalar_add(vareps[:, :], meanvar[:, :, 1], EPS).then_inc(var_done, 1)

        def norm_apply(b):
            dve.wait_ge(rstd_done, b + 1)
            if later(b):
                dve.wait_ge(xt_ps, b * DC)
            for t in range(QT):
                nc.vector.tensor_scalar(xn[:, t, :], X[:, bass.ds(b * QT + t, 1), :].rearrange("p a d -> p (a d)"),
                                        meanvar[:, t, 0:1], rstd[:, t:t + 1],
                                        ALU.subtract, ALU.mult).then_inc(xn_done, 1)

        def xt_low(b, c):
            dve.wait_ge(xth_done, b * DC + c + 1)
            nc.vector.tensor_tensor(xt_lo[:, c, :], bank_a[:, :], xt_hi[:, c, :].bitcast(F32),
                                    ALU.subtract).then_inc(xtl_done, 1)

        def row_max(G, i, t):
            n = G * 16 + i * QT + t
            dve.wait_ge(nat_ps, n + 1)
            if i % 2 == 0 and t == 0 and later(G):
                dve.wait_ge(nm_done, G * 2 + i // 2 - 1)
            nc.vector.tensor_reduce(negmax[i // 2][:, t, i % 2:i % 2 + 1], natural[t % 2][:, :], AX.X, ALU.max,
                                    negate=True).then_inc(max_done, 1)

        def max_split(G, p):
            dve.wait_ge(max_done, G * 16 + 8 * p + 8)
            if later(G):
                dve.wait_ge(mt_ps, G * 2 + p - 1)
            nc.vector.tensor_copy(nm[p][:, :, :, 0].bitcast(F32R), negmax[p][:, :, :]).then_inc(nm_hi, 1)
            dve.wait_ge(nm_hi, G * 2 + p + 1)
            nc.vector.tensor_tensor(nm[p][:, :, :, 1], negmax[p][:, :, :], nm[p][:, :, :, 0],
                                    ALU.subtract).then_inc(nm_done, 1)

        def normalise(b, g):
            G = b * NG + g
            dve.wait_ge(nt_ps, G + 1)
            view = bank_o[:, :].rearrange("p (t i) -> p t i", i=2 * HD)
            nc.vector.reciprocal(rden[:, :], view[:, :, HD]).then_inc(rden_done, 1)
            dve.wait_ge(rden_done, G + 1)
            nc.vector.tensor_tensor(
                O[:, bass.ds(b * QT, QT), g * GH * HD:(g + 1) * GH * HD].rearrange("p t (i j) -> p t i j", i=GH),
                view[:, :, 0:HD].rearrange("p (t i) j -> p t i j", t=QT),
                rden[:, :].rearrange("p (t i) -> p t i", t=QT).unsqueeze(3).broadcast_to([P, QT, GH, HD]),
                ALU.mult).then_inc(on_done, 1)

        for g in range(2):
            for p in range(2):
                nc.vector.memset(k_st[g][p][0][64:128, :].bitcast(F32), 0.0)
                last = nc.vector.memset(k_st[g][p][1][0:64, :].bitcast(F32), 0.0)
        last.then_inc(consts, 1)
        dve.wait_ge(x_first, 16)
        norm_stats(0)
        dve.wait_ge(w_hi_done, 2)
        nc.vector.tensor_tensor(w_lo[:, :, :], w_raw[:, :, :], w_hi[:, :, :].bitcast(F32),
                                ALU.subtract).then_inc(w_split, 1)
        norm_apply(0)
        for c in range(DC):
            xt_low(0, c)
        for i in range(GH):
            if i == 2:
                max_split(0, 0)
            for t in range(QT):
                row_max(0, i, t)
        dve.wait_ge(x_rest, 16 * (B - 1))

        def batch(b, odd, has_prev, has_next):
            for g in range(NG):
                G = b * NG + g
                ahead = has_next or g < NG - 1
                for i in range(GH):
                    for kt in range(QT):
                        if (i, kt) == (0, 0):
                            max_split(G, 1)
                        if (i, kt) == (2, 0) and ahead:
                            max_split(G + 1, 0)
                        if ahead:
                            row_max(G + 1, i, kt)
                        if g == 0 and has_next:
                            if (i, kt) == (0, 1):
                                norm_stats(b + 1)
                            if (i, kt) == (1, 0):
                                norm_apply(b + 1)
                        if A_SLOT.get((g, i, kt), ("", 0))[0] == "xt" and has_next:
                            xt_low(b + 1, A_SLOT[g, i, kt][1])
                        if (i, kt) == (1, 2) and g > 0:
                            normalise(b, g - 1)
                        if (i, kt) == (1, 2) and g == 0 and has_prev:
                            normalise(b - 1, NG - 1)
        pairs(dve, batch)
        normalise(B - 1, NG - 1)

    def tensor_engine(pe):
        def a_job(b, what, n):
            if what == "xt":
                pe.wait_ge(xn_done, b * QT + QT)
                if n == 0:
                    if later(b):
                        pe.wait_ge(v_done, b * QT)
                else:
                    pe.wait_ge(xtl_done, b * DC + n)
                for t in range(QT):
                    last = nc.tensor.transpose(bank_a[:, t * P:(t + 1) * P], xn[:, t, n * P:(n + 1) * P], ident[:, :])
                last.then_inc(xt_ps, 1)
                return
            if what == "qk":
                cols, out = slice(0, 2 * D), bank_a[:, :]
                if n == 0:
                    pe.wait_ge(xtl_done, b * DC + DC)
                else:
                    pe.wait_ge(v_done, b * QT + n)
            else:
                cols, out = slice(2 * D, 3 * D), bank_a[:, 0:D]
                pe.wait_ge(qk_out, b * QT + n + 1)
            terms = [(c, x, w) for c in range(DC) for x, w in ((xt_lo, w_hi), (xt_hi, w_lo), (xt_hi, w_hi))]
            for k, (c, x, w) in enumerate(terms):
                last = nc.tensor.matmul(out, x[:, c, n * P:(n + 1) * P], w[:, c, cols],
                                        start=k == 0, stop=k == len(terms) - 1)
            last.then_inc(qk_ps if what == "qk" else v_ps, 1)

        def t_job(G, p, kind):
            if kind == "q":
                pe.wait_ge(staged, G * 4 + 2 * p + 1)
                if later(G * 2 + p):
                    pe.wait_ge(k_done, G * 2 + p)
                src = stage_q[p]
            else:
                pe.wait_ge(staged, G * 4 + 2 * p + 2)
                pe.wait_ge(q_done, G * 2 + p + 1)
                src = stage_k[p]
            for t in range(QT):
                last = nc.tensor.matmul(bank_t[:, t * P:(t + 1) * P], src[:, t, :], ident_r[:, :], start=True, stop=True)
            last.then_inc(tr_ps, 1)

        def natural_scores(G, gp, i, t):
            p, a = i // 2, i % 2
            n = G * 16 + i * QT + t
            if a == 0 and t == 0:
                pe.wait_ge(k_done, G * 2 + p + 1)
            if later(n - 1):
                pe.wait_ge(max_done, n - 1)
            nc.tensor.matmul(natural[t % 2][:, :], q_st[gp][p][:, t * P:(t + 1) * P], k_st[gp][p][a][:, :],
                             start=True, stop=True).then_inc(nat_ps, 1)

        def m_job(G, p):
            pe.wait_ge(nm_done, G * 2 + p + 1)
            if later(G * 2 + p):
                pe.wait_ge(mt_done, G * 2 + p)
            if p == 0 and later(G - 1):
                pe.wait_ge(on_done, G - 1)
            for t in range(QT):
                last = nc.tensor.transpose(bank_o[0:4, t * P:(t + 1) * P],
                                           nm[p][:, t, :, :].rearrange("p i s -> p (i s)"), ident[:, :])
            last.then_inc(mt_ps, 1)

        def n_job(G, before_mt):
            pe.wait_ge(ot_done, G + 1)
            pe.wait_ge(mt_done, before_mt)
            for t in range(QT):
                last = nc.tensor.transpose(bank_o[:, t * P:(t + 1) * P], o_t[:, t * P:(t + 1) * P], ident[:, :])
            last.then_inc(nt_ps, 1)

        def attend(b, odd, hl, kt):
            head = b * H + hl
            i = hl % GH
            pe.wait_ge(exp_done, head * QT + kt + 1)
            if i == 0 and kt == 0 and later(b * NG + hl // GH):
                pe.wait_ge(ot_done, b * NG + hl // GH)
            if hl == 0 and kt == 0:
                pe.wait_ge(v_done, b * QT + QT)
            last = nc.tensor.matmul(av[32 * i:32 * i + 32, :], v_aug[odd][:, kt, hl, :], probs[hl % 2][kt][:, :],
                                    start=kt == 0, stop=kt == QT - 1)
            if kt == QT - 1:
                last.then_inc(av_ps, 1)

        pe.wait_ge(w_hi_done, 2)
        pe.wait_ge(consts, 2)
        for n in range(DC):
            a_job(0, "xt", n)
        pe.wait_ge(w_split, 1)
        for t in range(QT):
            a_job(0, "qk", t)
            a_job(0, "v", t)
        for p in range(2):
            for kind in "qk":
                t_job(0, p, kind)
        for i in range(GH):
            for t in range(QT):
                natural_scores(0, 0, i, t)
            if i == 2:
                m_job(0, 0)
        for kind in "qk":
            t_job(1, 0, kind)

        def batch(b, odd, has_prev, has_next):
            for g in range(NG):
                G = b * NG + g
                gp = g % 2
                for i in range(GH):
                    p, a = i // 2, i % 2
                    hl = g * GH + i
                    for kt in range(QT):
                        n = (b * H + hl) * QT + kt
                        if kt == 0 and a == 0:
                            pe.wait_ge(m_in[p], (G + 1) * 32)
                        if later(n - 1):
                            pe.wait_ge(exp_done, n - 1)
                        nc.tensor.matmul(score[kt % 2][:, :], k_st[gp][p][a][:, kt * P:(kt + 1) * P],
                                         q_st[gp][p][:, :], start=True, stop=True).then_inc(sc_ps, 1)
                        if has_next or g < NG - 1:
                            natural_scores(G + 1, 1 - gp, i, kt)
                        if hl > 0:
                            attend(b, odd, hl - 1, kt)
                        elif has_prev:
                            attend(b - 1, 1 - odd, H - 1, kt)
                        if (i, kt) in T_SLOT:
                            ahead, tp, kind = T_SLOT[i, kt]
                            if has_next or g + ahead < NG:
                                t_job(G + ahead, tp, kind)
                        if (g, i, kt) in A_SLOT and has_next:
                            a_job(b + 1, *A_SLOT[g, i, kt])
                        if (i, kt) == (0, 2):
                            m_job(G, 1)
                        if (i, kt) == (1, 1) and (has_prev or g > 0):
                            n_job(G - 1, G * 2 + 2)
                        if (i, kt) == (2, 2) and (has_next or g < NG - 1):
                            m_job(G + 1, 0)
        pairs(pe, batch)
        for kt in range(QT):
            attend(B - 1, (B - 1) % 2, H - 1, kt)
        pe.wait_ge(on_done, B * NG - 1)
        n_job(B * NG - 1, B * NG * 2)

    return sync_engine, gpsimd_engine, scalar_engine, vector_engine, tensor_engine


NT = B * QT
E, HID = 16, 128
S = 512
SC = S // P
U32 = mybir.dt.uint32
TILES = 2 * NT + E


class Chain:

    def __init__(self, engine, semaphore, per):
        self.engine, self.semaphore, self.per, self.round, self.n = engine, semaphore, per, 0, 0

    def start(self, round_):
        self.round, self.n = round_, 0

    def step(self, instruction):
        self.n += 1
        instruction.then_inc(self.semaphore, 1)
        self.engine.wait_ge(self.semaphore, self.round * self.per + self.n)


def for_rows(engine, row):
    row(0)
    with engine.Fori(1, B) as b:
        row(b)


def run_block(nc, sync=None, gpsimd=None, scalar=None, vector=None, tensor=None):
    with nc.Block() as block:
        if sync:
            block.sync(sync)
        if gpsimd:
            block.gpsimd(gpsimd)
        if scalar:
            block.scalar(scalar)
        if vector:
            block.vector(vector)
        if tensor:
            block.tensor(tensor)


def tiles_of(T, b, n=QT):
    return T[:, bass.ds(b * QT, n), :]


def feed_forward(nc, ctx, w_out, b_out, gate_t, experts_t, iota_in, upper_in, steps_in, rows128_in, rows_in, rows_out, out, X, O, ident):
    def sb(name, shape, dt=F32):
        return ctx.enter_context(nc.sbuf_tensor(name, shape, dt))

    def sem(name):
        return ctx.enter_context(nc.semaphore(name))

    W1, W2 = 0, E * DC * HID
    S1 = W2 + E * D
    S2, S3 = S1 + DC * S, S1 + 2 * DC * S
    ALL = S3 + SC * D
    CHUNK = ALL // B
    w_hi = sb("weights_hi", [P, ALL], F32R)
    w_lo = sb("weights_lo", [P, ALL], F32R)
    iota = sb("iota", [P, E])
    rows128 = sb("rows128", [P, NT])
    halves = sb("halves32", [P, QT])
    ids = sb("ids", [P, NT, 2])
    wts = sb("wts", [P, NT, 2])
    owner_i = sb("owner_i", [1, 4 + TILES], mybir.dt.int32)
    slots_i = sb("slots_i", [P, NT, 2], U32)

    def three(out_ap, pieces, first=True, last=True):
        k = 0
        for st, mv in pieces:
            for a, b in ((st[1], mv[0]), (st[0], mv[1]), (st[0], mv[0])):
                ins = nc.tensor.matmul(out_ap, a, b, start=first and k == 0, stop=last and k == 3 * len(pieces) - 1)
                k += 1
        return ins

    def three_acc(out_ap, st, mv, start, stop):
        for k, (a, b) in enumerate(((st[1], mv[0]), (st[0], mv[1]), (st[0], mv[0]))):
            ins = nc.tensor.matmul(out_ap, a, b, start=start and k == 0, stop=stop and k == 2, skip_group_check=True)
        return ins

    def weight(c0, n):
        return w_hi[:, c0:c0 + n], w_lo[:, c0:c0 + n]

    def one(T, n):
        return T[:, bass.ds(n, 1), :].rearrange("p a d -> p (a d)")

    def in_row(b):
        return not isinstance(b, int) or 0 <= b < B

    def row_steps(engine, step):
        for s in range(4):
            step(s)
        with engine.Fori(4, B - 1) as s:
            step(s)
        for s in range(B - 1, B + 3):
            step(s)

    with ExitStack() as sub:
        psem = lambda name: sub.enter_context(nc.semaphore("p_" + name))
        sbt = lambda name, shape, dt=F32: sub.enter_context(nc.sbuf_tensor("p_" + name, shape, dt))
        bank = lambda name, shape: sub.enter_context(nc.psum_tensor("p_" + name, shape, F32))
        small_in, small_hi, small_lo, raw_in, raw_hi, raw_lo = (psem(x) for x in "small_in small_hi small_lo raw_in raw_hi raw_lo".split())
        flat_s, ta_s, ha_s, la_s, proj_s, bn1_s, ag1_s, var1_s, pow1_s, nmr1_s = (
            psem(x) for x in "flat ta ha la proj bn1 ag1 var1 pow1 nmr1".split())
        z_s, x1_s, bn2_s, ag2_s, var2_s, pow2_s, nmr2_s = (psem(x) for x in "z x1 bn2 ag2 var2 pow2 nmr2".split())
        x2_s, tc_s, keep_s, hc_s, lc_s, gate_s, lt_s, lg_s, chain_s, gap_s, ratio_s, route_s = (
            psem(x) for x in "x2 tc keep hc lc gate lt lg chain gap ratio route".split())
        halves_s = psem("halves")
        held = [psem(f"held{i}") for i in range(2)]
        small_raw = sbt("small_raw", [P, DC * D + DC * P + D])
        small_h = sbt("small_h", [P, DC * D + DC * P + D], F32R)
        small_l = sbt("small_l", [P, DC * D + DC * P + D], F32R)
        raw = sbt("raw", [P, CHUNK])
        first_row = sbt("first_row", [P, P], F32R)
        heads = sbt("heads", [P, QT, D])
        x2 = sbt("x2", [P, QT, D])
        ta_hi, ta_lo, tc_hi, tc_lo = (sbt(x, [P, DC, N], F32R) for x in ("ta_hi", "ta_lo", "tc_hi", "tc_lo"))
        stats = [sbt(f"stats{i}", [P, QT, 6]) for i in range(2)]
        meanvar = [sbt(f"meanvar{i}", [P, QT, 2]) for i in range(2)]
        vareps = [sbt(f"vareps{i}", [P, QT]) for i in range(2)]
        rstd = [sbt(f"rstd{i}", [P, QT]) for i in range(2)]
        nmr = [sbt(f"nmr{i}", [P, QT]) for i in range(2)]
        lt = sbt("lt", [E, N])
        logits = sbt("logits", [P, QT, E])
        top = sbt("top", [P, QT, 8])
        topi = sbt("topi", [P, QT, 8], U32)
        ratio = sbt("ratio", [P, QT])
        den = sbt("den", [P, QT])
        gap = sbt("gap", [P, QT])
        bank_a = [bank(f"a{c}", [P, N]) for c in range(DC)]
        bank_y = [bank(f"y{c}", [P, 2, D]) for c in range(2)]
        bank_c = [bank(f"c{c}", [P, N]) for c in range(DC)]
        bank_g = bank("g", [P, N])
        bank_l = bank("l", [P, QT, E])
        small = lambda c0, n: (small_h[:, c0:c0 + n], small_l[:, c0:c0 + n])
        GW, BIAS = DC * D, DC * D + DC * P

        def sync(sp):
            sp.dma_start(small_raw[:, 0:GW], w_out).then_inc(small_in, 16)
            sp.dma_start(small_raw[:, GW:BIAS], gate_t).then_inc(small_in, 16)
            sp.dma_start(small_raw[:, BIAS:], b_out[None, :].broadcast_to([P, D])).then_inc(small_in, 16)
            sp.dma_start(iota[:, :], iota_in).then_inc(small_in, 16)
            sp.dma_start(rows128[:, :], rows128_in).then_inc(small_in, 16)

            def step(s):
                if in_row(s):
                    if later(s):
                        sp.wait_ge(raw_lo, s)
                    sp.dma_start(raw[:, :], experts_t[:, bass.ds(s * CHUNK, CHUNK)]).then_inc(raw_in, 16)
            row_steps(sp, step)

        def gpsimd(pool):
            nc.gpsimd.memset(halves[:, :], -0.5).then_inc(halves_s, 1)
            pool.wait_ge(halves_s, 1)

            def step(s):
                if in_row(s - 1):
                    pool.wait_ge(var2_s, s)
                    if later(s - 1):
                        pool.wait_ge(nmr2_s, s - 1)
                        pool.wait_ge(x2_s, (s - 1) * QT)
                    nc.gpsimd.tensor_tensor(rstd[1][:, :], vareps[1][:, :], halves[:, :], ALU.pow).then_inc(pow2_s, 1)
                if in_row(s):
                    pool.wait_ge(var1_s, s + 1)
                    if later(s):
                        pool.wait_ge(z_s, s * QT)
                    nc.gpsimd.tensor_tensor(rstd[0][:, :], vareps[0][:, :], halves[:, :], ALU.pow).then_inc(pow1_s, 1)
                if in_row(s - 2):
                    pool.wait_ge(x2_s, (s - 1) * QT)
                    nc.gpsimd.tensor_copy(tiles_of(O, s - 2), x2[:, :, :]).then_inc(keep_s, 1)
                if in_row(s):
                    pool.wait_ge(raw_hi, s + 1)
                    nc.gpsimd.tensor_tensor(w_lo[:, bass.ds(s * CHUNK, CHUNK)], raw[:, :],
                                            w_hi[:, bass.ds(s * CHUNK, CHUNK)].bitcast(F32), ALU.subtract).then_inc(raw_lo, 1)
            row_steps(pool, step)

        def scalar(act):
            def copy_heads(b):
                if later(b):
                    act.wait_ge(ta_s, b * DC)
                nc.scalar.copy(heads[:, :, :], tiles_of(O, b)).then_inc(flat_s, 1)

            def step(s):
                if in_row(s):
                    for c in range(DC):
                        act.wait_ge(ta_s, s * DC + c + 1)
                        if later(s):
                            act.wait_ge(proj_s, s * 2)
                        nc.scalar.copy(ta_hi[:, c, :], bank_a[c][:, :]).then_inc(ha_s, 1)
                b = s - 1
                if in_row(b):
                    act.wait_ge(nmr1_s, b + 1)
                    for t in range(QT):
                        nc.scalar.activation(one(O, b * QT + t), bank_y[t // 2][:, t % 2, :], ACT.Identity,
                                             bias=nmr[0][:, t:t + 1], scale=rstd[0][:, t:t + 1]).then_inc(z_s, 1)
                if in_row(s + 1):
                    copy_heads(s + 1)
                b = s - 2
                if in_row(b):
                    act.wait_ge(nmr2_s, b + 1)
                    if later(b):
                        act.wait_ge(tc_s, b * DC)
                        act.wait_ge(keep_s, b)
                    for t in range(QT):
                        nc.scalar.activation(x2[:, t, :], one(X, b * QT + t), ACT.Identity,
                                             bias=nmr[1][:, t:t + 1], scale=rstd[1][:, t:t + 1]).then_inc(x2_s, 1)
                if in_row(s):
                    act.wait_ge(raw_in, (s + 1) * 16)
                    nc.scalar.copy(w_hi[:, bass.ds(s * CHUNK, CHUNK)], raw[:, :]).then_inc(raw_hi, 1)
                if in_row(b):
                    for c in range(DC):
                        act.wait_ge(tc_s, b * DC + c + 1)
                        if later(b):
                            act.wait_ge(gate_s, b)
                        nc.scalar.copy(tc_hi[:, c, :], bank_c[c][:, :]).then_inc(hc_s, 1)
                if in_row(s - 3):
                    act.wait_ge(gap_s, s - 2)
                    nc.scalar.activation(ratio[:, :], gap[:, :], ACT.Exp).then_inc(ratio_s, 1)
                if in_row(b):
                    act.wait_ge(gate_s, b + 1)
                    if later(b):
                        act.wait_ge(lg_s, b)
                    nc.scalar.copy(lt[:, :], bank_g[0:E, :]).then_inc(lt_s, 1)
            act.wait_ge(small_in, 80)
            nc.scalar.copy(small_h[:, :], small_raw[:, :]).then_inc(small_hi, 1)
            copy_heads(0)
            row_steps(act, step)

        def vector(dve):
            chain = Chain(dve, chain_s, 5)

            def statistics(i, b, source, bn_s, ag_s, var_s):
                dve.sem_inc(held[0], 1)
                for t in range(QT):
                    nc.vector.bn_stats(stats[i][:, t, :], source(t)).then_inc(bn_s, 1)
                dve.wait_ge(bn_s, b * QT + QT)
                dve.sem_inc(held[0], 1)
                for t in range(QT):
                    last = nc.vector.bn_aggr(meanvar[i][:, t, :], stats[i][:, t, :])
                last.then_inc(ag_s, 1)
                dve.wait_ge(ag_s, b + 1)
                nc.vector.tensor_scalar_add(vareps[i][:, :], meanvar[i][:, :, 1], EPS).then_inc(var_s, 1)

            def scale_of_mean(i):
                return nc.vector.scalar_tensor_tensor(nmr[i][:, :], meanvar[i][:, :, 0], -1.0, rstd[i][:, :], ALU.mult, ALU.mult)

            def step(s):
                if in_row(s):
                    for c in range(DC):
                        dve.wait_ge(ha_s, s * DC + c + 1)
                        nc.vector.tensor_tensor(ta_lo[:, c, :], bank_a[c][:, :], ta_hi[:, c, :].bitcast(F32), ALU.subtract).then_inc(la_s, 1)
                e = s - 3
                if in_row(e):
                    chain.start(e)
                    dve.wait_ge(lg_s, e + 1)
                    chain.step(nc.vector.tensor_copy(logits[:, :, :], bank_l[:, :, :]))
                    dve.sem_inc(held[0], 1)
                    for t in range(QT):
                        last = nc.vector.max(top[:, t, :], logits[:, t, :])
                    chain.step(last)
                    nc.vector.tensor_tensor(gap[:, :], top[:, :, 1], top[:, :, 0], ALU.subtract).then_inc(gap_s, 1)
                    for t in range(QT):
                        last = nc.vector.max_index(topi[:, t, :], top[:, t, :], logits[:, t, :])
                    chain.step(last)
                    nc.vector.tensor_copy(ids[:, bass.ds(e * QT, QT), :], topi[:, :, 0:2])
                b = s - 1
                if in_row(b):
                    dve.wait_ge(z_s, b * QT + QT)
                    nc.vector.tensor_tensor(tiles_of(X, b), tiles_of(X, b), tiles_of(O, b), ALU.add).then_inc(x1_s, 1)
                    dve.wait_ge(x1_s, b + 1)
                    statistics(1, b, lambda t: one(X, b * QT + t), bn2_s, ag2_s, var2_s)
                if in_row(s):
                    dve.wait_ge(proj_s, s * 2 + 2)
                    statistics(0, s, lambda t: bank_y[t // 2][:, t % 2, :], bn1_s, ag1_s, var1_s)
                b = s - 2
                if in_row(b):
                    for c in range(DC):
                        dve.wait_ge(hc_s, b * DC + c + 1)
                        nc.vector.tensor_tensor(tc_lo[:, c, :], bank_c[c][:, :], tc_hi[:, c, :].bitcast(F32), ALU.subtract).then_inc(lc_s, 1)
                if in_row(s - 1):
                    dve.wait_ge(pow2_s, s)
                    if later(s - 1):
                        dve.wait_ge(x2_s, (s - 1) * QT)
                    scale_of_mean(1).then_inc(nmr2_s, 1)
                if in_row(s):
                    dve.wait_ge(pow1_s, s + 1)
                    if later(s):
                        dve.wait_ge(z_s, s * QT)
                    scale_of_mean(0).then_inc(nmr1_s, 1)
                if in_row(e):
                    dve.wait_ge(ratio_s, e + 1)
                    chain.step(nc.vector.tensor_scalar_add(den[:, :], ratio[:, :], 1.0))
                    chain.step(nc.vector.reciprocal(wts[:, bass.ds(e * QT, QT), 0], den[:, :]))
                    nc.vector.tensor_tensor(wts[:, bass.ds(e * QT, QT), 1], ratio[:, :], wts[:, bass.ds(e * QT, QT), 0], ALU.mult).then_inc(route_s, 1)

            nc.vector.memset(first_row[:, :].bitcast(F32), 0.0).then_inc(small_lo, 1)
            dve.wait_ge(small_lo, 1)
            nc.vector.memset(first_row[0:1, :].bitcast(F32), 1.0)
            dve.wait_ge(small_hi, 1)
            nc.vector.tensor_tensor(small_l[:, :], small_raw[:, :], small_h[:, :].bitcast(F32), ALU.subtract).then_inc(small_lo, 1)
            row_steps(dve, step)

        def tensor(pe):
            def transposes(banks, src, sem):
                for c in range(DC):
                    for t in range(QT):
                        last = nc.tensor.transpose(banks[c][:, t * P:(t + 1) * P], src[:, t, c * P:(c + 1) * P], ident[:, :])
                    last.then_inc(sem, 1)

            def transpose_heads(b):
                pe.wait_ge(flat_s, b + 1)
                if later(b):
                    pe.wait_ge(la_s, b * DC)
                transposes(bank_a, heads, ta_s)

            def step(s):
                if in_row(s - 3):
                    pe.wait_ge(lt_s, s - 2)
                    if later(s - 3):
                        pe.wait_ge(route_s, s - 3)
                    pe.sem_inc(held[1], 1)
                    for t in range(QT):
                        last = nc.tensor.transpose(bank_l[:, t, :], lt[:, t * P:(t + 1) * P], ident[0:E, 0:E])
                    last.then_inc(lg_s, 1)
                if in_row(s):
                    pe.wait_ge(la_s, s * DC + DC)
                    if later(s):
                        pe.wait_ge(z_s, s * QT)
                    for k in range(2):
                        for t in (2 * k, 2 * k + 1):
                            cols = slice(t * P, (t + 1) * P)
                            for bias_part in (small_l, small_h):
                                nc.tensor.matmul(bank_y[k][:, t % 2, :], first_row[:, :], bias_part[:, BIAS:BIAS + D],
                                                 start=t % 2 == 0 and bias_part is small_l, stop=False, skip_group_check=True)
                            for c in range(DC):
                                last = three_acc(bank_y[k][:, t % 2, :], (ta_hi[:, c, cols], ta_lo[:, c, cols]), small(c * D, D),
                                                 False, t % 2 == 1 and c == DC - 1)
                        last.then_inc(proj_s, 1)
                if in_row(s + 1):
                    transpose_heads(s + 1)
                b = s - 2
                if in_row(b):
                    pe.wait_ge(x2_s, b * QT + QT)
                    if later(b):
                        pe.wait_ge(lc_s, b * DC)
                    transposes(bank_c, x2, tc_s)
                    pe.wait_ge(lc_s, b * DC + DC)
                    if later(b):
                        pe.wait_ge(lt_s, b)
                    three(bank_g[:, :], [(small(GW + c * P, P), (tc_hi[:, c, :], tc_lo[:, c, :])) for c in range(DC)]).then_inc(gate_s, 1)
            transpose_heads(0)
            pe.wait_ge(small_lo, 2)
            row_steps(pe, step)
        run_block(nc, sync=sync, gpsimd=gpsimd, scalar=scalar, vector=vector, tensor=tensor)

    with ExitStack() as sub:
        psem = lambda name: sub.enter_context(nc.semaphore(name))
        sbt = lambda name, shape, dt=F32: sub.enter_context(nc.sbuf_tensor(name, shape, dt))
        in_s, hot_s, const_s, pe_s, chain_s, place_s, moved_s, row_s = (psem("s_" + x) for x in "in hot const pe chain place moved row".split())
        hot = [sbt(f"hot{k}", [P, NT, E]) for k in range(2)]
        both = sbt("both", [P, NT, E], F32R)
        upper = sbt("upper", [P, P])
        upper_r = sbt("upper_r", [P, P], F32R)
        ones_r = sbt("ones_r", [P, P], F32R)
        run = [sbt(f"run{i}", [P, NT, E]) for i in range(2)]
        count = sbt("count", [P, E])
        needed = sbt("needed", [P, E])
        end = [sbt(f"end{i}", [P, E]) for i in range(2)]
        base = sbt("base", [P, E])
        passed_wide = sbt("passed_wide", [P, E, NT])
        place = sbt("place", [P, NT, E])
        chosen = [sbt(f"chosen{k}", [P, NT, E]) for k in range(2)]
        slots = sbt("slots", [P, NT, 2])
        steps = sbt("steps", [1, TILES])
        passed = sbt("passed", [1, TILES, E])
        owner = sbt("owner", [1, TILES])
        (flat_s, tr_s, hi_s, lo_s, a_s, g_s, silu_s, h_s, hh_s, hl_s, y_s, out_s) = (
            psem("s_" + x) for x in "flat tr hi lo a g silu h hh hl y out".split())
        flat = sbt("flat", [P, QT, D])
        t_hi, t_lo = (sbt(x, [P, DC, N], F32R) for x in ("t_hi", "t_lo"))
        silu = [sbt(f"silu{i}", [P, N]) for i in range(2)]
        h_hi = [sbt(f"h_hi{i}", [P, N], F32R) for i in range(2)]
        h_lo = [sbt(f"h_lo{i}", [P, N], F32R) for i in range(2)]
        bank_t, bank_a, bank_g, bank_y = ([sub.enter_context(nc.psum_tensor(f"s_b{x}{c}", [P, N], F32)) for c in range(2)] for x in "tagy")
        bank_all, bank_in = (bank_y[i][:, :].rearrange("p (t e) -> p t e", e=E) for i in range(2))

        def sync(sp):
            sp.dma_start(upper[:, :], upper_in).then_inc(in_s, 16)
            sp.dma_start(steps[:, :], steps_in[0:1, :]).then_inc(in_s, 16)
            sp.wait_ge(in_s, 32)

        def scalar(act):
            def copy_row(b):
                if later(b):
                    act.wait_ge(tr_s, b * DC)
                nc.scalar.copy(flat[:, :, :], tiles_of(O, b)).then_inc(flat_s, 1)

            def high(b):
                for c in range(DC):
                    act.wait_ge(tr_s, b * DC + c + 1)
                    if later(b):
                        act.wait_ge(g_s, b * SC)
                    nc.scalar.copy(t_hi[:, c, :], bank_t[c][:, :]).then_inc(hi_s, 1)

            def keep(b):
                act.wait_ge(y_s, b * SC + SC)
                act.wait_ge(moved_s, b + 1)
                for k in range(2):
                    nc.scalar.copy(O[:, bass.ds(b * QT + 2 * k, 2), :].rearrange("p t d -> p (t d)"), bank_y[k][:, :]).then_inc(out_s, 1)

            def row(b):
                high(b)
                if not isinstance(b, int) or b + 1 < B:
                    copy_row(b + 1)
                for n in range(SC):
                    m = b * SC + n
                    act.wait_ge(a_s, m + 1)
                    if later(m - 1):
                        act.wait_ge(hl_s, m - 1)
                    nc.scalar.activation(silu[n % 2][:, :], bank_a[n % 2][:, :], ACT.Silu).then_inc(silu_s, 1)
                    act.wait_ge(h_s, m + 1)
                    if later(m - 1):
                        act.wait_ge(y_s, m - 1)
                    nc.scalar.copy(h_hi[n % 2][:, :], silu[n % 2][:, :]).then_inc(hh_s, 1)
                    if n == 0 and later(b):
                        keep(b - 1)

            act.wait_ge(in_s, 32)
            nc.scalar.copy(upper_r[:, :], upper[:, :]).then_inc(const_s, 1)
            nc.scalar.activation(ones_r[:, :], upper[:, :], ACT.Copy, scale=0.0, bias=1.0).then_inc(const_s, 1)
            copy_row(0)
            row(0)
            with act.Fori(1, B - 1) as b:
                row(b)
            row(B - 1)
            keep(B - 1)

        def tensor(pe):
            def transposes(b):
                pe.wait_ge(flat_s, b + 1)
                for c in range(DC):
                    if later(b):
                        pe.wait_ge(lo_s, b * DC)
                    for t in range(QT):
                        last = nc.tensor.transpose(bank_t[c][:, t * P:(t + 1) * P], flat[:, t, c * P:(c + 1) * P], ident[:, :])
                    last.then_inc(tr_s, 1)

            def first(b, n):
                m = b * SC + n
                if later(m - 1):
                    pe.wait_ge(silu_s, m - 1)
                for base, banks, w_sem, done in ((S1, bank_a, None, a_s), (S2, bank_g, h_s, g_s)):
                    if w_sem and later(m - 1):
                        pe.wait_ge(w_sem, m - 1)
                    three(banks[n % 2][:, :], [(weight(base + c * S + n * P, P), (t_hi[:, c, :], t_lo[:, c, :])) for c in range(DC)]).then_inc(done, 1)

            def second(b, n):
                m = b * SC + n
                pe.wait_ge(hl_s, m + 1)
                if n == 0:
                    if later(b):
                        pe.wait_ge(out_s, b * 2)
                    else:
                        pe.wait_ge(place_s, 1)
                for t in range(QT):
                    lhs = (h_hi[n % 2][:, t * P:(t + 1) * P], h_lo[n % 2][:, t * P:(t + 1) * P])
                    last = three_acc(bank_y[t // 2][:, (t % 2) * D:(t % 2 + 1) * D], lhs, weight(S3 + n * D, D),
                                     n == 0 and t % 2 == 0, n == SC - 1)
                last.then_inc(y_s, 1)

            def row(b, has_next):
                pe.wait_ge(lo_s, b * DC + DC)
                first(b, 0)
                for n in range(1, SC):
                    first(b, n)
                    if n == SC - 1 and has_next:
                        transposes(b + 1)
                    second(b, n - 1)
                second(b, SC - 1)

            transposes(0)
            pe.wait_ge(const_s, 2)
            pe.wait_ge(hot_s, 1)
            m = both[:, :, :].rearrange("p t e -> p (t e)")
            nc.tensor.matmul(bank_y[0][:, :], ones_r[:, :], m, start=True, stop=True).then_inc(pe_s, 1)
            nc.tensor.matmul(bank_y[1][:, :], upper_r[:, :], m, start=True, stop=True).then_inc(pe_s, 1)
            row(0, True)
            with pe.Fori(1, B - 1) as b:
                row(b, True)
            row(B - 1, False)

        def vector(dve):
            chain = Chain(dve, chain_s, 0)
            chain.start(0)
            experts = iota[:, :].unsqueeze(1).broadcast_to([P, NT, E])
            for k in range(2):
                chain.step(nc.vector.tensor_tensor(hot[k][:, :, :], experts, ids[:, :, k:k + 1].broadcast_to([P, NT, E]), ALU.is_equal))
            nc.vector.tensor_tensor(both[:, :, :], hot[0][:, :, :], hot[1][:, :, :], ALU.add).then_inc(hot_s, 1)
            dve.wait_ge(pe_s, 1)
            chain.step(nc.vector.tensor_copy(run[0][:, :, :], bank_all))
            src = 0
            for shift in (1, 2, 4, 8, 16):
                nc.vector.tensor_copy(run[1 - src][:, 0:shift, :], run[src][:, 0:shift, :])
                chain.step(nc.vector.tensor_tensor(run[1 - src][:, shift:NT, :], run[src][:, shift:NT, :], run[src][:, 0:NT - shift, :], ALU.add))
                src = 1 - src
            total = run[src][:, NT - 1, :]
            wide = passed_wide[:, :, :]
            chain.step(nc.vector.tensor_tensor(wide, total.unsqueeze(2).broadcast_to([P, E, NT]), rows128[:, :].unsqueeze(1).broadcast_to([P, E, NT]), ALU.is_gt))
            chain.step(nc.vector.tensor_reduce(end[0][:, :], wide, AX.X, ALU.add))
            chain.step(nc.vector.tensor_copy(needed[:, :], end[0][:, :]))
            es = 0
            for shift in (1, 2, 4, 8):
                nc.vector.tensor_copy(end[1 - es][:, 0:shift], end[es][:, 0:shift])
                chain.step(nc.vector.tensor_tensor(end[1 - es][:, shift:E], end[es][:, shift:E], end[es][:, 0:E - shift], ALU.add))
                es = 1 - es
            nc.vector.tensor_tensor(passed[:, :, :], steps[:, :].unsqueeze(2).broadcast_to([1, TILES, E]), end[es][0:1, :].unsqueeze(1).broadcast_to([1, TILES, E]), ALU.is_ge).then_inc(hot_s, 1)
            dve.wait_ge(hot_s, 2)
            chain.step(nc.vector.tensor_reduce(owner[:, :], passed[:, :, :], AX.X, ALU.add))
            chain.step(nc.vector.tensor_scalar(owner[:, :], owner[:, :], float(E - 1), float(D), ALU.min, ALU.mult))
            chain.step(nc.vector.tensor_copy(owner_i[:, 4:], owner[:, :]))
            chain.step(nc.vector.tensor_tensor(base[:, :], end[es][:, :], needed[:, :], ALU.subtract))
            chain.step(nc.vector.tensor_scalar_mul(base[:, :], base[:, :], float(P)))
            dve.wait_ge(pe_s, 2)
            chain.step(nc.vector.tensor_tensor(place[:, :, :], bank_in, base[:, :].unsqueeze(1).broadcast_to([P, NT, E]), ALU.add))
            chain.step(nc.vector.tensor_tensor(place[:, 1:NT, :], place[:, 1:NT, :], run[src][:, 0:NT - 1, :], ALU.add))
            for k in range(2):
                chain.step(nc.vector.tensor_tensor(chosen[k][:, :, :], hot[k][:, :, :], place[:, :, :], ALU.mult))
            for k in range(2):
                chain.step(nc.vector.tensor_reduce(slots[:, :, k], chosen[k][:, :, :], AX.X, ALU.add))
            nc.vector.tensor_copy(slots_i[:, :, :], slots[:, :, :]).then_inc(place_s, 1)

            def low(b):
                for c in range(DC):
                    dve.wait_ge(hi_s, b * DC + c + 1)
                    nc.vector.tensor_tensor(t_lo[:, c, :], bank_t[c][:, :], t_hi[:, c, :].bitcast(F32), ALU.subtract).then_inc(lo_s, 1)

            def row(b):
                low(b)
                for n in range(SC):
                    m = b * SC + n
                    dve.wait_ge(silu_s, m + 1)
                    dve.wait_ge(g_s, m + 1)
                    nc.vector.tensor_tensor(silu[n % 2][:, :], silu[n % 2][:, :], bank_g[n % 2][:, :], ALU.mult).then_inc(h_s, 1)
                    dve.wait_ge(hh_s, m + 1)
                    nc.vector.tensor_tensor(h_lo[n % 2][:, :], silu[n % 2][:, :], h_hi[n % 2][:, :].bitcast(F32), ALU.subtract).then_inc(hl_s, 1)
            for_rows(dve, row)

        def gpsimd(pool):
            pool.wait_ge(place_s, 1)
            for b in range(B):
                for t in range(b * QT, b * QT + QT):
                    for k in range(2):
                        nc.gpsimd.indirect_dma_start(out=rows_in, out_offset=bass.IndirectOffsetOnAxis(ap=slots_i[:, t, k:k + 1], axis=0),
                                                     in_=O[:, t, :], in_offset=None).then_inc(row_s, 16)
                pool.wait_ge(row_s, 16 * QT * 2 * (b + 1))
                pool.sem_inc(moved_s, 1)
        run_block(nc, sync=sync, gpsimd=gpsimd, scalar=scalar, vector=vector, tensor=tensor)

    with ExitStack() as sub:
        psem = lambda name: sub.enter_context(nc.semaphore(name))
        sbt = lambda name, shape, dt=F32: sub.enter_context(nc.sbuf_tensor(name, shape, dt))
        (xt_s, xhi_s, xlo_s, h_s, silu_s, gt_s, ghi_s, glo_s, y_s, yb_s) = (
            psem("m_" + x) for x in "xt xhi xlo h silu gt ghi glo y yb".split())
        load_s = [psem(f"m_load{i}") for i in range(2)]
        store_s = [psem(f"m_store{i}") for i in range(2)]
        rows = [sbt(f"m_rows{i}", [P, 4, D]) for i in range(2)]
        x_hi = [sbt(f"m_xhi{i}", [P, D], F32R) for i in range(2)]
        x_lo = [sbt(f"m_xlo{i}", [P, D], F32R) for i in range(2)]
        g = [sbt(f"m_g{i}", [P, HID]) for i in range(2)]
        g_hi = [sbt(f"m_ghi{i}", [P, P], F32R) for i in range(2)]
        g_lo = [sbt(f"m_glo{i}", [P, P], F32R) for i in range(2)]
        y = [sbt(f"m_y{i}", [P, 4, D]) for i in range(2)]
        bank = lambda name: [sub.enter_context(nc.psum_tensor(f"m_{name}{i}", [P, D], F32)) for i in range(2)]
        bank_x, bank_h, bank_g, bank_y = bank("bx"), bank("bh"), bank("bg"), bank("by")

        def for_tiles(engine, step, lag):
            for s in range(8):
                step(s, s, 0)
            with engine.Fori(1, TILES // 8) as eight:
                for i in range(8):
                    step(eight * 8 + i, i, eight)
            for s in range(TILES, TILES + lag):
                step(s, s % 8, TILES // 8)

        def valid(s):
            return not isinstance(s, int) or 0 <= s < TILES

        in_v = rows_in.rearrange("(n f p) d -> n p f d", f=4, p=P)
        out_v = rows_out.rearrange("(n f p) d -> n p f d", f=4, p=P)

        def sync(sp):
            def load(four, half, round_):
                if later(round_):
                    sp.wait_ge(xt_s, (four - 1) * 4)
                sp.dma_start(rows[half][:, :, :], in_v[bass.ds(four, 1)].rearrange("a p f d -> p (a f) d")).then_inc(load_s[half], 16)
            load(0, 0, 0)
            load(1, 1, 0)
            with sp.Fori(1, TILES // 8) as eight:
                for half in range(2):
                    load(eight * 2 + half, half, eight)

        def gpsimd(pool):
            def store(four, half):
                pool.wait_ge(yb_s, four * 4 + 4)
                pool.dma_start(out_v[bass.ds(four, 1)].rearrange("a p f d -> p (a f) d"), y[half][:, :, :]).then_inc(store_s[half], 16)
            with pool.Fori(0, TILES // 8) as eight:
                for half in range(2):
                    store(eight * 2 + half, half)
            for half in range(2):
                pool.wait_ge(store_s[half], 16 * (TILES // 8))

        def scalar(act):
            def step(s, i, eight):
                if valid(s):
                    act.wait_ge(xt_s, s + 1)
                    if later(s - 1):
                        act.wait_ge(h_s, s - 1)
                    nc.scalar.copy(x_hi[i % 2][:, :], bank_x[i % 2][:, :]).then_inc(xhi_s, 1)
                if valid(s - 1):
                    act.wait_ge(h_s, s)
                    if later(s - 2):
                        act.wait_ge(gt_s, s - 2)
                    nc.scalar.activation(g[(i - 1) % 2][:, :], bank_h[(i - 1) % 2][:, 0:HID], ACT.Silu).then_inc(silu_s, 1)
                if valid(s - 2):
                    act.wait_ge(gt_s, s - 1)
                    if later(s - 3):
                        act.wait_ge(y_s, s - 3)
                    nc.scalar.copy(g_hi[i % 2][:, :], bank_g[i % 2][:, 0:P]).then_inc(ghi_s, 1)
            for_tiles(act, step, 2)

        def vector(dve):
            def step(s, i, eight):
                if valid(s):
                    dve.wait_ge(xhi_s, s + 1)
                    nc.vector.tensor_tensor(x_lo[i % 2][:, :], bank_x[i % 2][:, :], x_hi[i % 2][:, :].bitcast(F32), ALU.subtract).then_inc(xlo_s, 1)
                if valid(s - 2):
                    dve.wait_ge(ghi_s, s - 1)
                    nc.vector.tensor_tensor(g_lo[i % 2][:, :], bank_g[i % 2][:, 0:P], g_hi[i % 2][:, :].bitcast(F32), ALU.subtract).then_inc(glo_s, 1)
                if valid(s - 3):
                    dve.wait_ge(y_s, s - 2)
                    j = (i - 3) % 8
                    before = eight if j < 5 else eight - 1
                    if j % 4 == 0 and later(before):
                        dve.wait_ge(store_s[j // 4], before * 16)
                    nc.vector.tensor_copy(y[j // 4][:, j % 4, :], bank_y[j % 2][:, :]).then_inc(yb_s, 1)
            for_tiles(dve, step, 3)

        def tensor(pe):
            at_r = [pe.alloc_register(name=f"expert_at{j}") for j in range(12)]

            def step(s, i, eight):
                if i == 0:
                    if valid(s - 4):
                        pe.load(at_r[0:4], owner_i[0:1, bass.ds(s, 4)])
                    if valid(s):
                        pe.load(at_r[4:12], owner_i[0:1, bass.ds(s + 4, 8)])
                expert_of = lambda j: pe.snap(at_r[4 + j], min_val=0, max_val=(E - 1) * D)
                if valid(s):
                    pe.wait_ge(load_s[i // 4], (eight + 1) * 16)
                    if later(s - 1):
                        pe.wait_ge(xlo_s, s - 1)
                    for c in range(DC):
                        last = nc.tensor.transpose(bank_x[i % 2][:, c * P:(c + 1) * P], rows[i // 4][:, i % 4, c * P:(c + 1) * P], ident[:, :])
                    last.then_inc(xt_s, 1)
                if valid(s - 1):
                    q = (i - 1) % 2
                    at = expert_of(i - 1)
                    pe.wait_ge(xlo_s, s)
                    if later(s - 2):
                        pe.wait_ge(silu_s, s - 2)
                    k = 0
                    for c in range(DC):
                        for a, b in ((x_lo, 0), (x_hi, 1), (x_hi, 0)):
                            last = nc.tensor.matmul(bank_h[q][:, 0:HID], a[q][:, c * P:(c + 1) * P], (w_hi, w_lo)[b][:, bass.ds(at + (W1 + c * HID), HID)],
                                                    start=k == 0, stop=k == 5)
                            k += 1
                    last.then_inc(h_s, 1)
                if valid(s - 2):
                    pe.wait_ge(silu_s, s - 1)
                    if later(s - 3):
                        pe.wait_ge(glo_s, s - 3)
                    nc.tensor.transpose(bank_g[i % 2][:, 0:P], g[i % 2][:, :], ident[:, :]).then_inc(gt_s, 1)
                if valid(s - 3):
                    q = (i - 3) % 2
                    at = expert_of(i - 3)
                    pe.wait_ge(glo_s, s - 2)
                    if later(s - 4):
                        pe.wait_ge(yb_s, s - 4)
                    for k, (a, b) in enumerate(((g_lo, 0), (g_hi, 1), (g_hi, 0))):
                        last = nc.tensor.matmul(bank_y[q][:, :], a[q][:, :], (w_hi, w_lo)[b][:, bass.ds(at + W2, D)], start=k == 0, stop=k == 2)
                    last.then_inc(y_s, 1)
            for_tiles(pe, step, 3)
        run_block(nc, sync=sync, gpsimd=gpsimd, scalar=scalar, vector=vector, tensor=tensor)

    with ExitStack() as sub:
        psem = lambda name: sub.enter_context(nc.semaphore("e_" + name))
        sbt = lambda name, shape, dt=F32: sub.enter_context(nc.sbuf_tensor("e_" + name, shape, dt))
        (sum0_s, sum_s, bn_s, ag_s, var_s, pow_s, nmr_s, z_s, res_s, out_s, held) = (
            psem(x) for x in "sum0 sum bn ag var pow nmr z res out held".split())
        rows_s = [psem(f"rows{i}") for i in range(2)]
        picked = [[[sbt(f"picked{i}{t}{k}", [P, D]) for k in range(2)] for t in range(QT)] for i in range(2)]
        stats = sbt("stats", [P, QT, 6])
        meanvar = sbt("meanvar", [P, QT, 2])
        vareps = sbt("vareps", [P, QT])
        rstd = sbt("rstd", [P, QT])
        nmr = sbt("nmr", [P, QT])
        out_v = out.rearrange("b (t p) d -> p (b t) d", p=P)

        def pairs(engine, row):
            for b in range(2):
                row(b, b)
            with engine.Fori(1, B // 2) as two:
                for odd in range(2):
                    row(two * 2 + odd, odd)

        def sync(sp):
            def row(b):
                sp.wait_ge(res_s, b + 1)
                sp.dma_start(out_v[:, bass.ds(b * QT, QT), :], tiles_of(X, b)).then_inc(out_s, 16)
            for_rows(sp, row)
            sp.wait_ge(out_s, 16 * B)

        def gpsimd(pool):
            def scale_row(b):
                pool.wait_ge(var_s, b + 1)
                if later(b):
                    pool.wait_ge(z_s, b * QT)
                nc.gpsimd.tensor_tensor(rstd[:, :], vareps[:, :], halves[:, :], ALU.pow).then_inc(pow_s, 1)

            for b in range(B):
                for t in range(QT):
                    if b > 1:
                        pool.wait_ge(sum_s, (b - 2) * QT + t + 1)
                    for k in range(2):
                        nc.gpsimd.indirect_dma_start(out=picked[b % 2][t][k][:, :], out_offset=None, in_=rows_out,
                                                     in_offset=bass.IndirectOffsetOnAxis(ap=slots_i[:, b * QT + t, k:k + 1], axis=0)).then_inc(rows_s[b % 2], 16)
                if b > 0:
                    scale_row(b - 1)
            scale_row(B - 1)

        def scalar(act):
            def row(b):
                act.wait_ge(nmr_s, b + 1)
                for t in range(QT):
                    nc.scalar.activation(one(O, b * QT + t), one(O, b * QT + t), ACT.Identity,
                                         bias=nmr[:, t:t + 1], scale=rstd[:, t:t + 1]).then_inc(z_s, 1)
            for_rows(act, row)

        def vector(dve):
            def add_rows(b, odd):
                dve.wait_ge(rows_s[odd], (b - odd + 2) * QT * 16)
                for k, done in ((0, sum0_s), (1, sum_s)):
                    for t in range(QT):
                        n = b * QT + t
                        if k == 1:
                            dve.wait_ge(sum0_s, n + 1)
                        nc.vector.scalar_tensor_tensor(one(O, n), picked[odd][t][k][:, :], wts[:, bass.ds(n, 1), k],
                                                       one(O, n), ALU.mult, ALU.add).then_inc(done, 1)
                for t in range(QT):
                    dve.wait_ge(sum_s, b * QT + t + 1)
                    dve.sem_inc(held, 1)
                    nc.vector.bn_stats(stats[:, t, :], one(O, b * QT + t)).then_inc(bn_s, 1)
                dve.wait_ge(bn_s, b * QT + QT)
                dve.sem_inc(held, 1)
                for t in range(QT):
                    last = nc.vector.bn_aggr(meanvar[:, t, :], stats[:, t, :])
                last.then_inc(ag_s, 1)
                dve.wait_ge(ag_s, b + 1)
                if later(b):
                    dve.wait_ge(pow_s, b)
                nc.vector.tensor_scalar_add(vareps[:, :], meanvar[:, :, 1], EPS).then_inc(var_s, 1)
                dve.wait_ge(pow_s, b + 1)
                if later(b):
                    dve.wait_ge(z_s, b * QT)
                nc.vector.scalar_tensor_tensor(nmr[:, :], meanvar[:, :, 0], -1.0, rstd[:, :], ALU.mult, ALU.mult).then_inc(nmr_s, 1)

            def residual(b):
                dve.wait_ge(z_s, b * QT + QT)
                nc.vector.tensor_tensor(tiles_of(X, b), tiles_of(X, b), tiles_of(O, b), ALU.add).then_inc(res_s, 1)

            def row(b, odd):
                add_rows(b, odd)
                if later(b):
                    residual(b - 1)
            pairs(dve, row)
            residual(B - 1)
        run_block(nc, sync=sync, gpsimd=gpsimd, scalar=scalar, vector=vector)


def transformer_layer(nc, x, w_qkv, w_out, b_out, gate_t, experts_t, cos, sin, ident_in, iota,
                      upper, steps, rows128, rows_in, rows_out, out):
    with ExitStack() as ctx:
        X = ctx.enter_context(nc.sbuf_tensor("X", [P, NT, D], F32))
        O = ctx.enter_context(nc.sbuf_tensor("O", [P, NT, D], F32))
        ident = ctx.enter_context(nc.sbuf_tensor("identity", [P, P], F32))
        ident_r = ctx.enter_context(nc.sbuf_tensor("identity_r", [P, P], F32R))
        with ExitStack() as sub:
            sync, gpsimd, scalar, vector, tensor = attention(nc, sub, x, w_qkv, cos, sin, ident_in, rows_in,
                                                               X, O, ident, ident_r)
            run_block(nc, sync, gpsimd, scalar, vector, tensor)
        with ExitStack() as sub:
            feed_forward(nc, sub, w_out, b_out, gate_t, experts_t, iota, upper, steps,
                         rows128, rows_in, rows_out, out, X, O, ident)


def kernel(L0_attn_x, L0_attn_w_qkv, L0_attn_w_out, L0_attn_b_out, L0_ffn_gate_w, L0_ffn_w1, L0_ffn_w2,
           L0_ffn_sfc1, L0_ffn_sfc2, L0_ffn_sfc3):
    import numpy as np
    import concourse.bacc as bacc
    from concourse.bass_utils import run_bass_kernel_spmd

    def rows(a):
        a = np.asarray(a)
        return np.ascontiguousarray(a.reshape(-1, P, a.shape[1]).transpose(1, 0, 2).reshape(P, -1))

    w1 = np.asarray(L0_ffn_w1)
    w2 = np.asarray(L0_ffn_w2)
    gate = np.zeros((D, P), w1.dtype)
    gate[:, 0:E] = np.asarray(L0_ffn_gate_w).T
    freqs = np.float32(10000.0) ** (-np.arange(0, HD, 2, dtype=np.float32) / np.float32(HD))
    angles = np.arange(N, dtype=np.float32)[:, None] * freqs
    sin = np.repeat(np.sin(angles), 2, axis=1).astype(np.float32)
    sin[:, 0:HD // 2] *= -1
    inputs = {
        "x": np.asarray(L0_attn_x),
        "w_qkv": np.asarray(L0_attn_w_qkv),
        "w_out": rows(L0_attn_w_out),
        "b_out": np.asarray(L0_attn_b_out),
        "gate_t": rows(gate),
        "experts_t": np.concatenate([
            w1.reshape(E, HID, DC, P).transpose(3, 0, 2, 1).reshape(P, -1),
            w2.transpose(2, 0, 1).reshape(P, -1),
            rows(np.asarray(L0_ffn_sfc1).T), rows(np.asarray(L0_ffn_sfc2).T), rows(np.asarray(L0_ffn_sfc3).T)], axis=1),
        "cos": np.repeat(np.cos(angles), 2, axis=1).astype(np.float32),
        "sin": sin,
        "ident_in": np.eye(P, dtype=np.float32),
        "upper": np.triu(np.ones((P, P), np.float32), 1),
        "steps": np.arange(TILES, dtype=np.float32)[None, :],
        "rows128": np.tile(np.arange(NT, dtype=np.float32) * P, (P, 1)),
        "iota": np.tile(np.arange(E, dtype=np.float32), (P, 1)),
    }
    nc = bacc.Bacc("TRN2", target_bir_lowering=False, num_devices=1)
    aps = {k: nc.dram_tensor("in_" + k, a.shape, mybir.dt.from_np(a.dtype), kind="ExternalInput").ap()
           for k, a in inputs.items()}
    out = nc.dram_tensor("out", (B, N, D), F32, kind="ExternalOutput").ap()
    rows_in, rows_out = (nc.dram_tensor(name, (TILES * P, D), F32, kind="Internal").ap() for name in ("rows_in", "rows_out"))
    transformer_layer(nc, **aps, rows_in=rows_in, rows_out=rows_out, out=out)
    results = run_bass_kernel_spmd(nc, [{"in_" + k: a for k, a in inputs.items()}], core_ids=[0])
    return results.results[0]["out"]
```

```python
import concourse.bass as bass
from concourse import mybir
from contextlib import ExitStack

B, N, D, H, HD = 8, 512, 256, 16, 16
P = 128
QT = N // P
DC = D // P
GH = 4
NG = H // GH
EPS = 1e-5

F32 = mybir.dt.float32
F32R = mybir.dt.float32r
ALU = mybir.AluOpType
ACT = mybir.ActivationFunctionType
AX = mybir.AxisListType


def later(count):
    return not isinstance(count, int) or count > 0


def attention(nc, ctx, x_in, w_qkv, cos_in, sin_in, ident_in, rows_in, X, O, ident, ident_r):
    def sb(name, shape, dt=F32):
        return ctx.enter_context(nc.sbuf_tensor(name, shape, dt))

    def ps(name):
        return ctx.enter_context(nc.psum_tensor(name, [P, 512], F32))

    def sem(name):
        return ctx.enter_context(nc.semaphore(name))

    w_raw = sb("w_raw", [P, DC, 3 * D])
    w_hi = sb("w_hi", [P, DC, 3 * D], F32R)
    w_lo = sb("w_lo", [P, DC, 3 * D], F32R)
    cos = sb("cos", [P, QT, HD])
    sin = sb("sin", [P, QT, HD])
    halves = sb("halves", [P, QT])
    zero = sb("zero", [P, D])
    stats = sb("stats", [P, QT, 6])
    meanvar = sb("meanvar", [P, QT, 2])
    vareps = sb("vareps", [P, QT])
    rstd = sb("rstd", [P, QT])
    xn = sb("xn", [P, QT, D])
    xt_hi = sb("xt_hi", [P, DC, N], F32R)
    xt_lo = sb("xt_lo", [P, DC, N], F32R)
    qk_raw = [sb(f"qk_raw{i}", [P, 2 * D]) for i in range(2)]
    rope_a = sb("rope_a", [P, 2 * D])
    rope_b = sb("rope_b", [P, 2 * D])
    qk = [sb(f"qk{i}", [P, QT, 2 * D]) for i in range(2)]
    v_aug = [sb(f"v_aug{i}", [P, QT, H, 2 * HD]) for i in range(2)]
    stage_q = [[sb(f"stage_q{g}{p}", [P, QT, P], F32R) for p in range(2)] for g in range(2)]
    stage_k = [sb(f"stage_k{i}", [P, QT, P], F32R) for i in range(2)]
    q_st = [[sb(f"q_st{g}{p}", [P, N], F32R) for p in range(2)] for g in range(2)]
    k_st = [[[sb(f"k_st{g}{p}{a}", [P, N], F32R) for a in range(2)] for p in range(2)] for g in range(2)]
    probs = [[sb(f"probs{h}{k}", [P, N]) for k in range(QT)] for h in range(2)]
    negmax = [sb(f"negmax{p}", [P, QT, 2]) for p in range(2)]
    o_t = sb("o_t", [P, N])
    rden = sb("rden", [P, QT * GH])

    score = [ps(f"score{i}") for i in range(2)]
    natural = [ps(f"natural{i}") for i in range(2)]
    av = ps("av")
    bank_t = ps("bank_t")
    bank_a = ps("bank_a")
    bank_o = ps("bank_o")

    held = [sem(f"held{i}") for i in range(2)]
    zero_done = sem("zero_done")
    filled = sem("filled")
    x_first = sem("x_first")
    x_rest = sem("x_rest")
    w_loaded = sem("w_loaded")
    tables = sem("tables")
    w_hi_done = sem("w_hi_done")
    w_split = sem("w_split")
    consts = sem("consts")
    ones_v = sem("ones_v")
    stats_done = sem("stats_done")
    aggr_done = sem("aggr_done")
    var_done = sem("var_done")
    rstd_done = sem("rstd_done")
    xn_done = sem("xn_done")
    xt_ps = sem("xt_ps")
    xth_done = sem("xth_done")
    xtl_done = sem("xtl_done")
    qk_ps = sem("qk_ps")
    qk_out = sem("qk_out")
    v_ps = sem("v_ps")
    v_done = sem("v_done")
    rope_part = sem("rope_part")
    rope_part_v = sem("rope_part_v")
    rope_sum = sem("rope_sum")
    qk_done = sem("qk_done")
    stage_hi = sem("stage_hi")
    staged = sem("staged")
    tr_ps = sem("tr_ps")
    q_done = sem("q_done")
    k_done = sem("k_done")
    nat_ps = sem("nat_ps")
    max_done = sem("max_done")
    nm_hi = sem("nm_hi")
    nm_done = sem("nm_done")
    mt_ps = sem("mt_ps")
    mt_done = sem("mt_done")
    sc_ps = sem("sc_ps")
    exp_done = sem("exp_done")
    av_ps = sem("av_ps")
    ot_done = sem("ot_done")
    nt_ps = sem("nt_ps")
    rden_done = sem("rden_done")
    on_done = sem("on_done")

    x_v = x_in.rearrange("b (t p) d -> p (b t) d", p=P)
    w_v = w_qkv.rearrange("(c p) n -> p c n", p=P)

    A_JOBS = [("xt", 0), ("xt", 1), ("qk", 0), ("qk", 1), ("qk", 2), ("v", 0), ("qk", 3), ("v", 1)]
    A_PE = dict(zip([(0, 0), (0, 4), (0, 9), (0, 12), (1, 2), (1, 4), (1, 9), (1, 12)], A_JOBS))
    A_OUT = dict(zip([(0, 1), (0, 7), (0, 10), (0, 15), (1, 3), (1, 7), (1, 9), (1, 15)], A_JOBS))
    A_LOW = {(0, 2): 0, (0, 7): 1}
    T_PE = {1: (1, 1, "q"), 4: (1, 1, "k"), 8: (2, 0, "q"), 11: (2, 0, "k")}
    T_OUT = {3: (1, 1, "q", 0), 5: (1, 1, "k", 0), 6: (1, 1, "k", 1),
             9: (2, 0, "q", 0), 11: (2, 0, "k", 0), 14: (2, 0, "k", 1)}
    SPLIT = {0: (0, 1), 8: (1, 0)}
    M_PE = {2: (0, 1), 10: (1, 0)}
    M_OUT = {4: (0, 1), 10: (1, 0)}
    STAGE = {5: (0, "q"), 7: (0, "k"), 10: (1, "q"), 12: (1, "k")}
    NORM_STATS = {1: 0, 2: 1, 3: 2, 4: 3}
    NORM_AGGREGATE = 4
    NORM_APPLY = {6: 0, 9: 1, 11: 2, 14: 3}
    O_OUT, N_PE, NORMALISE = 2, 5, 6

    def columns(buf, off, n, dt):
        return (buf[:, :, :] if dt == F32R else buf[:, :, :].bitcast(F32)).rearrange(
            "p t (a r) -> p t a r", a=2)[:, :, :, off:off + n]

    def staging(odd, g, p, kind):
        c0 = (kind == "k") * D + (g * GH + 2 * p) * HD
        src = qk[odd][:, :, c0:c0 + 2 * HD].rearrange("p t (a j) -> p t a j", a=2)
        if kind == "q":
            return stage_q[g % 2][p], (0, 32), 16, src
        return stage_k[p], (0, 16), 32, src

    two_banks = lambda job: (bank_a, bank_t)[job % 2]

    def rope_products(engine, t, a, b, done):
        heads = lambda x: x.rearrange("p (h d) -> p h d", d=HD)
        src = heads(qk_raw[t % 2][:, :])
        c = cos[:, t, :].unsqueeze(1).broadcast_to([P, 2 * H, HD])
        engine.tensor_tensor(heads(a[:, :]), src, c, ALU.mult).then_inc(done, 1)
        for half in range(2):
            cols = slice(8 * half, 8 * half + 8)
            engine.tensor_tensor(heads(b[:, :])[:, :, cols], src[:, :, 1 - half::2],
                                 sin[:, t, cols].unsqueeze(1).broadcast_to([P, 2 * H, 8]), ALU.mult).then_inc(done, 1)

    def pairs(engine, batch):
        for b in range(2):
            batch(b, b % 2, b > 0, True)
        with engine.Fori(1, B // 2 - 1) as two:
            for odd in range(2):
                batch(two * 2 + odd, odd, True, True)
        for b in range(B - 2, B):
            batch(b, b % 2, True, b < B - 1)

    def sync_engine(sp):
        sp.dma_start(X[:, 0:QT, :], x_v[:, 0:QT, :]).then_inc(x_first, 16)
        sp.dma_start(w_raw[:, :, :], w_v).then_inc(w_loaded, 16)
        sp.dma_start(ident[:, :], ident_in).then_inc(tables, 16)
        sp.dma_start(cos[:, :, :], cos_in.rearrange("(t p) d -> p t d", p=P)).then_inc(tables, 16)
        sp.dma_start(sin[:, :, :], sin_in.rearrange("(t p) d -> p t d", p=P)).then_inc(tables, 16)
        for b in range(1, B):
            sp.dma_start(X[:, b * QT:(b + 1) * QT, :], x_v[:, b * QT:(b + 1) * QT, :]).then_inc(x_rest, 16)

        sp.wait_ge(zero_done, 1)
        fill = rows_in.rearrange("(n s p) d -> n p s d", n=4, p=P)
        for n in range(4):
            sp.dma_start(fill[n], zero[:, :].unsqueeze(1).broadcast_to([P, fill.shape[2], D])).then_inc(filled, 16)

        sp.wait_ge(filled, 64)

    def gpsimd_engine(pool):
        nc.gpsimd.memset(halves[:, :], -0.5)
        nc.gpsimd.memset(zero[:, :], 0.0).then_inc(zero_done, 1)
        for p in range(2):
            for g in range(2):
                nc.gpsimd.memset(stage_q[g][p][:, :, :].bitcast(F32), 0.0)
            nc.gpsimd.memset(stage_k[p][:, :, :].bitcast(F32), 0.0)
        for i in range(2):
            last = nc.gpsimd.memset(v_aug[i][:, :, :, :], 1.0)
        last.then_inc(ones_v, 1)
        pool.wait_ge(ones_v, 1)
        for p in range(2):
            ones = stage_k[p][:, :, :].bitcast(F32).rearrange("p t (a r) -> p (t a) r", a=2)
            last = nc.gpsimd.memset(ones[:, :, 48:50], 1.0)
        last.then_inc(consts, 1)
        pool.wait_ge(consts, 2)

        def row_scale(b):
            pool.wait_ge(var_done, b + 1)
            if later(b):
                pool.wait_ge(xn_done, b * QT)
            nc.gpsimd.tensor_tensor(rstd[:, :], vareps[:, :], halves[:, :], ALU.pow).then_inc(rstd_done, 1)

        def rope(b, odd, t, elsewhere=2):
            n = b * QT + t
            pool.wait_ge(qk_out, n + 1)
            if later(n):
                pool.wait_ge(qk_done, n)
            rope_products(nc.gpsimd, t, rope_a, rope_b, rope_part)
            pool.wait_ge(rope_part, (n - elsewhere) * 3 + 3)
            nc.gpsimd.tensor_tensor(qk[odd][:, t, :], rope_a[:, :], rope_b[:, :], ALU.add).then_inc(qk_done, 1)

        pool.wait_ge(tables, 48)
        row_scale(0)
        for t in (0, 2):
            rope(0, 0, t, t // 2)
        row_scale(1)

        def batch(b, odd, has_prev, has_next):
            if has_next:
                for t in range(QT):
                    rope(b + 1, 1 - odd, t)
            if not (isinstance(b, int) and b + 2 >= B):
                row_scale(b + 2)
        pairs(pool, batch)

    def scalar_engine(act):
        def evacuate_t(G, gp, p, kind, half):
            if kind == "q":
                act.wait_ge(tr_ps, G * 4 + 2 * p + 1)
                if later(G * 16 + 8 * p - 24):
                    act.wait_ge(sc_ps, G * 16 + 8 * p - 24)
                nc.scalar.copy(q_st[gp][p][:, :], bank_t[:, :]).then_inc(q_done, 1)
            else:
                act.wait_ge(tr_ps, G * 4 + 2 * p + 2)
                rows = slice(64 * half, 64 * half + 64)
                nc.scalar.copy(k_st[gp][p][half][rows, :], bank_t[rows, :]).then_inc(k_done, 1)

        def a_job(b, odd, what, n, bank=bank_a):
            if what == "xt":
                act.wait_ge(xt_ps, b * DC + n + 1)
                if later(b) and n == 0:
                    act.wait_ge(v_ps, b * 2)
                nc.scalar.copy(xt_hi[:, n, :], bank[:, :]).then_inc(xth_done, 1)
            if what == "qk":
                act.wait_ge(qk_ps, b * QT + n + 1)
                if later(b * QT + n - 1):
                    act.wait_ge(qk_done, b * QT + n - 1)
                nc.scalar.copy(qk_raw[n % 2][:, :], bank[:, :]).then_inc(qk_out, 1)
            if what == "v":
                act.wait_ge(v_ps, b * 2 + n + 1)
                if later(b * H - H) and n == 0:
                    act.wait_ge(av_ps, b * H - H)
                nc.scalar.copy(v_aug[odd][:, 2 * n:2 * n + 2, :, 0:HD].rearrange("p t h d -> p (t h) d"),
                               bank[:, :].rearrange("p (h d) -> p h d", d=HD)).then_inc(v_done, 1)

        def max_job(G, gp, p):
            act.wait_ge(mt_ps, G * 2 + p + 1)
            nc.scalar.copy(q_st[gp][p][:, :], bank_o[:, :]).then_inc(mt_done, 1)

        def out_job(G):
            act.wait_ge(av_ps, G * GH + GH)
            if later(G):
                act.wait_ge(nt_ps, G)
            nc.scalar.copy(o_t[:, :], av[:, :]).then_inc(ot_done, 1)

        act.wait_ge(tables, 48)
        nc.scalar.copy(ident_r[:, :], ident[:, :]).then_inc(w_hi_done, 1)
        act.wait_ge(w_loaded, 16)
        nc.scalar.copy(w_hi[:, :, :], w_raw[:, :, :]).then_inc(w_hi_done, 1)
        act.wait_ge(consts, 2)
        for job, (what, n) in enumerate(A_JOBS):
            a_job(0, 0, what, n, two_banks(job))
        for p in range(2):
            for kind, half in (("q", 0), ("k", 0), ("k", 1)):
                evacuate_t(0, 0, p, kind, half)
        max_job(0, 0, 0)
        for kind, half in (("q", 0), ("k", 0), ("k", 1)):
            evacuate_t(1, 1, 0, kind, half)

        def batch(b, odd, has_prev, has_next):
            for g in range(NG):
                G = b * NG + g
                for i in range(GH):
                    head = b * H + g * GH + i
                    for kt in range(QT):
                        act.wait_ge(sc_ps, head * QT + kt + 1)
                        if kt == 0 and later(head - 1):
                            act.wait_ge(av_ps, head - 1)
                        nc.scalar.activation(probs[i % 2][kt][:, :], score[kt % 2][:, :], ACT.Exp,
                                             scale=HD ** -0.5).then_inc(exp_done, 1)
                        u = i * QT + kt
                        if u == O_OUT and (has_prev or g > 0):
                            out_job(G - 1)
                        if u in T_OUT:
                            ahead, p, kind, half = T_OUT[u]
                            if has_next or g + ahead < NG:
                                evacuate_t(G + ahead, (g + ahead) % 2, p, kind, half)
                        if u in M_OUT:
                            ahead, p = M_OUT[u]
                            if has_next or g + ahead < NG:
                                max_job(G + ahead, (g + ahead) % 2, p)
                        if (g, u) in A_OUT and has_next:
                            a_job(b + 1, 1 - odd, *A_OUT[g, u])
        pairs(act, batch)
        out_job(B * NG - 1)

    def vector_engine(dve):
        def norm_stats(b, t):
            dve.sem_inc(held[0], 1)
            nc.vector.bn_stats(stats[:, t, :], X[:, bass.ds(b * QT + t, 1), :].rearrange("p a d -> p (a d)")).then_inc(stats_done, 1)

        def norm_aggregate(b):
            dve.wait_ge(stats_done, b * QT + QT)
            dve.sem_inc(held[0], 1)
            for t in range(QT):
                nc.vector.bn_aggr(meanvar[:, t, :], stats[:, t, :]).then_inc(aggr_done, 1)
            dve.wait_ge(aggr_done, b * QT + QT)
            nc.vector.tensor_scalar_add(vareps[:, :], meanvar[:, :, 1], EPS).then_inc(var_done, 1)

        def norm_apply(b, t):
            if t == 0:
                dve.wait_ge(rstd_done, b + 1)
                if later(b):
                    dve.wait_ge(xt_ps, b * DC)
            nc.vector.tensor_scalar(xn[:, t, :], X[:, bass.ds(b * QT + t, 1), :].rearrange("p a d -> p (a d)"),
                                    meanvar[:, t, 0:1], rstd[:, t:t + 1],
                                    ALU.subtract, ALU.mult).then_inc(xn_done, 1)

        def xt_low(b, c, bank=bank_a):
            dve.wait_ge(xth_done, b * DC + c + 1)
            nc.vector.tensor_tensor(xt_lo[:, c, :], bank[:, :], xt_hi[:, c, :].bitcast(F32),
                                    ALU.subtract).then_inc(xtl_done, 1)

        def row_max(G, i, t):
            n = G * 16 + i * QT + t
            dve.wait_ge(nat_ps, n + 1)
            if i % 2 == 0 and t == 0 and later(G):
                dve.wait_ge(nm_done, G * 2 + i // 2 - 1)
            nc.vector.tensor_reduce(negmax[i // 2][:, t, i % 2:i % 2 + 1], natural[t % 2][:, :], AX.X, ALU.max,
                                    negate=True).then_inc(max_done, 1)

        def max_split(G, gp, p):
            dve.wait_ge(max_done, G * 16 + 8 * p + 8)
            place = lambda off, dt: columns(stage_q[gp][p], off, 1, dt).rearrange("p t a r -> p t (a r)")
            nc.vector.tensor_copy(place(48, F32R), negmax[p][:, :, :]).then_inc(nm_hi, 1)
            dve.wait_ge(nm_hi, G * 2 + p + 1)
            nc.vector.tensor_tensor(place(49, F32R), negmax[p][:, :, :], place(48, F32), ALU.subtract).then_inc(nm_done, 1)

        def stage(b, odd, g, p, kind):
            G = b * NG + g
            buf, his, lo, src = staging(odd, g, p, kind)
            if kind == "q":
                if g == 0 and p == 0:
                    dve.wait_ge(qk_done, b * QT + QT)
                if later((G - 2) * 2 + p + 1):
                    dve.wait_ge(mt_ps, (G - 2) * 2 + p + 1)
                    dve.sem_inc(held[0], 1)
                    nc.vector.memset(columns(buf, 48, 2, F32), 0.0)
            elif later((G - 1) * 4 + 2 * p + 2):
                dve.wait_ge(tr_ps, (G - 1) * 4 + 2 * p + 2)
            nc.vector.tensor_copy(columns(buf, his[0], HD, F32R), src).then_inc(stage_hi, 1)
            nc.vector.tensor_copy(columns(buf, his[1], HD, F32R), src)
            dve.wait_ge(stage_hi, G * 4 + 2 * p + (kind == "k") + 1)
            nc.vector.tensor_tensor(columns(buf, lo, HD, F32R), src, columns(buf, his[0], HD, F32), ALU.subtract).then_inc(staged, 1)

        def normalise(b, g):
            G = b * NG + g
            dve.wait_ge(nt_ps, G + 1)
            view = bank_o[:, :].rearrange("p (t i) -> p t i", i=2 * HD)
            nc.vector.reciprocal(rden[:, :], view[:, :, HD]).then_inc(rden_done, 1)
            dve.wait_ge(rden_done, G + 1)
            nc.vector.tensor_tensor(
                O[:, bass.ds(b * QT, QT), g * GH * HD:(g + 1) * GH * HD].rearrange("p t (i j) -> p t i j", i=GH),
                view[:, :, 0:HD].rearrange("p (t i) j -> p t i j", t=QT),
                rden[:, :].rearrange("p (t i) -> p t i", t=QT).unsqueeze(3).broadcast_to([P, QT, GH, HD]),
                ALU.mult).then_inc(on_done, 1)

        for g in range(2):
            for p in range(2):
                nc.vector.memset(k_st[g][p][0][64:128, :].bitcast(F32), 0.0)
                last = nc.vector.memset(k_st[g][p][1][0:64, :].bitcast(F32), 0.0)
        last.then_inc(consts, 1)
        dve.wait_ge(x_first, 16)
        for t in range(QT):
            norm_stats(0, t)
        norm_aggregate(0)
        dve.wait_ge(w_hi_done, 2)
        nc.vector.tensor_tensor(w_lo[:, :, :], w_raw[:, :, :], w_hi[:, :, :].bitcast(F32),
                                ALU.subtract).then_inc(w_split, 1)
        for t in range(QT):
            norm_apply(0, t)
        for c in range(DC):
            xt_low(0, c, two_banks(c))
        dve.wait_ge(consts, 2)
        dve.wait_ge(tables, 48)
        for t in (1, 3):
            dve.wait_ge(qk_out, t + 1)
            rope_products(nc.vector, t, probs[1][0], probs[1][1], rope_part_v)
            dve.wait_ge(rope_part_v, (t // 2 + 1) * 3)
            nc.vector.tensor_tensor(qk[0][:, t, :], probs[1][0][:, :], probs[1][1][:, :], ALU.add).then_inc(rope_sum, 1)
            dve.wait_ge(rope_sum, t // 2 + 1)
            dve.wait_ge(qk_done, t)
            dve.sem_inc(qk_done, 1)
        for g in range(2):
            for p in range(2):
                for kind in "qk":
                    stage(0, 0, g, p, kind)
        for i in range(GH):
            if i == 2:
                max_split(0, 0, 0)
            for t in range(QT):
                row_max(0, i, t)
        dve.wait_ge(x_rest, 16 * (B - 1))
        for t in range(QT):
            norm_stats(1, t)
        norm_aggregate(1)
        for t in range(QT):
            norm_apply(1, t)

        def batch(b, odd, has_prev, has_next):
            for g in range(NG):
                G = b * NG + g
                ahead = has_next or g < NG - 1
                for i in range(GH):
                    for kt in range(QT):
                        u = i * QT + kt
                        if ahead:
                            row_max(G + 1, i, kt)
                        if u in SPLIT and (SPLIT[u][0] == 0 or ahead):
                            max_split(G + SPLIT[u][0], (g + SPLIT[u][0]) % 2, SPLIT[u][1])
                        if (g, u) in A_LOW and has_next:
                            xt_low(b + 1, A_LOW[g, u])
                        if u == NORMALISE and g > 0:
                            normalise(b, g - 1)
                        if u == NORMALISE and g == 0 and has_prev:
                            normalise(b - 1, NG - 1)
                        if u in STAGE:
                            if g < 2:
                                stage(b, odd, g + 2, *STAGE[u])
                            elif has_next:
                                stage(b + 1, 1 - odd, g - 2, *STAGE[u])
                        if g == NG - 1 and not (isinstance(b, int) and b + 2 >= B):
                            if u in NORM_STATS:
                                norm_stats(b + 2, NORM_STATS[u])
                            if u == NORM_AGGREGATE:
                                norm_aggregate(b + 2)
                            if u in NORM_APPLY:
                                norm_apply(b + 2, NORM_APPLY[u])
        pairs(dve, batch)
        normalise(B - 1, NG - 1)

    def tensor_engine(pe):
        def a_wait(b, what, n):
            if what == "xt":
                if n:
                    pe.wait_ge(xtl_done, b * DC + n)
                else:
                    pe.wait_ge(xn_done, b * QT + QT)
                    pe.wait_ge(v_done, b * 2)
            elif what == "v":
                pe.wait_ge(qk_out, b * QT + 3 + n)
            elif n == 0:
                pe.wait_ge(xtl_done, b * DC + DC)
            elif n == QT - 1:
                pe.wait_ge(v_done, b * 2 + 1)
            else:
                pe.wait_ge(qk_out, b * QT + n)

        def a_job(what, n, bank=bank_a):
            if what == "xt":
                for t in range(QT):
                    last = nc.tensor.transpose(bank[:, t * P:(t + 1) * P], xn[:, t, n * P:(n + 1) * P], ident[:, :])
                last.then_inc(xt_ps, 1)
                return
            if what == "qk":
                tiles, cols, width = [n], slice(0, 2 * D), 2 * D
            else:
                tiles, cols, width = [2 * n, 2 * n + 1], slice(2 * D, 3 * D), D
            terms = [(k, t, c, x, w) for k, t in enumerate(tiles) for c in range(DC)
                     for x, w in ((xt_lo, w_hi), (xt_hi, w_lo), (xt_hi, w_hi))]
            for j, (k, t, c, x, w) in enumerate(terms):
                last = nc.tensor.matmul(bank[:, k * width:(k + 1) * width], x[:, c, t * P:(t + 1) * P], w[:, c, cols],
                                        start=j == 0, stop=j == len(terms) - 1, skip_group_check=True)
            last.then_inc(qk_ps if what == "qk" else v_ps, 1)

        def t_job(G, gp, p, kind):
            if kind == "q":
                pe.wait_ge(staged, G * 4 + 2 * p + 1)
                if later(G * 2 + p):
                    pe.wait_ge(k_done, (G * 2 + p) * 2)
                src = stage_q[gp][p]
            else:
                pe.wait_ge(staged, G * 4 + 2 * p + 2)
                pe.wait_ge(q_done, G * 2 + p + 1)
                src = stage_k[p]
            for t in range(QT):
                last = nc.tensor.matmul(bank_t[:, t * P:(t + 1) * P], src[:, t, :], ident_r[:, :], start=True, stop=True)
            last.then_inc(tr_ps, 1)

        def natural_scores(G, gp, i, t):
            p, a = i // 2, i % 2
            n = G * 16 + i * QT + t
            if a == 0 and t == 0:
                pe.wait_ge(k_done, (G * 2 + p + 1) * 2)
            if later(n - 1):
                pe.wait_ge(max_done, n - 1)
            nc.tensor.matmul(natural[t % 2][:, :], q_st[gp][p][:, t * P:(t + 1) * P], k_st[gp][p][a][:, :],
                             start=True, stop=True).then_inc(nat_ps, 1)

        def m_job(G, gp, p):
            pe.wait_ge(nm_done, G * 2 + p + 1)
            if later(G * 2 + p):
                pe.wait_ge(mt_done, G * 2 + p)
            if p == 0 and later(G - 1):
                pe.wait_ge(on_done, G - 1)
            for t in range(QT):
                last = nc.tensor.matmul(bank_o[:, t * P:(t + 1) * P], stage_q[gp][p][:, t, :], ident_r[:, :], start=True, stop=True)
            last.then_inc(mt_ps, 1)

        def n_job(G, before_mt):
            pe.wait_ge(ot_done, G + 1)
            pe.wait_ge(mt_done, before_mt)
            for t in range(QT):
                last = nc.tensor.transpose(bank_o[:, t * P:(t + 1) * P], o_t[:, t * P:(t + 1) * P], ident[:, :])
            last.then_inc(nt_ps, 1)

        def attend(b, odd, hl, kt):
            head = b * H + hl
            i = hl % GH
            pe.wait_ge(exp_done, head * QT + kt + 1)
            if i == 0 and kt == 0 and later(b * NG + hl // GH):
                pe.wait_ge(ot_done, b * NG + hl // GH)
            if hl == 0 and kt == 0:
                pe.wait_ge(v_done, b * 2 + 2)
            last = nc.tensor.matmul(av[32 * i:32 * i + 32, :], v_aug[odd][:, kt, hl, :], probs[hl % 2][kt][:, :],
                                    start=kt == 0, stop=kt == QT - 1)
            if kt == QT - 1:
                last.then_inc(av_ps, 1)

        pe.wait_ge(w_hi_done, 2)
        pe.wait_ge(consts, 2)
        pe.wait_ge(xn_done, QT)
        read_out = {"xt": xtl_done, "qk": qk_out, "v": v_done}
        for job, (what, n) in enumerate(A_JOBS):
            if job == DC:
                pe.wait_ge(w_split, 1)
                pe.wait_ge(xtl_done, DC)
            elif job > DC:
                what_before, n_before = A_JOBS[job - 2]
                if what_before != "xt":
                    pe.wait_ge(read_out[what_before], n_before + 1)
            a_job(what, n, two_banks(job))
        pe.wait_ge(v_done, 2)
        for p in range(2):
            for kind in "qk":
                t_job(0, 0, p, kind)
        for i in range(GH):
            for t in range(QT):
                natural_scores(0, 0, i, t)
            if i == 2:
                m_job(0, 0, 0)
        for kind in "qk":
            t_job(1, 1, 0, kind)

        def batch(b, odd, has_prev, has_next):
            for g in range(NG):
                G = b * NG + g
                gp = g % 2
                for i in range(GH):
                    p, a = i // 2, i % 2
                    hl = g * GH + i
                    for kt in range(QT):
                        n = (b * H + hl) * QT + kt
                        if kt == 0 and a == 0:
                            pe.wait_ge(mt_done, G * 2 + p + 1)
                        if later(n - 1):
                            pe.wait_ge(exp_done, n - 1)
                        nc.tensor.matmul(score[kt % 2][:, :], k_st[gp][p][a][:, kt * P:(kt + 1) * P],
                                         q_st[gp][p][:, :], start=True, stop=True).then_inc(sc_ps, 1)
                        if has_next or g < NG - 1:
                            natural_scores(G + 1, 1 - gp, i, kt)
                        u = i * QT + kt
                        if i > 0:
                            attend(b, odd, hl - 1, kt)
                        elif kt < 2:
                            for k in (2 * kt, 2 * kt + 1):
                                if hl > 0:
                                    attend(b, odd, hl - 1, k)
                                elif has_prev:
                                    attend(b - 1, 1 - odd, H - 1, k)
                        if u in T_PE:
                            ahead, tp, kind = T_PE[u]
                            if has_next or g + ahead < NG:
                                t_job(G + ahead, (g + ahead) % 2, tp, kind)
                        if u in M_PE:
                            ahead, mp = M_PE[u]
                            if has_next or g + ahead < NG:
                                m_job(G + ahead, (gp + ahead) % 2, mp)
                        if u == N_PE and (has_prev or g > 0):
                            n_job(G - 1, G * 2 + 2)
                        if (g, u) in A_PE and has_next:
                            a_wait(b + 1, *A_PE[g, u])
                            a_job(*A_PE[g, u])
        pairs(pe, batch)
        for kt in range(QT):
            attend(B - 1, (B - 1) % 2, H - 1, kt)
        pe.wait_ge(on_done, B * NG - 1)
        n_job(B * NG - 1, B * NG * 2)

    return sync_engine, gpsimd_engine, scalar_engine, vector_engine, tensor_engine


NT = B * QT
E, HID = 16, 128
S = 512
SC = S // P
U32 = mybir.dt.uint32
TILES = 2 * NT + E


class Chain:

    def __init__(self, engine, semaphore, per):
        self.engine, self.semaphore, self.per, self.round, self.n = engine, semaphore, per, 0, 0

    def start(self, round_):
        self.round, self.n = round_, 0

    def step(self, instruction):
        self.n += 1
        instruction.then_inc(self.semaphore, 1)
        self.engine.wait_ge(self.semaphore, self.round * self.per + self.n)


def for_rows(engine, row):
    row(0)
    with engine.Fori(1, B) as b:
        row(b)


def run_block(nc, sync=None, gpsimd=None, scalar=None, vector=None, tensor=None):
    with nc.Block() as block:
        if sync:
            block.sync(sync)
        if gpsimd:
            block.gpsimd(gpsimd)
        if scalar:
            block.scalar(scalar)
        if vector:
            block.vector(vector)
        if tensor:
            block.tensor(tensor)


def tiles_of(T, b, n=QT):
    return T[:, bass.ds(b * QT, n), :]


def feed_forward(nc, ctx, w_out, b_out, gate_t, experts_t, iota_in, upper_in, steps_in, rows128_in, rows_in, rows_out, out, X, O, ident):
    def sb(name, shape, dt=F32):
        return ctx.enter_context(nc.sbuf_tensor(name, shape, dt))

    def sem(name):
        return ctx.enter_context(nc.semaphore(name))

    W1, W2 = 0, E * DC * HID
    S1 = W2 + E * D
    S2, S3 = S1 + DC * S, S1 + 2 * DC * S
    ALL = S3 + SC * D
    CHUNK = ALL // B
    weights = sb("weights", [P, ALL // P, 2, P], F32R)
    iota = sb("iota", [P, E])
    rows128 = sb("rows128", [P, NT])
    halves = sb("halves32", [P, QT])
    ids = sb("ids", [P, NT, 2])
    wts = sb("wts", [P, NT, 2])
    owner_i = sb("owner_i", [1, TILES], mybir.dt.int32)
    slots_i = sb("slots_i", [P, NT, 2], U32)

    def three(out_ap, pieces, first=True, last=True):
        k = 0
        for st, mv in pieces:
            for a, b in ((st[1], mv[0]), (st[0], mv[1]), (st[0], mv[0])):
                ins = nc.tensor.matmul(out_ap, a, b, start=first and k == 0, stop=last and k == 3 * len(pieces) - 1)
                k += 1
        return ins

    def three_acc(out_ap, st, mv, start, stop):
        for k, (a, b) in enumerate(((st[1], mv[0]), (st[0], mv[1]), (st[0], mv[0]))):
            ins = nc.tensor.matmul(out_ap, a, b, start=start and k == 0, stop=stop and k == 2, skip_group_check=True)
        return ins

    def weight(c0, n):
        return [weights[:, c0 // P:(c0 + n) // P, k, :].rearrange("p a r -> p (a r)") if n == P else
                weights[:, c0 // P:(c0 + n) // P, k, :] for k in range(2)]

    PORTIONS = [(0, CHUNK // P // 2), (CHUNK // P // 2, CHUNK // P - CHUNK // P // 2)]

    def portion(s, h, k):
        return weights[:, bass.ds(s * (CHUNK // P) + PORTIONS[h][0], PORTIONS[h][1]), k, :]

    def one(T, n):
        return T[:, bass.ds(n, 1), :].rearrange("p a d -> p (a d)")

    def in_row(b):
        return not isinstance(b, int) or 0 <= b < B

    def row_steps(engine, step):
        for s in range(4):
            step(s)
        with engine.Fori(4, B - 1) as s:
            step(s)
        for s in range(B - 1, B + 3):
            step(s)

    with ExitStack() as sub:
        psem = lambda name: sub.enter_context(nc.semaphore("p_" + name))
        sbt = lambda name, shape, dt=F32: sub.enter_context(nc.sbuf_tensor("p_" + name, shape, dt))
        bank = lambda name, shape: sub.enter_context(nc.psum_tensor("p_" + name, shape, F32))
        small_in, small_hi, small_lo = (psem(x) for x in "small_in small_hi small_lo".split())
        raw_in, raw_hi, raw_lo = ([psem(f"{x}{h}") for h in range(2)] for x in ("raw_in", "raw_hi", "raw_lo"))
        flat_s, ta_s, ha_s, la_s, proj_s, bn1_s, ag1_s, var1_s, pow1_s, nmr1_s = (
            psem(x) for x in "flat ta ha la proj bn1 ag1 var1 pow1 nmr1".split())
        z_s, x1_s, bn2_s, ag2_s, var2_s, pow2_s, nmr2_s = (psem(x) for x in "z x1 bn2 ag2 var2 pow2 nmr2".split())
        x2_s, tc_s, keep_s, hc_s, lc_s, gate_s, lt_s, lg_s, chain_s, gap_s, ratio_s, route_s = (
            psem(x) for x in "x2 tc keep hc lc gate lt lg chain gap ratio route".split())
        halves_s = psem("halves")
        held = [psem(f"held{i}") for i in range(2)]
        small_raw = sbt("small_raw", [P, DC * D + DC * P + D])
        small_h = sbt("small_h", [P, DC * D + DC * P + D], F32R)
        small_l = sbt("small_l", [P, DC * D + DC * P + D], F32R)
        raw = [sbt(f"raw{h}", [P, n * P]) for h, (b0, n) in enumerate(PORTIONS)]
        first_row = sbt("first_row", [P, P], F32R)
        heads = sbt("heads", [P, QT, D])
        x2 = sbt("x2", [P, QT, D])
        ta_hi, ta_lo, tc_hi, tc_lo = (sbt(x, [P, DC, N], F32R) for x in ("ta_hi", "ta_lo", "tc_hi", "tc_lo"))
        stats = [sbt(f"stats{i}", [P, QT, 6]) for i in range(2)]
        meanvar = [sbt(f"meanvar{i}", [P, QT, 2]) for i in range(2)]
        vareps = [sbt(f"vareps{i}", [P, QT]) for i in range(2)]
        rstd = [sbt(f"rstd{i}", [P, QT]) for i in range(2)]
        nmr = [sbt(f"nmr{i}", [P, QT]) for i in range(2)]
        lt = sbt("lt", [E, N])
        logits = sbt("logits", [P, QT, E])
        top = sbt("top", [P, QT, 8])
        topi = sbt("topi", [P, QT, 8], U32)
        ratio = sbt("ratio", [P, QT])
        den = sbt("den", [P, QT])
        gap = sbt("gap", [P, QT])
        bank_a = [bank(f"a{c}", [P, N]) for c in range(DC)]
        bank_y = [bank(f"y{c}", [P, 2, D]) for c in range(2)]
        bank_c = [bank(f"c{c}", [P, N]) for c in range(DC)]
        bank_g = bank("g", [P, N])
        bank_l = bank("l", [P, QT, E])
        small = lambda c0, n: (small_h[:, c0:c0 + n], small_l[:, c0:c0 + n])
        GW, BIAS = DC * D, DC * D + DC * P

        def sync(sp):
            sp.dma_start(small_raw[:, 0:GW], w_out).then_inc(small_in, 16)
            sp.dma_start(small_raw[:, GW:BIAS], gate_t).then_inc(small_in, 16)
            sp.dma_start(small_raw[:, BIAS:], b_out[None, :].broadcast_to([P, D])).then_inc(small_in, 16)
            sp.dma_start(iota[:, :], iota_in).then_inc(small_in, 16)
            sp.dma_start(rows128[:, :], rows128_in).then_inc(small_in, 16)

            def step(s):
                if in_row(s):
                    for h, (b0, n) in enumerate(PORTIONS):
                        if later(s):
                            sp.wait_ge(raw_lo[h], s)
                        sp.dma_start(raw[h][:, :], experts_t[:, bass.ds(s * CHUNK + b0 * P, n * P)]).then_inc(raw_in[h], 16)
            row_steps(sp, step)

        def gpsimd(pool):
            nc.gpsimd.memset(halves[:, :], -0.5).then_inc(halves_s, 1)
            pool.wait_ge(halves_s, 1)

            def step(s):
                if in_row(s - 2):
                    pool.wait_ge(x2_s, (s - 1) * QT)
                    nc.gpsimd.tensor_copy(tiles_of(O, s - 2), x2[:, :, :]).then_inc(keep_s, 1)
                if in_row(s - 1):
                    pool.wait_ge(var2_s, s)
                    if later(s - 1):
                        pool.wait_ge(nmr2_s, s - 1)
                        pool.wait_ge(x2_s, (s - 1) * QT)
                    nc.gpsimd.tensor_tensor(rstd[1][:, :], vareps[1][:, :], halves[:, :], ALU.pow).then_inc(pow2_s, 1)
                if in_row(s):
                    pool.wait_ge(var1_s, s + 1)
                    if later(s):
                        pool.wait_ge(z_s, s * QT)
                    nc.gpsimd.tensor_tensor(rstd[0][:, :], vareps[0][:, :], halves[:, :], ALU.pow).then_inc(pow1_s, 1)
                if in_row(s):
                    for h in range(2):
                        pool.wait_ge(raw_hi[h], s + 1)
                        nc.gpsimd.tensor_tensor(portion(s, h, 1), raw[h][:, :].rearrange("p (a r) -> p a r", r=P),
                                                portion(s, h, 0).bitcast(F32), ALU.subtract).then_inc(raw_lo[h], 1)
            row_steps(pool, step)

        def scalar(act):
            def split(s, h):
                act.wait_ge(raw_in[h], (s + 1) * 16)
                nc.scalar.copy(portion(s, h, 0), raw[h][:, :].rearrange("p (a r) -> p a r", r=P)).then_inc(raw_hi[h], 1)

            def copy_heads(b):
                if later(b):
                    act.wait_ge(ta_s, b * DC)
                nc.scalar.copy(heads[:, :, :], tiles_of(O, b)).then_inc(flat_s, 1)

            def step(s):
                if in_row(s):
                    for c in range(DC):
                        act.wait_ge(ta_s, s * DC + c + 1)
                        if later(s):
                            act.wait_ge(proj_s, s * 2)
                        nc.scalar.copy(ta_hi[:, c, :], bank_a[c][:, :]).then_inc(ha_s, 1)
                b = s - 2
                if in_row(b):
                    act.wait_ge(nmr2_s, b + 1)
                    if later(b):
                        act.wait_ge(tc_s, b * DC)
                        act.wait_ge(keep_s, b)
                    for t in range(QT):
                        nc.scalar.activation(x2[:, t, :], one(X, b * QT + t), ACT.Identity,
                                             bias=nmr[1][:, t:t + 1], scale=rstd[1][:, t:t + 1]).then_inc(x2_s, 1)
                b = s - 3
                if in_row(b):
                    act.wait_ge(gate_s, b + 1)
                    if later(b):
                        act.wait_ge(lg_s, b)
                    nc.scalar.copy(lt[:, :], bank_g[0:E, :]).then_inc(lt_s, 1)
                b = s - 1
                if in_row(b):
                    act.wait_ge(nmr1_s, b + 1)
                    for t in range(QT):
                        nc.scalar.activation(one(O, b * QT + t), bank_y[t // 2][:, t % 2, :], ACT.Identity,
                                             bias=nmr[0][:, t:t + 1], scale=rstd[0][:, t:t + 1]).then_inc(z_s, 1)
                b = s - 2
                if in_row(b):
                    for c in range(DC):
                        act.wait_ge(tc_s, b * DC + c + 1)
                        if later(b):
                            act.wait_ge(gate_s, b)
                        nc.scalar.copy(tc_hi[:, c, :], bank_c[c][:, :]).then_inc(hc_s, 1)
                if in_row(s + 1):
                    copy_heads(s + 1)
                if in_row(s - 3):
                    act.wait_ge(gap_s, s - 2)
                    nc.scalar.activation(ratio[:, :], gap[:, :], ACT.Exp).then_inc(ratio_s, 1)
                if in_row(s):
                    split(s, 0)
                    split(s, 1)
            act.wait_ge(small_in, 80)
            nc.scalar.copy(small_h[:, :], small_raw[:, :]).then_inc(small_hi, 1)
            copy_heads(0)
            row_steps(act, step)

        def vector(dve):
            chain = Chain(dve, chain_s, 5)

            def statistics(i, b, source, bn_s, ag_s, var_s):
                for t in range(QT):
                    if i == 0 and t % 2 == 0:
                        dve.wait_ge(proj_s, b * 2 + t // 2 + 1)
                    dve.sem_inc(held[0], 1)
                    nc.vector.bn_stats(stats[i][:, t, :], source(t)).then_inc(bn_s, 1)
                dve.wait_ge(bn_s, b * QT + QT)
                dve.sem_inc(held[0], 1)
                for t in range(QT):
                    last = nc.vector.bn_aggr(meanvar[i][:, t, :], stats[i][:, t, :])
                last.then_inc(ag_s, 1)
                dve.wait_ge(ag_s, b + 1)
                nc.vector.tensor_scalar_add(vareps[i][:, :], meanvar[i][:, :, 1], EPS).then_inc(var_s, 1)

            def scale_of_mean(i):
                return nc.vector.scalar_tensor_tensor(nmr[i][:, :], meanvar[i][:, :, 0], -1.0, rstd[i][:, :], ALU.mult, ALU.mult)

            def step(s):
                if in_row(s):
                    for c in range(DC):
                        dve.wait_ge(ha_s, s * DC + c + 1)
                        nc.vector.tensor_tensor(ta_lo[:, c, :], bank_a[c][:, :], ta_hi[:, c, :].bitcast(F32), ALU.subtract).then_inc(la_s, 1)
                e = s - 3
                if in_row(e):
                    chain.start(e)
                    dve.wait_ge(lg_s, e + 1)
                    chain.step(nc.vector.tensor_copy(logits[:, :, :], bank_l[:, :, :]))
                    dve.sem_inc(held[0], 1)
                    for t in range(QT):
                        last = nc.vector.max(top[:, t, :], logits[:, t, :])
                    chain.step(last)
                    nc.vector.tensor_tensor(gap[:, :], top[:, :, 1], top[:, :, 0], ALU.subtract).then_inc(gap_s, 1)
                    for t in range(QT):
                        last = nc.vector.max_index(topi[:, t, :], top[:, t, :], logits[:, t, :])
                    chain.step(last)
                    nc.vector.tensor_copy(ids[:, bass.ds(e * QT, QT), :], topi[:, :, 0:2])
                b = s - 1
                if in_row(b):
                    dve.wait_ge(z_s, b * QT + QT)
                    nc.vector.tensor_tensor(tiles_of(X, b), tiles_of(X, b), tiles_of(O, b), ALU.add).then_inc(x1_s, 1)
                b = s - 2
                if in_row(b):
                    for c in range(DC):
                        dve.wait_ge(hc_s, b * DC + c + 1)
                        nc.vector.tensor_tensor(tc_lo[:, c, :], bank_c[c][:, :], tc_hi[:, c, :].bitcast(F32), ALU.subtract).then_inc(lc_s, 1)
                b = s - 1
                if in_row(b):
                    dve.wait_ge(x1_s, b + 1)
                    statistics(1, b, lambda t: one(X, b * QT + t), bn2_s, ag2_s, var2_s)
                if in_row(s):
                    statistics(0, s, lambda t: bank_y[t // 2][:, t % 2, :], bn1_s, ag1_s, var1_s)
                if in_row(s - 1):
                    dve.wait_ge(pow2_s, s)
                    if later(s - 1):
                        dve.wait_ge(x2_s, (s - 1) * QT)
                    scale_of_mean(1).then_inc(nmr2_s, 1)
                if in_row(s):
                    dve.wait_ge(pow1_s, s + 1)
                    if later(s):
                        dve.wait_ge(z_s, s * QT)
                    scale_of_mean(0).then_inc(nmr1_s, 1)
                if in_row(e):
                    dve.wait_ge(ratio_s, e + 1)
                    chain.step(nc.vector.tensor_scalar_add(den[:, :], ratio[:, :], 1.0))
                    chain.step(nc.vector.reciprocal(wts[:, bass.ds(e * QT, QT), 0], den[:, :]))
                    nc.vector.tensor_tensor(wts[:, bass.ds(e * QT, QT), 1], ratio[:, :], wts[:, bass.ds(e * QT, QT), 0], ALU.mult).then_inc(route_s, 1)

            nc.vector.memset(first_row[:, :].bitcast(F32), 0.0).then_inc(small_lo, 1)
            dve.wait_ge(small_lo, 1)
            nc.vector.memset(first_row[0:1, :].bitcast(F32), 1.0)
            dve.wait_ge(small_hi, 1)
            nc.vector.tensor_tensor(small_l[:, :], small_raw[:, :], small_h[:, :].bitcast(F32), ALU.subtract).then_inc(small_lo, 1)
            row_steps(dve, step)

        def tensor(pe):
            def transposes(banks, src, sem):
                for c in range(DC):
                    for t in range(QT):
                        last = nc.tensor.transpose(banks[c][:, t * P:(t + 1) * P], src[:, t, c * P:(c + 1) * P], ident[:, :])
                    last.then_inc(sem, 1)

            def transpose_heads(b):
                pe.wait_ge(flat_s, b + 1)
                if later(b):
                    pe.wait_ge(la_s, b * DC)
                transposes(bank_a, heads, ta_s)

            def step(s):
                b = s - 2
                if in_row(b):
                    pe.wait_ge(x2_s, b * QT + QT)
                    if later(b):
                        pe.wait_ge(lc_s, b * DC)
                    transposes(bank_c, x2, tc_s)
                if in_row(s - 3):
                    pe.wait_ge(lt_s, s - 2)
                    if later(s - 3):
                        pe.wait_ge(route_s, s - 3)
                    pe.sem_inc(held[1], 1)
                    for t in range(QT):
                        last = nc.tensor.transpose(bank_l[:, t, :], lt[:, t * P:(t + 1) * P], ident[0:E, 0:E])
                    last.then_inc(lg_s, 1)
                if in_row(s):
                    pe.wait_ge(la_s, s * DC + DC)
                    for k in range(2):
                        if later(s):
                            pe.wait_ge(z_s, s * QT - 2 + 2 * k)
                        for t in (2 * k, 2 * k + 1):
                            cols = slice(t * P, (t + 1) * P)
                            for bias_part in (small_l, small_h):
                                nc.tensor.matmul(bank_y[k][:, t % 2, :], first_row[:, :], bias_part[:, BIAS:BIAS + D],
                                                 start=t % 2 == 0 and bias_part is small_l, stop=False, skip_group_check=True)
                            for c in range(DC):
                                last = three_acc(bank_y[k][:, t % 2, :], (ta_hi[:, c, cols], ta_lo[:, c, cols]), small(c * D, D),
                                                 False, t % 2 == 1 and c == DC - 1)
                        last.then_inc(proj_s, 1)
                if in_row(s + 1):
                    transpose_heads(s + 1)
                b = s - 2
                if in_row(b):
                    pe.wait_ge(lc_s, b * DC + DC)
                    if later(b):
                        pe.wait_ge(lt_s, b)
                    three(bank_g[:, :], [(small(GW + c * P, P), (tc_hi[:, c, :], tc_lo[:, c, :])) for c in range(DC)]).then_inc(gate_s, 1)
            transpose_heads(0)
            pe.wait_ge(small_lo, 2)
            row_steps(pe, step)
        run_block(nc, sync=sync, gpsimd=gpsimd, scalar=scalar, vector=vector, tensor=tensor)

    HALF = B // 2

    def shared_rows(engine, row):
        row(0, True)
        with engine.Fori(1, HALF - 1) as r:
            row(r, True)
        row(HALF - 1, False)

    def shared_expert(stack, name, b0, moved_s, counted_s):
        (flat_s, tr_s, hi_s, lo_s, a_s, g_s, silu_s, h_s, hh_s, hl_s, y_s, out_s) = (
            stack.enter_context(nc.semaphore(f"{name}_{x}")) for x in "flat tr hi lo a g silu h hh hl y out".split())
        sbt = lambda x, shape, dt=F32: stack.enter_context(nc.sbuf_tensor(f"{name}_{x}", shape, dt))
        flat = sbt("flat", [P, QT, D])
        t_hi, t_lo = (sbt(x, [P, DC, N], F32R) for x in ("t_hi", "t_lo"))
        silu = [sbt(f"silu{i}", [P, N]) for i in range(2)]
        h_hi = [sbt(f"h_hi{i}", [P, N], F32R) for i in range(2)]
        h_lo = [sbt(f"h_lo{i}", [P, N], F32R) for i in range(2)]
        bank_t, bank_a, bank_g, bank_y = ([stack.enter_context(nc.psum_tensor(f"{name}_b{x}{c}", [P, N], F32)) for c in range(2)] for x in "tagy")

        class Steps:
            banks, out = bank_y, out_s

            def copy_row(act, r):
                if later(r):
                    act.wait_ge(tr_s, r * DC)
                nc.scalar.copy(flat[:, :, :], tiles_of(O, b0 + r)).then_inc(flat_s, 1)

            def high(act, r):
                for c in range(DC):
                    act.wait_ge(tr_s, r * DC + c + 1)
                    if later(r):
                        act.wait_ge(g_s, r * SC)
                    nc.scalar.copy(t_hi[:, c, :], bank_t[c][:, :]).then_inc(hi_s, 1)

            def silus(act, r, n):
                m = r * SC + n
                act.wait_ge(a_s, m + 1)
                if later(m - 1):
                    act.wait_ge(hl_s, m - 1)
                nc.scalar.activation(silu[n % 2][:, :], bank_a[n % 2][:, :], ACT.Silu).then_inc(silu_s, 1)
                act.wait_ge(h_s, m + 1)
                if later(m - 1):
                    act.wait_ge(y_s, m - 1)
                nc.scalar.copy(h_hi[n % 2][:, :], silu[n % 2][:, :]).then_inc(hh_s, 1)

            def keep(act, r):
                act.wait_ge(y_s, r * SC + SC)
                if moved_s:
                    act.wait_ge(moved_s, r + 1)
                for k in range(2):
                    nc.scalar.copy(O[:, bass.ds((b0 + r) * QT + 2 * k, 2), :].rearrange("p t d -> p (t d)"), bank_y[k][:, :]).then_inc(out_s, 1)

            def low(dve, r):
                for c in range(DC):
                    dve.wait_ge(hi_s, r * DC + c + 1)
                    nc.vector.tensor_tensor(t_lo[:, c, :], bank_t[c][:, :], t_hi[:, c, :].bitcast(F32), ALU.subtract).then_inc(lo_s, 1)

            def multiply(dve, r, n):
                m = r * SC + n
                dve.wait_ge(silu_s, m + 1)
                dve.wait_ge(g_s, m + 1)
                nc.vector.tensor_tensor(silu[n % 2][:, :], silu[n % 2][:, :], bank_g[n % 2][:, :], ALU.mult).then_inc(h_s, 1)

            def hidden_low(dve, r, n):
                dve.wait_ge(hh_s, r * SC + n + 1)
                nc.vector.tensor_tensor(h_lo[n % 2][:, :], silu[n % 2][:, :], h_hi[n % 2][:, :].bitcast(F32), ALU.subtract).then_inc(hl_s, 1)

            def transposes(pe, r):
                pe.wait_ge(flat_s, r + 1)
                if later(r):
                    pe.wait_ge(lo_s, r * DC)
                for c in range(DC):
                    for t in range(QT):
                        last = nc.tensor.transpose(bank_t[c][:, t * P:(t + 1) * P], flat[:, t, c * P:(c + 1) * P], ident[:, :])
                    last.then_inc(tr_s, 1)

            def first(pe, r, n):
                m = r * SC + n
                if later(m - 1):
                    pe.wait_ge(silu_s, m - 1)
                three(bank_a[n % 2][:, :], [(weight(S1 + c * S + n * P, P), (t_hi[:, c, :], t_lo[:, c, :])) for c in range(DC)]).then_inc(a_s, 1)
                if later(m - 1):
                    pe.wait_ge(h_s, m - 1)
                three(bank_g[n % 2][:, :], [(weight(S2 + c * S + n * P, P), (t_hi[:, c, :], t_lo[:, c, :])) for c in range(DC)]).then_inc(g_s, 1)

            def second(pe, r, n):
                m = r * SC + n
                pe.wait_ge(hl_s, m + 1)
                if n == 0:
                    if later(r):
                        pe.wait_ge(out_s, r * 2)
                    elif counted_s:
                        pe.wait_ge(counted_s, 1)
                for t in range(QT):
                    lhs = (h_hi[n % 2][:, t * P:(t + 1) * P], h_lo[n % 2][:, t * P:(t + 1) * P])
                    last = three_acc(bank_y[t // 2][:, (t % 2) * D:(t % 2 + 1) * D], lhs, weight(S3 + n * D, D),
                                     n == 0 and t % 2 == 0, n == SC - 1)
                last.then_inc(y_s, 1)

            def layers(pe):
                def row(r, has_next):
                    pe.wait_ge(lo_s, r * DC + DC)
                    Steps.first(pe, r, 0)
                    for n in range(1, SC):
                        Steps.first(pe, r, n)
                        if n == SC - 1 and has_next:
                            Steps.transposes(pe, r + 1)
                        Steps.second(pe, r, n - 1)
                    Steps.second(pe, r, SC - 1)
                shared_rows(pe, row)
        return Steps

    with ExitStack() as sub:
        psem = lambda name: sub.enter_context(nc.semaphore(name))
        sbt = lambda name, shape, dt=F32: sub.enter_context(nc.sbuf_tensor(name, shape, dt))
        in_s, hot_s, const_s, pe_s, chain_s, place_s, moved_s, row_s = (psem("s_" + x) for x in "in hot const pe chain place moved row".split())
        hot = [sbt(f"hot{k}", [P, NT, E]) for k in range(2)]
        both = sbt("both", [P, NT, E], F32R)
        upper = sbt("upper", [P, P])
        upper_r = sbt("upper_r", [P, P], F32R)
        ones_r = sbt("ones_r", [P, P], F32R)
        run = [sbt(f"run{i}", [P, NT, E]) for i in range(2)]
        count = sbt("count", [P, E])
        needed = sbt("needed", [P, E])
        end = [sbt(f"end{i}", [P, E]) for i in range(2)]
        base = sbt("base", [P, E])
        passed_wide = sbt("passed_wide", [P, E, NT])
        place = sbt("place", [P, NT, E])
        chosen = [sbt(f"chosen{k}", [P, NT, E]) for k in range(2)]
        slots = sbt("slots", [P, NT, 2])
        steps = sbt("steps", [1, TILES])
        passed = sbt("passed", [1, TILES, E])
        owner = sbt("owner", [1, TILES])
        shared = shared_expert(sub, "s_shared", 0, moved_s, place_s)
        bank_all, bank_in = (shared.banks[i][:, :].rearrange("p (t e) -> p t e", e=E) for i in range(2))

        def sync(sp):
            sp.dma_start(upper[:, :], upper_in).then_inc(in_s, 16)
            sp.dma_start(steps[:, :], steps_in[0:1, :]).then_inc(in_s, 16)
            sp.wait_ge(in_s, 32)

        def scalar(act):
            def row(r, has_next):
                shared.high(act, r)
                if has_next:
                    shared.copy_row(act, r + 1)
                for n in range(SC):
                    shared.silus(act, r, n)
                    if n == 0 and later(r):
                        shared.keep(act, r - 1)

            act.wait_ge(in_s, 32)
            nc.scalar.copy(upper_r[:, :], upper[:, :]).then_inc(const_s, 1)
            nc.scalar.activation(ones_r[:, :], upper[:, :], ACT.Copy, scale=0.0, bias=1.0).then_inc(const_s, 1)
            shared.copy_row(act, 0)
            shared_rows(act, row)
            shared.keep(act, HALF - 1)

        def tensor(pe):
            shared.transposes(pe, 0)
            pe.wait_ge(const_s, 2)
            pe.wait_ge(hot_s, 1)
            m = both[:, :, :].rearrange("p t e -> p (t e)")
            nc.tensor.matmul(shared.banks[0][:, :], ones_r[:, :], m, start=True, stop=True).then_inc(pe_s, 1)
            nc.tensor.matmul(shared.banks[1][:, :], upper_r[:, :], m, start=True, stop=True).then_inc(pe_s, 1)
            shared.layers(pe)

        def vector(dve):
            chain = Chain(dve, chain_s, 0)
            chain.start(0)
            experts = iota[:, :].unsqueeze(1).broadcast_to([P, NT, E])
            for k in range(2):
                chain.step(nc.vector.tensor_tensor(hot[k][:, :, :], experts, ids[:, :, k:k + 1].broadcast_to([P, NT, E]), ALU.is_equal))
            nc.vector.tensor_tensor(both[:, :, :], hot[0][:, :, :], hot[1][:, :, :], ALU.add).then_inc(hot_s, 1)
            dve.wait_ge(pe_s, 1)
            chain.step(nc.vector.tensor_copy(run[0][:, :, :], bank_all))
            src = 0
            for shift in (1, 2, 4, 8, 16):
                nc.vector.tensor_copy(run[1 - src][:, 0:shift, :], run[src][:, 0:shift, :])
                chain.step(nc.vector.tensor_tensor(run[1 - src][:, shift:NT, :], run[src][:, shift:NT, :], run[src][:, 0:NT - shift, :], ALU.add))
                src = 1 - src
            total = run[src][:, NT - 1, :]
            wide = passed_wide[:, :, :]
            chain.step(nc.vector.tensor_tensor(wide, total.unsqueeze(2).broadcast_to([P, E, NT]), rows128[:, :].unsqueeze(1).broadcast_to([P, E, NT]), ALU.is_gt))
            chain.step(nc.vector.tensor_reduce(end[0][:, :], wide, AX.X, ALU.add))
            chain.step(nc.vector.tensor_copy(needed[:, :], end[0][:, :]))
            es = 0
            for shift in (1, 2, 4, 8):
                nc.vector.tensor_copy(end[1 - es][:, 0:shift], end[es][:, 0:shift])
                chain.step(nc.vector.tensor_tensor(end[1 - es][:, shift:E], end[es][:, shift:E], end[es][:, 0:E - shift], ALU.add))
                es = 1 - es
            nc.vector.tensor_tensor(passed[:, :, :], steps[:, :].unsqueeze(2).broadcast_to([1, TILES, E]), end[es][0:1, :].unsqueeze(1).broadcast_to([1, TILES, E]), ALU.is_ge).then_inc(hot_s, 1)
            dve.wait_ge(hot_s, 2)
            chain.step(nc.vector.tensor_reduce(owner[:, :], passed[:, :, :], AX.X, ALU.add))
            chain.step(nc.vector.tensor_scalar(owner[:, :], owner[:, :], float(E - 1), float(D // P), ALU.min, ALU.mult))
            chain.step(nc.vector.tensor_copy(owner_i[:, :], owner[:, :]))
            chain.step(nc.vector.tensor_tensor(base[:, :], end[es][:, :], needed[:, :], ALU.subtract))
            chain.step(nc.vector.tensor_scalar_mul(base[:, :], base[:, :], float(P)))
            dve.wait_ge(pe_s, 2)
            chain.step(nc.vector.tensor_tensor(place[:, :, :], bank_in, base[:, :].unsqueeze(1).broadcast_to([P, NT, E]), ALU.add))
            chain.step(nc.vector.tensor_tensor(place[:, 1:NT, :], place[:, 1:NT, :], run[src][:, 0:NT - 1, :], ALU.add))
            for k in range(2):
                chain.step(nc.vector.tensor_tensor(chosen[k][:, :, :], hot[k][:, :, :], place[:, :, :], ALU.mult))
            for k in range(2):
                chain.step(nc.vector.tensor_reduce(slots[:, :, k], chosen[k][:, :, :], AX.X, ALU.add))
            nc.vector.tensor_copy(slots_i[:, :, :], slots[:, :, :]).then_inc(place_s, 1)

            def row(r, has_next):
                shared.low(dve, r)
                for n in range(SC):
                    shared.multiply(dve, r, n)
                    shared.hidden_low(dve, r, n)
            shared_rows(dve, row)

        def gpsimd(pool):
            pool.wait_ge(place_s, 1)
            for b in range(B):
                for t in range(b * QT, b * QT + QT):
                    for k in range(2):
                        nc.gpsimd.indirect_dma_start(out=rows_in, out_offset=bass.IndirectOffsetOnAxis(ap=slots_i[:, t, k:k + 1], axis=0),
                                                     in_=O[:, t, :], in_offset=None).then_inc(row_s, 16)
                if b < HALF or b == B - 1:
                    pool.wait_ge(row_s, 16 * QT * 2 * (b + 1))
                    pool.sem_inc(moved_s, 1)
        run_block(nc, sync=sync, gpsimd=gpsimd, scalar=scalar, vector=vector, tensor=tensor)

    with ExitStack() as sub:
        psem = lambda name: sub.enter_context(nc.semaphore(name))
        sbt = lambda name, shape, dt=F32: sub.enter_context(nc.sbuf_tensor(name, shape, dt))
        (xt_s, xhi_s, xlo_s, h_s, pre_s, silu_s, gt_s, ghi_s, glo_s, y_s, yb_s) = (
            psem("m_" + x) for x in "xt xhi xlo h pre silu gt ghi glo y yb".split())
        load_s = [psem(f"m_load{i}") for i in range(4)]
        store_s = [psem(f"m_store{i}") for i in range(2)]
        rows = [sbt(f"m_rows{i}", [P, 2, D]) for i in range(4)]
        x_hi = [sbt(f"m_xhi{i}", [P, D], F32R) for i in range(2)]
        x_lo = [sbt(f"m_xlo{i}", [P, D], F32R) for i in range(2)]
        pre = [sbt(f"m_pre{i}", [P, HID]) for i in range(2)]
        g = [sbt(f"m_g{i}", [P, HID]) for i in range(2)]
        g_hi = [sbt(f"m_ghi{i}", [P, P], F32R) for i in range(2)]
        g_lo = [sbt(f"m_glo{i}", [P, P], F32R) for i in range(2)]
        y = [sbt(f"m_y{i}", [P, 4, D]) for i in range(2)]
        bank = lambda name: [sub.enter_context(nc.psum_tensor(f"m_{name}{i}", [P, D], F32)) for i in range(2)]
        bank_x, bank_h, bank_g, bank_y = bank("bx"), bank("bh"), bank("bg"), bank("by")

        def for_tiles(engine, step, lag):
            for s in range(8):
                step(s, s, 0)
            with engine.Fori(1, TILES // 8) as eight:
                for i in range(8):
                    step(eight * 8 + i, i, eight)
            for s in range(TILES, TILES + lag):
                step(s, s % 8, TILES // 8)

        def valid(s):
            return not isinstance(s, int) or 0 <= s < TILES

        in_v = rows_in.rearrange("(n f p) d -> n p f d", f=2, p=P)
        out_v = rows_out.rearrange("(n f p) d -> n p f d", f=4, p=P)

        def sync(sp):
            def load(two, j, round_):
                if later(round_):
                    sp.wait_ge(xt_s, (two - 3) * 2)
                sp.dma_start(rows[j][:, :, :], in_v[bass.ds(two, 1)].rearrange("a p f d -> p (a f) d")).then_inc(load_s[j], 16)
            for j in range(4):
                load(j, j, 0)
            with sp.Fori(1, TILES // 8) as eight:
                for j in range(4):
                    load(eight * 4 + j, j, eight)

        def gpsimd(pool):
            def store(four, half):
                pool.wait_ge(yb_s, four * 4 + 4)
                pool.dma_start(out_v[bass.ds(four, 1)].rearrange("a p f d -> p (a f) d"), y[half][:, :, :]).then_inc(store_s[half], 16)
            with pool.Fori(0, TILES // 8) as eight:
                for half in range(2):
                    store(eight * 2 + half, half)
            for half in range(2):
                pool.wait_ge(store_s[half], 16 * (TILES // 8))

        def scalar(act):
            def step(s, i, eight):
                if valid(s - 2):
                    act.wait_ge(pre_s, s - 1)
                    if later(s - 3):
                        act.wait_ge(gt_s, s - 3)
                    nc.scalar.activation(g[i % 2][:, :], pre[i % 2][:, :], ACT.Silu).then_inc(silu_s, 1)
                if valid(s):
                    act.wait_ge(xt_s, s + 1)
                    if later(s - 1):
                        act.wait_ge(h_s, s - 1)
                    nc.scalar.copy(x_hi[i % 2][:, :], bank_x[i % 2][:, :]).then_inc(xhi_s, 1)
                if valid(s - 4):
                    j = (i - 4) % 8
                    before = eight if j < 4 else eight - 1
                    act.wait_ge(y_s, s - 3)
                    if j % 4 == 0 and later(before):
                        act.wait_ge(store_s[j // 4], before * 16)
                    nc.scalar.copy(y[j // 4][:, j % 4, :], bank_y[j % 2][:, :]).then_inc(yb_s, 1)
                if valid(s - 2):
                    act.wait_ge(gt_s, s - 1)
                    if later(s - 3):
                        act.wait_ge(y_s, s - 3)
                    nc.scalar.copy(g_hi[i % 2][:, :], bank_g[i % 2][:, 0:P]).then_inc(ghi_s, 1)
            for_tiles(act, step, 4)

        def vector(dve):
            def step(s, i, eight):
                if valid(s):
                    dve.wait_ge(xhi_s, s + 1)
                    nc.vector.tensor_tensor(x_lo[i % 2][:, :], bank_x[i % 2][:, :], x_hi[i % 2][:, :].bitcast(F32), ALU.subtract).then_inc(xlo_s, 1)
                if valid(s - 1):
                    q = (i - 1) % 2
                    dve.wait_ge(h_s, s)
                    if later(s - 2):
                        dve.wait_ge(silu_s, s - 2)
                    nc.vector.tensor_reduce(pre[q][:, :], bank_h[q][:, :].rearrange("p (k r) -> p r k", k=2), AX.X, ALU.add).then_inc(pre_s, 1)
                if valid(s - 2):
                    dve.wait_ge(ghi_s, s - 1)
                    nc.vector.tensor_tensor(g_lo[i % 2][:, :], bank_g[i % 2][:, 0:P], g_hi[i % 2][:, :].bitcast(F32), ALU.subtract).then_inc(glo_s, 1)
            for_tiles(dve, step, 2)

        def tensor(pe):
            at_r = [pe.alloc_register(name=f"expert_at{j}") for j in range(8)]

            def step(s, i, eight):
                if i % 4 == 0 and valid(s):
                    pe.load(at_r[i:i + 4], owner_i[0:1, bass.ds(s, 4)])
                expert_of = lambda j: pe.snap(at_r[j % 8], min_val=0, max_val=(E - 1) * (D // P))
                if valid(s):
                    pe.wait_ge(load_s[i // 2], (eight + 1) * 16)
                    if later(s - 1):
                        pe.wait_ge(xlo_s, s - 1)
                    for c in range(DC):
                        last = nc.tensor.transpose(bank_x[i % 2][:, c * P:(c + 1) * P], rows[i // 2][:, i % 2, c * P:(c + 1) * P], ident[:, :])
                    last.then_inc(xt_s, 1)
                if valid(s - 1):
                    q = (i - 1) % 2
                    at = expert_of(i - 1)
                    pe.wait_ge(xlo_s, s)
                    if later(s - 2):
                        pe.wait_ge(pre_s, s - 2)
                    terms = [(x, c) for c in range(DC) for x in (x_lo, x_hi)]
                    for k, (x, c) in enumerate(terms):
                        block = weights[:, bass.ds(at + (W1 // P + c), 1), :, :].rearrange("p a k r -> p (a k r)")
                        last = nc.tensor.matmul(bank_h[q][:, :], x[q][:, c * P:(c + 1) * P], block,
                                                start=k == 0, stop=k == len(terms) - 1)
                    last.then_inc(h_s, 1)
                if valid(s - 2):
                    pe.wait_ge(silu_s, s - 1)
                    if later(s - 3):
                        pe.wait_ge(glo_s, s - 3)
                    nc.tensor.transpose(bank_g[i % 2][:, 0:P], g[i % 2][:, :], ident[:, :]).then_inc(gt_s, 1)
                if valid(s - 3):
                    q = (i - 3) % 2
                    at = expert_of(i - 3)
                    pe.wait_ge(glo_s, s - 2)
                    if later(s - 4):
                        pe.wait_ge(yb_s, s - 4)
                    for k, (a, b) in enumerate(((g_lo, 0), (g_hi, 1), (g_hi, 0))):
                        last = nc.tensor.matmul(bank_y[q][:, :], a[q][:, :], weights[:, bass.ds(at + W2 // P, D // P), b, :], start=k == 0, stop=k == 2)
                    last.then_inc(y_s, 1)
            for_tiles(pe, step, 3)
        run_block(nc, sync=sync, gpsimd=gpsimd, scalar=scalar, vector=vector, tensor=tensor)

    with ExitStack() as sub:
        psem = lambda name: sub.enter_context(nc.semaphore("e_" + name))
        sbt = lambda name, shape, dt=F32: sub.enter_context(nc.sbuf_tensor("e_" + name, shape, dt))
        (sum0_s, sum_s, bn_s, ag_s, var_s, pow_s, nmr_s, z_s, res_s, out_s, held) = (
            psem(x) for x in "sum0 sum bn ag var pow nmr z res out held".split())
        rows_s = [psem(f"rows{i}") for i in range(2)]
        picked = [[[sbt(f"picked{i}{t}{k}", [P, D]) for k in range(2)] for t in range(QT)] for i in range(2)]
        stats = sbt("stats", [P, QT, 6])
        meanvar = sbt("meanvar", [P, QT, 2])
        vareps = sbt("vareps", [P, QT])
        rstd = sbt("rstd", [P, QT])
        nmr = sbt("nmr", [P, QT])
        out_v = out.rearrange("b (t p) d -> p (b t) d", p=P)

        shared = shared_expert(sub, "e_shared", HALF, None, None)

        def sync(sp):
            def row(b):
                sp.wait_ge(res_s, b + 1)
                sp.dma_start(out_v[:, bass.ds(b * QT, QT), :], tiles_of(X, b)).then_inc(out_s, 16)
            for_rows(sp, row)
            sp.wait_ge(out_s, 16 * B)

        def gpsimd(pool):
            def scale_row(b):
                pool.wait_ge(var_s, b + 1)
                if later(b):
                    pool.wait_ge(z_s, b * QT)
                nc.gpsimd.tensor_tensor(rstd[:, :], vareps[:, :], halves[:, :], ALU.pow).then_inc(pow_s, 1)

            for b in range(B):
                for t in range(QT):
                    if b > 1:
                        pool.wait_ge(sum_s, (b - 2) * QT + t + 1)
                    for k in range(2):
                        nc.gpsimd.indirect_dma_start(out=picked[b % 2][t][k][:, :], out_offset=None, in_=rows_out,
                                                     in_offset=bass.IndirectOffsetOnAxis(ap=slots_i[:, b * QT + t, k:k + 1], axis=0)).then_inc(rows_s[b % 2], 16)
                if b > 0:
                    scale_row(b - 1)
            scale_row(B - 1)

        def scalar(act):
            def normalise(b):
                act.wait_ge(nmr_s, b + 1)
                for t in range(QT):
                    nc.scalar.activation(one(O, b * QT + t), one(O, b * QT + t), ACT.Identity,
                                         bias=nmr[:, t:t + 1], scale=rstd[:, t:t + 1]).then_inc(z_s, 1)

            def pair(j, has_next):
                if has_next:
                    shared.copy_row(act, j + 1)
                shared.silus(act, j, 0)
                if later(j):
                    shared.keep(act, j - 1)
                shared.silus(act, j, 1)
                if later(j):
                    normalise(j * 2 - 2)
                shared.silus(act, j, 2)
                shared.silus(act, j, 3)
                if has_next:
                    shared.high(act, j + 1)
                if later(j):
                    normalise(j * 2 - 1)
            shared.copy_row(act, 0)
            shared.high(act, 0)
            shared_rows(act, pair)
            shared.keep(act, HALF - 1)
            normalise(B - 2)
            normalise(B - 1)

        def tensor(pe):
            shared.transposes(pe, 0)
            shared.layers(pe)

        def vector(dve):
            def add_expert(j, odd, k, t0):
                b = j * 2 + odd
                if k == 0 and t0 == 0:
                    dve.wait_ge(rows_s[odd], (j + 1) * QT * 2 * 16)
                for t in (t0, t0 + 1):
                    n = b * QT + t
                    if k == 1:
                        dve.wait_ge(sum0_s, n + 1)
                    nc.vector.scalar_tensor_tensor(one(O, n), picked[odd][t][k][:, :], wts[:, bass.ds(n, 1), k],
                                                   one(O, n), ALU.mult, ALU.add).then_inc((sum0_s, sum_s)[k], 1)

            def variances(b):
                for t in range(QT):
                    dve.wait_ge(sum_s, b * QT + t + 1)
                    dve.sem_inc(held, 1)
                    nc.vector.bn_stats(stats[:, t, :], one(O, b * QT + t)).then_inc(bn_s, 1)
                dve.wait_ge(bn_s, b * QT + QT)
                dve.sem_inc(held, 1)
                for t in range(QT):
                    last = nc.vector.bn_aggr(meanvar[:, t, :], stats[:, t, :])
                last.then_inc(ag_s, 1)
                dve.wait_ge(ag_s, b + 1)
                nc.vector.tensor_scalar_add(vareps[:, :], meanvar[:, :, 1], EPS).then_inc(var_s, 1)

            def scale_of_mean(b):
                dve.wait_ge(pow_s, b + 1)
                if later(b):
                    dve.wait_ge(z_s, b * QT)
                nc.vector.scalar_tensor_tensor(nmr[:, :], meanvar[:, :, 0], -1.0, rstd[:, :], ALU.mult, ALU.mult).then_inc(nmr_s, 1)

            def residual(b):
                dve.wait_ge(z_s, b * QT + QT)
                nc.vector.tensor_tensor(tiles_of(X, b), tiles_of(X, b), tiles_of(O, b), ALU.add).then_inc(res_s, 1)

            def pair(j, has_next):
                shared.multiply(dve, j, 0)
                if later(j):
                    add_expert(j - 1, 1, 0, 0)
                shared.hidden_low(dve, j, 0)
                if later(j):
                    add_expert(j - 1, 1, 0, 2)
                    scale_of_mean(j * 2 - 2)
                shared.multiply(dve, j, 1)
                if later(j):
                    add_expert(j - 1, 1, 1, 0)
                shared.hidden_low(dve, j, 1)
                if later(j):
                    add_expert(j - 1, 1, 1, 2)
                    variances(j * 2 - 1)
                    dve.wait_ge(shared.out, j * 2)
                shared.multiply(dve, j, 2)
                add_expert(j, 0, 0, 0)
                shared.hidden_low(dve, j, 2)
                add_expert(j, 0, 0, 2)
                shared.multiply(dve, j, 3)
                add_expert(j, 0, 1, 0)
                shared.hidden_low(dve, j, 3)
                if has_next:
                    shared.low(dve, j + 1)
                add_expert(j, 0, 1, 2)
                if later(j):
                    scale_of_mean(j * 2 - 1)
                variances(j * 2)
                if later(j):
                    residual(j * 2 - 2)
                    residual(j * 2 - 1)
            shared.low(dve, 0)
            shared_rows(dve, pair)
            scale_of_mean(B - 2)
            dve.wait_ge(shared.out, HALF * 2)
            for k in range(2):
                for t0 in (0, 2):
                    add_expert(HALF - 1, 1, k, t0)
            variances(B - 1)
            residual(B - 2)
            scale_of_mean(B - 1)
            residual(B - 1)
        run_block(nc, sync=sync, gpsimd=gpsimd, scalar=scalar, vector=vector, tensor=tensor)


def transformer_layer(nc, x, w_qkv, w_out, b_out, gate_t, experts_t, cos, sin, ident_in, iota,
                      upper, steps, rows128, rows_in, rows_out, out):
    with ExitStack() as ctx:
        X = ctx.enter_context(nc.sbuf_tensor("X", [P, NT, D], F32))
        O = ctx.enter_context(nc.sbuf_tensor("O", [P, NT, D], F32))
        ident = ctx.enter_context(nc.sbuf_tensor("identity", [P, P], F32))
        ident_r = ctx.enter_context(nc.sbuf_tensor("identity_r", [P, P], F32R))
        with ExitStack() as sub:
            sync, gpsimd, scalar, vector, tensor = attention(nc, sub, x, w_qkv, cos, sin, ident_in, rows_in,
                                                               X, O, ident, ident_r)
            run_block(nc, sync, gpsimd, scalar, vector, tensor)
        with ExitStack() as sub:
            feed_forward(nc, sub, w_out, b_out, gate_t, experts_t, iota, upper, steps,
                         rows128, rows_in, rows_out, out, X, O, ident)


def kernel(L0_attn_x, L0_attn_w_qkv, L0_attn_w_out, L0_attn_b_out, L0_ffn_gate_w, L0_ffn_w1, L0_ffn_w2,
           L0_ffn_sfc1, L0_ffn_sfc2, L0_ffn_sfc3):
    import numpy as np
    import concourse.bacc as bacc
    from concourse.bass_utils import run_bass_kernel_spmd

    def rows(a):
        a = np.asarray(a)
        return np.ascontiguousarray(a.reshape(-1, P, a.shape[1]).transpose(1, 0, 2).reshape(P, -1))

    w1 = np.asarray(L0_ffn_w1)
    w2 = np.asarray(L0_ffn_w2)
    gate = np.zeros((D, P), w1.dtype)
    gate[:, 0:E] = np.asarray(L0_ffn_gate_w).T
    freqs = np.float32(10000.0) ** (-np.arange(0, HD, 2, dtype=np.float32) / np.float32(HD))
    angles = np.arange(N, dtype=np.float32)[:, None] * freqs
    sin = np.repeat(np.sin(angles), 2, axis=1).astype(np.float32)
    sin[:, 0:HD // 2] *= -1
    inputs = {
        "x": np.asarray(L0_attn_x),
        "w_qkv": np.asarray(L0_attn_w_qkv),
        "w_out": rows(L0_attn_w_out),
        "b_out": np.asarray(L0_attn_b_out),
        "gate_t": rows(gate),
        "experts_t": np.concatenate([
            w1.reshape(E, HID, DC, P).transpose(3, 0, 2, 1).reshape(P, -1),
            w2.transpose(2, 0, 1).reshape(P, -1),
            rows(np.asarray(L0_ffn_sfc1).T), rows(np.asarray(L0_ffn_sfc2).T), rows(np.asarray(L0_ffn_sfc3).T)], axis=1),
        "cos": np.repeat(np.cos(angles), 2, axis=1).astype(np.float32),
        "sin": sin,
        "ident_in": np.eye(P, dtype=np.float32),
        "upper": np.triu(np.ones((P, P), np.float32), 1),
        "steps": np.arange(TILES, dtype=np.float32)[None, :],
        "rows128": np.tile(np.arange(NT, dtype=np.float32) * P, (P, 1)),
        "iota": np.tile(np.arange(E, dtype=np.float32), (P, 1)),
    }
    nc = bacc.Bacc("TRN2", target_bir_lowering=False, num_devices=1)
    aps = {k: nc.dram_tensor("in_" + k, a.shape, mybir.dt.from_np(a.dtype), kind="ExternalInput").ap()
           for k, a in inputs.items()}
    out = nc.dram_tensor("out", (B, N, D), F32, kind="ExternalOutput").ap()
    rows_in, rows_out = (nc.dram_tensor(name, (TILES * P, D), F32, kind="Internal").ap() for name in ("rows_in", "rows_out"))
    transformer_layer(nc, **aps, rows_in=rows_in, rows_out=rows_out, out=out)
    results = run_bass_kernel_spmd(nc, [{"in_" + k: a for k, a in inputs.items()}], core_ids=[0])
    return results.results[0]["out"]
```
